# Optimizing a Trainium2 kernel written in Bass

```python
import numpy as np
import jax
import jax.numpy as jnp

def _softmax(x, axis=-1):
    return jax.nn.softmax(x, axis=axis)

def _gelu(x):
    return jax.nn.gelu(x, approximate=True)

def _silu(x):
    return jax.nn.silu(x)

def _sigmoid(x):
    return jax.nn.sigmoid(x)

def _layernorm(x, axis=-1, eps=1e-05):
    m = jnp.mean(x, axis=axis, keepdims=True)
    v = jnp.var(x, axis=axis, keepdims=True)
    return (x - m) / jnp.sqrt(v + eps)

def _scatter_add(tgt, idx, src, axis=0):
    return tgt.at[idx].add(src)

def _segment_sum(src, seg, n):
    return jax.ops.segment_sum(src, seg, n)
kernel_name = 'mk_flamingo_gated_d2_seqx_r4_d0dbe0'

def setup_inputs(seed: int=0):
    np.random.seed(seed)
    _w = jnp.asarray

    def _rec_inputs():
        import jax
        import jax.numpy as jnp
        _rk = jax.random.key(seed)
        x = 7.22e-05 + 1 * jax.random.normal(jax.random.fold_in(_rk, 1), (4, 512, 512), jnp.float32)
        _lenS = 512 - jax.random.randint(jax.random.fold_in(_rk, 7), (4,), 0, max(1, 512 // 4) + 1, jnp.int32)
        _lenS2 = 512 - jax.random.randint(jax.random.fold_in(_rk, 8), (4,), 0, max(1, 512 // 4) + 1, jnp.int32)
        _ctx_512P = jax.random.normal(jax.random.fold_in(_rk, 11), (4, 16, 128), jnp.float32)
        _ctx_512c = jax.random.dirichlet(jax.random.fold_in(_rk, 511), 0.3 * jnp.ones((16,), jnp.float32), (4, 512))
        _ctx_512t = jnp.einsum('bsk,bkd->bsd', _ctx_512c, _ctx_512P)
        _ctx_512t = _ctx_512t * jax.lax.rsqrt(jnp.mean(jnp.square(_ctx_512t)) + 1e-12) * 0.953939
        ctx_512 = -0.000514642 + 1.00011 * (_ctx_512t + 0.3 * jax.random.normal(jax.random.fold_in(_rk, 611), (4, 512, 128), jnp.float32))
        _g = jax.random.normal(jax.random.fold_in(_rk, 9001), (2, 2), jnp.float32)
        _g = jnp.sign(_g) * jnp.maximum(jnp.abs(_g), 1.0) + (_g == 0) * 1.0
        g_xattn = _g[0]
        g_ffn = _g[1]
        return (x, ctx_512, g_xattn, g_ffn)
    x, ctx_512, g_xattn, g_ffn = _rec_inputs()

    def _L0_xattn_setup():
        import jax, jax.numpy as jnp
        import numpy as np
        B, S, E = (2, 512, 512)
        QH, KVH = (32, 8)
        D = E // QH
        G = QH // KVH
        DROPOUT = 1.0
        key = jax.random.key(seed)
        k1, k2, k3 = jax.random.split(key, 3)
        q = jax.random.normal(k1, (B, S, E), dtype=jnp.float32)
        k = jax.random.normal(k2, (B, S, E // G), dtype=jnp.float32)
        v = jax.random.normal(k3, (B, S, E // G), dtype=jnp.float32)
        return {'q': q, 'k': k, 'v': v}
    _L0_xattn_all = _L0_xattn_setup()
    _L0_xattn_in = {k: v for k, v in _L0_xattn_all.items() if k in ()}
    del _L0_xattn_all

    def _L0_ffn_setup():
        import jax, jax.numpy as jnp
        import numpy as np
        H = 512
        E = 8
        TOPK = 2
        I_MOE = 256
        I_SH = 1024

        def _silu_and_mul(gu):
            g, u = jnp.split(gu, 2, axis=-1)
            return jax.nn.silu(g) * u
        key = jax.random.key(seed)
        ks = jax.random.split(key, 6)
        s = lambda *sh: 1.0 / np.sqrt(sh[-2])
        hidden_states = jax.random.normal(ks[0], (2, 256, H), dtype=jnp.float32)
        w_gate = jax.random.normal(ks[1], (H, E), dtype=jnp.float32) * (1.0 / np.sqrt(H))
        w_gate_up = jax.random.normal(ks[2], (E, H, 2 * I_MOE), dtype=jnp.float32) * (1.0 / np.sqrt(H))
        w_down = jax.random.normal(ks[3], (E, I_MOE, H), dtype=jnp.float32) * (1.0 / np.sqrt(I_MOE))
        w_sh_gate_up = jax.random.normal(ks[4], (H, 2 * I_SH), dtype=jnp.float32) * (1.0 / np.sqrt(H))
        w_sh_down = jax.random.normal(ks[5], (I_SH, H), dtype=jnp.float32) * (1.0 / np.sqrt(I_SH))
        return {'hidden_states': hidden_states, 'w_gate': w_gate, 'w_gate_up': w_gate_up, 'w_down': w_down, 'w_sh_gate_up': w_sh_gate_up, 'w_sh_down': w_sh_down}
    _L0_ffn_all = _L0_ffn_setup()
    _L0_ffn_in = {k: v for k, v in _L0_ffn_all.items() if k in ('w_gate', 'w_gate_up', 'w_down', 'w_sh_gate_up', 'w_sh_down')}
    del _L0_ffn_all

    def _L1_xattn_setup():
        import jax, jax.numpy as jnp
        import numpy as np
        import math
        NUM_Q_HEADS = 32
        NUM_KV_HEADS = 8
        key = jax.random.key(seed)
        k1, k2, k3 = jax.random.split(key, 3)
        B, S, E = (2, 512, 512)
        kv_E = NUM_KV_HEADS * (E // NUM_Q_HEADS)
        q = jax.random.normal(k1, (B, S, E), dtype=jnp.float32)
        k = jax.random.normal(k2, (B, S, kv_E), dtype=jnp.float32)
        v = jax.random.normal(k3, (B, S, kv_E), dtype=jnp.float32)
        return {'q': q, 'k': k, 'v': v}
    _L1_xattn_all = _L1_xattn_setup()
    _L1_xattn_in = {k: v for k, v in _L1_xattn_all.items() if k in ()}
    del _L1_xattn_all

    def _L1_ffn_setup():
        import jax, jax.numpy as jnp
        import numpy as np
        HID = 512
        N_EXP = 32
        F_EXP = 192
        TOP_K = 6
        F_SH = 384
        B, S = (1, 256)
        key = jax.random.key(seed)
        ks = jax.random.split(key, 8)
        s = 0.02
        return {'hidden_states': jax.random.normal(ks[0], (B, S, HID), dtype=jnp.float32), 'gate_w': jax.random.normal(ks[1], (HID, N_EXP), dtype=jnp.float32) * s, 'wg': jax.random.normal(ks[2], (N_EXP, HID, F_EXP), dtype=jnp.float32) * s, 'wu': jax.random.normal(ks[3], (N_EXP, HID, F_EXP), dtype=jnp.float32) * s, 'wd': jax.random.normal(ks[4], (N_EXP, F_EXP, HID), dtype=jnp.float32) * s, 'sg': jax.random.normal(ks[5], (HID, F_SH), dtype=jnp.float32) * s, 'su': jax.random.normal(ks[6], (HID, F_SH), dtype=jnp.float32) * s, 'sd': jax.random.normal(ks[7], (F_SH, HID), dtype=jnp.float32) * s}
    _L1_ffn_all = _L1_ffn_setup()
    _L1_ffn_in = {k: v for k, v in _L1_ffn_all.items() if k in ('gate_w', 'wg', 'wu', 'wd', 'sg', 'su', 'sd')}
    del _L1_ffn_all
    return {'x': x, 'ctx_512': ctx_512, 'g_xattn': g_xattn, 'g_ffn': g_ffn, 'L0_ffn_w_gate': _L0_ffn_in['w_gate'], 'L0_ffn_w_gate_up': _L0_ffn_in['w_gate_up'], 'L0_ffn_w_down': _L0_ffn_in['w_down'], 'L0_ffn_w_sh_gate_up': _L0_ffn_in['w_sh_gate_up'], 'L0_ffn_w_sh_down': _L0_ffn_in['w_sh_down'], 'L1_ffn_gate_w': _L1_ffn_in['gate_w'], 'L1_ffn_wg': _L1_ffn_in['wg'], 'L1_ffn_wu': _L1_ffn_in['wu'], 'L1_ffn_wd': _L1_ffn_in['wd'], 'L1_ffn_sg': _L1_ffn_in['sg'], 'L1_ffn_su': _L1_ffn_in['su'], 'L1_ffn_sd': _L1_ffn_in['sd']}

def reference(x, ctx_512, g_xattn, g_ffn, L0_ffn_w_gate, L0_ffn_w_gate_up, L0_ffn_w_down, L0_ffn_w_sh_gate_up, L0_ffn_w_sh_down, L1_ffn_gate_w, L1_ffn_wg, L1_ffn_wu, L1_ffn_wd, L1_ffn_sg, L1_ffn_su, L1_ffn_sd):
    import jax
    import jax.numpy as jnp

    def _L0_xattn_ref(q, k, v):
        import jax, jax.numpy as jnp
        import numpy as np
        B, S, E = (2, 512, 512)
        QH, KVH = (32, 8)
        D = E // QH
        G = QH // KVH
        DROPOUT = 1.0
        b, s, _ = q.shape
        qh = q.reshape(b, s, KVH, G, D).transpose(0, 2, 3, 1, 4)
        kh = k.reshape(b, s, KVH, D).transpose(0, 2, 1, 3)
        vh = v.reshape(b, s, KVH, D).transpose(0, 2, 1, 3)
        scale = 1.0 / jnp.sqrt(jnp.float32(D))
        scores = jnp.einsum('bkgsd,bktd->bkgst', qh, kh) * scale
        attn = jax.nn.softmax(scores, axis=-1) / DROPOUT
        out = jnp.einsum('bkgst,bktd->bkgsd', attn, vh)
        return out.transpose(0, 3, 1, 2, 4).reshape(b, s, E)

    def _L0_ffn_ref(hidden_states, w_gate, w_gate_up, w_down, w_sh_gate_up, w_sh_down):
        import jax, jax.numpy as jnp
        import numpy as np
        H = 512
        E = 8
        TOPK = 2
        I_MOE = 256
        I_SH = 1024

        def _silu_and_mul(gu):
            g, u = jnp.split(gu, 2, axis=-1)
            return jax.nn.silu(g) * u
        orig_shape = hidden_states.shape
        x = hidden_states.reshape(-1, orig_shape[-1])
        router_logits = x @ w_gate
        probs = jax.nn.softmax(router_logits, axis=-1)
        topk_w, topk_ids = jax.lax.top_k(probs, TOPK)
        topk_w = topk_w / jnp.sum(topk_w, axis=-1, keepdims=True)
        combine = jnp.sum(topk_w[..., None] * jax.nn.one_hot(topk_ids, E, dtype=x.dtype), axis=1)
        gu = jnp.einsum('th,ehf->etf', x, w_gate_up)
        act = _silu_and_mul(gu)
        eo = jnp.einsum('eti,eih->eth', act, w_down)
        routed = jnp.einsum('te,eth->th', combine, eo)
        shared = _silu_and_mul(x @ w_sh_gate_up) @ w_sh_down
        return (routed + shared).reshape(orig_shape)

    def _L1_xattn_ref(q, k, v):
        import jax, jax.numpy as jnp
        import numpy as np
        import math
        NUM_Q_HEADS = 32
        NUM_KV_HEADS = 8
        B, S, E = q.shape
        H, KV = (NUM_Q_HEADS, NUM_KV_HEADS)
        D = E // H
        G = H // KV
        scale = math.sqrt(D)
        qh = q.reshape(B, S, KV, G, D).transpose(0, 2, 3, 1, 4)
        kh = k.reshape(B, S, KV, D).transpose(0, 2, 1, 3)
        vh = v.reshape(B, S, KV, D).transpose(0, 2, 1, 3)
        scores = jnp.einsum('bkgsd,bktd->bkgst', qh, kh) / scale
        weights = jax.nn.softmax(scores, axis=-1)
        out = jnp.einsum('bkgst,bktd->bkgsd', weights, vh)
        return out.transpose(0, 3, 1, 2, 4).reshape(B, S, E)

    def _L1_ffn_ref(hidden_states, gate_w, wg, wu, wd, sg, su, sd):
        import jax, jax.numpy as jnp
        import numpy as np
        HID = 512
        N_EXP = 32
        F_EXP = 192
        TOP_K = 6
        F_SH = 384
        B, S = (1, 256)
        orig_shape = hidden_states.shape
        x = hidden_states.reshape(-1, HID)
        scores = jax.nn.sigmoid(x @ gate_w)
        topk_w, topk_i = jax.lax.top_k(scores, TOP_K)
        topk_w = topk_w / (jnp.sum(topk_w, axis=-1, keepdims=True) + 1e-20)
        combine = jnp.sum(jax.nn.one_hot(topk_i, N_EXP, dtype=topk_w.dtype) * topk_w[..., None], axis=1)
        g = jnp.einsum('td,edf->tef', x, wg)
        u = jnp.einsum('td,edf->tef', x, wu)
        act = jax.nn.silu(g) * u
        routed = jnp.einsum('tef,efd,te->td', act, wd, combine)
        routed = routed.reshape(orig_shape)
        shared = jax.nn.silu(hidden_states @ sg) * (hidden_states @ su) @ sd
        return routed + shared
    x = x + jnp.tanh(g_xattn[0]) * _L0_xattn_ref(_layernorm(x, axis=-1), ctx_512, ctx_512)
    x = x + jnp.tanh(g_ffn[0]) * _L0_ffn_ref(_layernorm(x, axis=-1), L0_ffn_w_gate, L0_ffn_w_gate_up, L0_ffn_w_down, L0_ffn_w_sh_gate_up, L0_ffn_w_sh_down)
    x = x + jnp.tanh(g_xattn[1]) * _L1_xattn_ref(_layernorm(x, axis=-1), ctx_512, ctx_512)
    x = x + jnp.tanh(g_ffn[1]) * _L1_ffn_ref(_layernorm(x, axis=-1), L1_ffn_gate_w, L1_ffn_wg, L1_ffn_wu, L1_ffn_wd, L1_ffn_sg, L1_ffn_su, L1_ffn_sd)
    return x

_drawn_inputs = setup_inputs


def setup_inputs(seed=0):
    import zlib

    import numpy as np

    out = dict(_drawn_inputs(seed))
    spreads = {'g_ffn': (-1.0, 0.6)}
    factors = {'L1_ffn_gate_w': 6.743,
     'L1_ffn_wg': 6.234,
     'L1_ffn_wu': 6.09,
     'L1_ffn_wd': 6.098,
     'L1_ffn_sg': 5.237,
     'L1_ffn_su': 5.15,
     'L1_ffn_sd': 5.15}
    for name, (base, spread) in spreads.items():
        noise = np.random.default_rng([zlib.crc32(name.encode()), seed]).standard_normal(out[name].shape)
        drawn = base * np.exp(spread * noise) if base else spread * noise
        out[name] = jnp.asarray(drawn.astype(out[name].dtype))
    for name, factor in factors.items():
        out[name] = (out[name] * factor).astype(out[name].dtype)
    return out
```

```python
from contextlib import ExitStack

import concourse.bass as bass
from concourse import mybir

ALU = mybir.AluOpType
ACT = mybir.ActivationFunctionType
AX = mybir.AxisListType
F32 = mybir.dt.float32
F32R = mybir.dt.float32r
I32 = mybir.dt.int32

P = 128
B, S, H = 4, 512, 512
TOK = B * S
TT = TOK // P
TPB = S // P
QH, KVH = 32, 8
D = H // QH
G = QH // KVH
KVD = KVH * D
EPS = 1e-5
UNITS = B * KVH
RING = 4
LAG_MAX, LAG_NEG, LAG_EXP, LAG_OUT = 1, 2, 3, 4


def make_attention(nc, layer, t):
    x = t["x"]
    with ExitStack() as ctx:
        def sb(name, shape, dt=F32):
            return ctx.enter_context(nc.sbuf_tensor(f"{name}_{layer}", shape, dt))

        def sem(name):
            return t["sem"]("attn_" + name)

        score_ps = ctx.enter_context(nc.psum_tensor(f"score_ps_{layer}", [P, 2, 2, S], F32))
        max_ps = ctx.enter_context(nc.psum_tensor(f"max_ps_{layer}", [P, 2, S], F32))
        out_ps = ctx.enter_context(nc.psum_tensor(f"out_ps_{layer}", [P, S], F32))
        turn_ps = ctx.enter_context(nc.psum_tensor(f"turn_ps_{layer}", [P, S], F32))

        xh = sb("xh", [P, UNITS + 1, TPB * G, D])
        ctx_tok = sb("ctx_tok", [P, TT, KVD])
        ctx_unit = sb("ctx_unit", [P, UNITS + 1, TPB, D])
        stats = sb("stats", [P, TT, 6])
        mean_var = sb("mean_var", [P, TT, 2])
        rstd = sb("rstd", [P, TT])
        minus_half = sb("minus_half", [P, TT])
        gate_raw = sb("gate_raw", [P, 2])
        gate = t["gates"]
        q_stack = sb("q_stack", [P, 2, TPB * G, 4, D], F32R)
        k_stack = sb("k_stack", [P, 2, TPB, 12, D], F32R)
        q_turned = sb("q_turned", [P, RING, 2, S], F32R)
        k_turned = sb("k_turned", [P, RING, 2, S], F32R)
        v_ones = sb("v_ones", [P, RING, TPB, 32])
        maxima = sb("maxima", [P, 2, TPB, G])
        neg_max = sb("neg_max", [P, 2, TPB, 2 * G], F32R)
        neg_rows = sb("neg_rows", [2 * G, 2, S], F32R)
        probs = sb("probs", [P, 2, 2, 2, S])
        out_rows = sb("out_rows", [P, S])
        recip = sb("recip", [P, TPB * G])
        scaled = sb("scaled", [P, TPB * G, D])

        ctx_loaded, gate_loaded = sem("ctx_loaded"), sem("gate_loaded")
        ln_stats, ln_var, ln_rstd, ln_done = sem("ln_stats"), sem("ln_var"), sem("ln_rstd"), sem("ln_done")
        gate_ready, ctx_sorted, pool_set, filled = sem("gate_ready"), sem("ctx_sorted"), sem("pool_set"), sem("filled")
        q_hi, k_hi, stacked = sem("q_hi"), sem("k_hi"), sem("stacked")
        turned, turn_copied = sem("turned"), sem("turn_copied")
        max_scored, max_taken = sem("max_scored"), sem("max_taken")
        neg_hi, neg_split, neg_turned, neg_copied = sem("neg_hi"), sem("neg_split"), sem("neg_turned"), sem("neg_copied")
        neg_placed = [sem("neg_placed_even"), sem("neg_placed_odd")]
        scored, exped, v_ready, pv_done = sem("scored"), sem("exped"), sem("v_ready"), sem("pv_done")
        out_copied, out_turned = sem("out_copied"), sem("out_turned")
        recip_raw, recip_ready, out_read, x_added = sem("recip_raw"), sem("recip_ready"), sem("out_read"), sem("x_added")

        def steps(eng, step):
            for k in range(RING):
                step(0, k)
            with eng.Fori(1, UNITS // RING) as turn:
                for k in range(RING):
                    step(turn * RING, k)
            for k in range(RING):
                step(UNITS, k)

        def stage(it, k, lag):
            if isinstance(it, int) and not 0 <= it + k - lag < UNITS:
                return None
            return it + (k - lag)

        block = ctx.enter_context(nc.Block())

        @block.sync
        def _(sp):
            sp.dma_start(ctx_tok[:], t["ctx"].rearrange("b (n p) d -> p (b n) d", p=P)).then_inc(ctx_loaded, 16)
            for i, g in enumerate((t["g_xattn"], t["g_ffn"])):
                sp.dma_start(gate_raw[:, i:i + 1], g[layer:layer + 1].rearrange("(a n) -> a n", a=1).to_broadcast([P, 1])
                             ).then_inc(gate_loaded, 16)

            def step(it, k):
                u = stage(it, k, LAG_NEG)
                if u is None:
                    return
                par, slot = (k - LAG_NEG) % 2, (k - LAG_NEG) % RING
                sp.wait_ge(neg_copied, u + 1)
                for part in range(2):
                    for a in range(2):
                        row, dst = part * G + 2 * a, 64 * a + 48 + part
                        sp.dma_start(q_turned[dst:dst + 1, slot, :, :].bitcast(F32),
                                     neg_rows[row:row + 2, par, :].bitcast(F32)).then_inc(neg_placed[par], 16)

            steps(sp, step)

        @block.gpsimd
        def _(pool):
            pool.memset(minus_half[:], -0.5).then_inc(pool_set, 1)
            pool.memset(v_ones[:], 0.0).then_inc(pool_set, 1)
            pool.wait_ge(pool_set, 2)
            pool.memset(v_ones[:, :, :, D:D + 1], 1.0).then_inc(pool_set, 1)
            pool.wait_ge(ln_var, 1)
            pool.tensor_tensor(out=rstd[:], in0=mean_var[:, :, 1], in1=minus_half[:], op=ALU.pow).then_inc(ln_rstd, 1)
            pool.wait_ge(ctx_sorted, 1)
            pool.wait_ge(pool_set, 3)

            def step(it, k):
                u = stage(it, k, 0)
                if u is None:
                    return
                if not isinstance(it, int) or it + k >= RING:
                    pool.wait_ge(pv_done, 4 * it + 4 * (k - RING + 1))
                pool.tensor_copy(v_ones[:, k, :, 0:D],
                                 ctx_unit[:, bass.ds(u, 1), :, :].rearrange("p a c d -> p (a c) d")
                                 ).then_inc(v_ready, 1)

            steps(pool, step)

        @block.tensor
        def _(pe):
            ident, ident_r = t["ident"], t["ident_r"]

            def turn_q_or_k(it, k, n):
                if stage(it, k, 0) is None:
                    return
                if n == 0:
                    pe.wait_ge(stacked, it + k + 1)
                if n == 0:
                    if stage(it, k, 1) is not None:
                        pe.wait_ge(turn_copied, 4 * it + 4 * k)
                    if stage(it, k, LAG_NEG) is not None:
                        pe.wait_ge(neg_copied, it + (k - LAG_NEG + 1))
                    if stage(it, k, LAG_OUT) is not None:
                        pe.wait_ge(out_read, it + (k - LAG_OUT + 1))
                else:
                    pe.wait_ge(turn_copied, 4 * it + 4 * k + n)
                for c in range(TPB):
                    if n < 2:
                        src = q_stack[:, k % 2, G * c + 2 * n:G * c + 2 * n + 2, :, :].rearrange("p h s d -> p (h s d)")
                    else:
                        src = k_stack[:, k % 2, c, 4 * (3 - n):4 * (3 - n) + 8, :].rearrange("p s d -> p (s d)")
                    mm = pe.transpose(turn_ps[:, c * P:(c + 1) * P].bitcast(F32R), src, ident_r[:])
                mm.then_inc(turned, 1)

            def turn_neg(it, k):
                if (u := stage(it, k, LAG_NEG)) is None:
                    return
                pe.wait_ge(neg_split, u + 1)
                if stage(it, k, 1) is not None:
                    pe.wait_ge(turn_copied, 4 * it + 4 * k)
                elif (out := stage(it, k, LAG_OUT)) is not None:
                    pe.wait_ge(out_read, out)
                for c in range(TPB):
                    mm = pe.transpose(turn_ps[0:2 * G, c * P:(c + 1) * P].bitcast(F32R),
                                      neg_max[:, (k - LAG_NEG) % 2, c, :], ident_r[:])
                mm.then_inc(neg_turned, 1)

            def turn_out(it, k):
                if (u := stage(it, k, LAG_OUT)) is None:
                    return
                pe.wait_ge(out_copied, u + 1)
                if stage(it, k, LAG_NEG) is not None:
                    pe.wait_ge(neg_copied, it + (k - LAG_NEG + 1))
                elif u > 0:
                    pe.wait_ge(out_read, u)
                for c in range(TPB):
                    mm = pe.transpose(turn_ps[:, c * P:(c + 1) * P], out_rows[:, c * P:(c + 1) * P], ident[:])
                mm.then_inc(out_turned, 1)

            def score_for_max(it, k, c, h):
                if (u := stage(it, k, LAG_MAX)) is None:
                    return
                slot = (k - LAG_MAX) % RING
                n = c * G + h
                if n == 0:
                    pe.wait_ge(turn_copied, 4 * u + 4)
                first = isinstance(it, int) and it + k - LAG_MAX == 0
                if not (first and n < 2):
                    pe.wait_ge(max_taken, TPB * G * u + (n - 1))
                pe.matmul(max_ps[:, n % 2, :], q_turned[:, slot, h // 2, c * P:(c + 1) * P],
                          k_turned[:, slot, h % 2, :], start=True, stop=True).then_inc(max_scored, 1)

            def score_for_exp(it, k, c, pair):
                lag, c = (LAG_EXP, c) if c < TPB else (LAG_EXP - 1, 0)
                if (u := stage(it, k, lag)) is None:
                    return
                slot = (k - lag) % RING
                if c == 0 and pair == 0:
                    pe.wait_ge(neg_placed[(k - lag) % 2], 32 * u + (64 if (k - lag) % 2 == 0 else 32))
                first = isinstance(it, int) and it + k - lag == 0
                n = 2 * c + pair
                if not (first and n < 2):
                    pe.wait_ge(exped, 2 * TPB * u + (n - 1))
                for a in range(2):
                    mm = pe.matmul(score_ps[:, pair, a, :], k_turned[:, slot, a, c * P:(c + 1) * P],
                                   q_turned[:, slot, pair, :], start=True, stop=True)
                mm.then_inc(scored, 1)

            def probs_times_v(it, k, c):
                if (u := stage(it, k, LAG_EXP)) is None:
                    return
                slot = (k - LAG_EXP) % RING
                first = isinstance(it, int) and it + k - LAG_EXP == 0
                if c == 0:
                    pe.wait_ge(v_ready, u + 1)
                    if not first:
                        pe.wait_ge(out_copied, u + 0)
                pe.wait_ge(exped, 2 * TPB * u + 2 * c + 2)
                for h in range(G):
                    mm = pe.matmul(out_ps[32 * h:32 * h + 32, :], v_ones[:, slot, c, :],
                                   probs[:, c % 2, h // 2, h % 2, :], start=(c == 0), stop=(c == TPB - 1))
                mm.then_inc(pv_done, 1)

            def step(it, k):
                for c in range(TPB):
                    score_for_max(it, k, c, 0)
                    if c == 3:
                        turn_q_or_k(it, k, 3)
                    score_for_exp(it, k, c + 1, 0)
                    score_for_max(it, k, c, 1)
                    if c == 0:
                        turn_neg(it, k)
                    elif c == 1:
                        turn_q_or_k(it, k, 0)
                    elif c == 2:
                        turn_q_or_k(it, k, 2)
                    score_for_exp(it, k, c + 1, 1)
                    score_for_max(it, k, c, 2)
                    probs_times_v(it, k, c)
                    score_for_max(it, k, c, 3)
                    if c == 0:
                        turn_out(it, k)
                    elif c == 1:
                        turn_q_or_k(it, k, 1)

            steps(pe, step)

        @block.scalar
        def _(act):
            act.wait_ge(gate_loaded, 32)
            act.activation(gate[:], gate_raw[:], ACT.Tanh).then_inc(gate_ready, 1)
            act.wait_ge(ctx_loaded, 16)
            for b in range(B):
                ins = act.activation(ctx_unit[:, b * KVH:(b + 1) * KVH, :, :].rearrange("p g c d -> p c g d"),
                                     ctx_tok[:, b * TPB:(b + 1) * TPB, :].rearrange("p c (g d) -> p c g d", g=KVH),
                                     ACT.Copy)
            ins.then_inc(ctx_sorted, 1)

            def copy_neg(it, k):
                if (u := stage(it, k, LAG_NEG)) is None:
                    return
                act.wait_ge(neg_turned, u + 1)
                if not isinstance(it, int) or it + k - LAG_NEG >= 2:
                    par = (k - LAG_NEG) % 2
                    act.wait_ge(neg_placed[par], 32 * u + (0 if par == 0 else -32))
                act.activation(neg_rows[:, (k - LAG_NEG) % 2, :], turn_ps[0:2 * G, :], ACT.Copy).then_inc(neg_copied, 1)

            def copy_turned(it, k, n):
                if stage(it, k, 0) is None:
                    return
                act.wait_ge(turned, 4 * it + 4 * k + n + 1)
                if n == 0 and (not isinstance(it, int) or it + k >= RING):
                    act.wait_ge(pv_done, 4 * it + 4 * (k - RING + 1))
                dst = (q_turned if n < 2 else k_turned)[:, k, n % 2, :]
                act.activation(dst, turn_ps[:], ACT.Copy).then_inc(turn_copied, 1)

            def exp(it, k, c, pair):
                if (u := stage(it, k, LAG_EXP)) is None:
                    return
                first = isinstance(it, int) and it + k - LAG_EXP == 0
                act.wait_ge(scored, 2 * TPB * u + 2 * c + pair + 1)
                if not (first and c < 2):
                    act.wait_ge(pv_done, TPB * u + (c - 1))
                act.activation(probs[:, c % 2, pair, :, :], score_ps[:, pair, :, :], ACT.Exp,
                               scale=float(D) ** -0.5).then_inc(exped, 1)

            def copy_out(it, k):
                if (u := stage(it, k, LAG_OUT)) is None:
                    return
                act.wait_ge(pv_done, TPB * u + TPB)
                if not (isinstance(it, int) and it + k - LAG_OUT == 0):
                    act.wait_ge(out_turned, u + 0)
                act.activation(out_rows[:], out_ps[:], ACT.Copy).then_inc(out_copied, 1)

            def step(it, k):
                exp(it, k, 0, 0)
                copy_out(it, k)
                exp(it, k, 0, 1)
                exp(it, k, 1, 0)
                copy_neg(it, k)
                exp(it, k, 1, 1)
                exp(it, k, 2, 0)
                copy_turned(it, k, 0)
                exp(it, k, 2, 1)
                copy_turned(it, k, 1)
                exp(it, k, 3, 0)
                copy_turned(it, k, 2)
                exp(it, k, 3, 1)
                copy_turned(it, k, 3)

            steps(act, step)

        @block.vector
        def _(dve):
            dve.memset(q_stack[:].bitcast(F32), 0.0).then_inc(filled, 1)
            dve.memset(k_stack[:].bitcast(F32), 0.0).then_inc(filled, 1)
            dve.memset(xh[:, UNITS, :, :], 0.0).then_inc(filled, 1)
            dve.memset(ctx_unit[:, UNITS, :, :], 0.0).then_inc(filled, 1)
            dve.wait_ge(filled, 4)
            dve.memset(k_stack[:, :, :, 7, 0:2].bitcast(F32), 1.0).then_inc(filled, 1)
            for i in range(TT):
                dve.bn_stats(stats[:, i, :], x[:, i, :]).then_inc(ln_stats, 1)
            for i in range(TT):
                dve.wait_ge(ln_stats, i + 1)
                dve.bn_aggr(mean_var[:, i, :], stats[:, i, :]).then_inc(ln_stats, 1)
            dve.wait_ge(ln_stats, 2 * TT)
            dve.tensor_scalar(mean_var[:, :, 1], mean_var[:, :, 1], EPS, None, ALU.add).then_inc(ln_var, 1)
            dve.wait_ge(ln_rstd, 1)
            for i in range(TT):
                b, c = i // TPB, i % TPB
                dve.tensor_scalar(xh[:, b * KVH:(b + 1) * KVH, c * G:(c + 1) * G, :].rearrange("p g h d -> p g (h d)"),
                                  x[:, i, :].rearrange("p (g e) -> p g e", g=KVH),
                                  mean_var[:, i, 0:1], rstd[:, i:i + 1], ALU.subtract, ALU.mult).then_inc(ln_done, 1)
            dve.wait_ge(ln_done, TT)
            dve.wait_ge(ctx_sorted, 1)
            dve.wait_ge(filled, 5)
            dve.wait_ge(gate_ready, 1)

            def stack(it, k, n):
                if isinstance(it, int) and it + k > UNITS:
                    return
                u, par = it + k, k % 2
                q, kk = q_stack[:, par, :, :, :], k_stack[:, par, :, :, :]
                qx = xh[:, bass.ds(u, 1), :, :].rearrange("p a h d -> p (a h) d")
                kx = ctx_unit[:, bass.ds(u, 1), :, :].rearrange("p a c d -> p (a c) d")
                if n == 0:
                    if not isinstance(it, int) or it + k >= 2:
                        dve.wait_ge(turned, 4 * it + 4 * (k - 1))
                    dve.tensor_copy(q[:, :, 0:3:2, :], qx[:, :, None, :].to_broadcast([P, TPB * G, 2, D])).then_inc(q_hi, 1)
                    dve.tensor_copy(kk[:, :, 4:6, :], kx[:, :, None, :].to_broadcast([P, TPB, 2, D])).then_inc(k_hi, 1)
                else:
                    dve.wait_ge(q_hi, it + k + 1)
                    dve.tensor_tensor(q[:, :, 1, :], qx, q[:, :, 0, :].bitcast(F32), ALU.subtract)
                    dve.wait_ge(k_hi, it + k + 1)
                    dve.tensor_tensor(kk[:, :, 6, :], kx, kk[:, :, 4, :].bitcast(F32), ALU.subtract).then_inc(stacked, 1)

            def take_max(it, k, c, heads):
                if (u := stage(it, k, LAG_MAX)) is None:
                    return
                for h in heads:
                    n = c * G + h
                    dve.wait_ge(max_scored, TPB * G * u + n + 1)
                    col = 2 * (h % 2) + h // 2
                    dve.tensor_reduce(maxima[:, (k - LAG_MAX) % 2, c, col:col + 1], max_ps[:, n % 2, :],
                                      AX.X, ALU.max).then_inc(max_taken, 1)

            def split_neg(it, k):
                if (u := stage(it, k, LAG_MAX)) is None:
                    return
                par = (k - LAG_MAX) % 2
                dve.wait_ge(max_taken, TPB * G * u + TPB * G)
                if not isinstance(it, int) or it + k - LAG_MAX >= 2:
                    dve.wait_ge(neg_turned, u + (-1))
                dve.tensor_scalar(neg_max[:, par, :, 0:G], maxima[:, par, :, :], -1.0, None, ALU.mult).then_inc(neg_hi, 1)
                dve.wait_ge(neg_hi, u + 1)
                dve.scalar_tensor_tensor(neg_max[:, par, :, G:2 * G], maxima[:, par, :, :], -1.0,
                                         neg_max[:, par, :, 0:G].bitcast(F32), ALU.mult, ALU.subtract
                                         ).then_inc(neg_split, 1)

            def add_out(it, k):
                if (u := stage(it, k, LAG_OUT)) is None:
                    return
                turned_out = turn_ps[:].rearrange("p (c h e) -> p (c h) e", c=TPB, h=G)
                dve.wait_ge(out_turned, u + 1)
                if not (isinstance(it, int) and it + k - LAG_OUT == 0):
                    dve.wait_ge(out_read, u + 0)
                dve.reciprocal(recip[:], turned_out[:, :, D]).then_inc(recip_raw, 1)
                dve.wait_ge(recip_raw, u + 1)
                dve.tensor_scalar(recip[:], recip[:], gate[:, 0:1], None, ALU.mult).then_inc(recip_ready, 1)
                dve.wait_ge(recip_ready, u + 1)
                if not (isinstance(it, int) and it + k - LAG_OUT == 0):
                    dve.wait_ge(x_added, u + 0)
                dve.tensor_tensor(scaled[:], turned_out[:, :, 0:D],
                                  recip[:, :, None].to_broadcast([P, TPB * G, D]), ALU.mult).then_inc(out_read, 1)
                dve.wait_ge(out_read, u + 1)
                b, g = u // KVH, u % KVH
                xu = x[:, bass.ds(b * TPB, TPB), bass.ds(g * (G * D), G * D)]
                dve.tensor_tensor(xu, xu, scaled[:].rearrange("p (c h) d -> p c (h d)", c=TPB), ALU.add).then_inc(x_added, 1)

            stack(0, 0, 0)
            stack(0, 0, 1)

            def step(it, k):
                take_max(it, k, 0, range(G))
                take_max(it, k, 1, (0,))
                add_out(it, k)
                take_max(it, k, 1, (1, 2, 3))
                stack(it, k + 1, 0)
                take_max(it, k, 2, range(G))
                stack(it, k + 1, 1)
                take_max(it, k, 3, range(G))
                split_neg(it, k)

            steps(dve, step)
            dve.wait_ge(x_added, UNITS)


CAP = TOK
CAPT = CAP // P
SCHED = P + 8
SOFT_SEMS = ("scattered_a", "scattered_b", "gathered_a", "gathered_b", "accumulated")


def make_ffn(nc, layer, t):
    x, gate = t["x"], t["gates"][:, 1:2]
    E, F, FS, K = t["E"], t["F"], t["FS"], t["K"]
    HC = H // P
    FC = FS // P
    FK = 2
    FW = F // FK
    NBK = 2 if FC % 2 == 0 else FC
    ROWS = TOK + P
    DUMMY = E * CAPT
    with ExitStack() as ctx:
        def sb(name, shape, dt=F32):
            return ctx.enter_context(nc.sbuf_tensor(f"{name}_f{layer}", shape, dt))

        def sem(name):
            return t["sem"]("ffn_" + name)

        def soft_sem(name):
            return t["soft_sems"][layer][name]

        def dram(name, shape, dt=F32):
            return nc.dram_tensor(f"{name}_f{layer}", shape, dt, kind="Internal").ap()

        bank = ctx.enter_context(nc.psum_tensor(f"bank_f{layer}", [P, 8, 512], F32))
        xh_rows = dram("xh_rows", (ROWS, H))
        acc_rows = dram("acc_rows", (ROWS, H))
        table = dram("table", (E * CAP, 2))
        sched_dram = dram("sched_dram", (P, 2), I32)

        stats, mean_var = sb("stats", [P, TT, 6]), sb("mean_var", [P, TT, 2])
        rstd, minus_half = sb("rstd", [P, TT]), sb("minus_half", [P, TT])
        xh = sb("xh", [P, TPB, H])
        xT = sb("xT", [P, HC, TOK])
        w_router = sb("w_router", [P, HC, E])
        logits_T = sb("logits_T", [E, S])
        logits = sb("logits", [P, TT, E])
        w_sh_gate, w_sh_up = sb("w_sh_gate", [P, HC, FS]), sb("w_sh_up", [P, HC, FS])
        w_sh_down = sb("w_sh_down", [P, FC, H])
        silu_T = sb("silu_T", [P, NBK, S])
        h_T = sb("h_T", [P, FC, S])
        w_gu = sb("w_gu", [P, 2, HC, 2 * F])
        w_dn = sb("w_dn", [FW, 2, FK, H])
        zero_tile = sb("zero_tile", [P, H])
        table_sb = sb("table_sb", [P, DUMMY + 1, 2])
        blank = sb("blank", [P, CAPT, 2])
        prob, above, tied, tmp, weight, mask, row1 = (sb(n, [P, TT, E]) for n in
            ("prob", "above", "tied", "tmp", "weight", "mask", "row1"))
        rank_i, rank_a = sb("rank_i", [P, TT, E], I32), sb("rank_a", [P, TT, E], I32)
        reset_e = sb("reset_e", [P, TT, E])
        reset_t, total_t, cum_t = sb("reset_t", [P, E, TT]), sb("total_t", [P, E, TT]), sb("cum_t", [P, E, TT])
        top, top_rows = sb("top", [P, TT, 8]), sb("top_rows", [P, TT, 8])
        stat1, stat2 = sb("stat1", [P, TT]), sb("stat2", [P, TT])
        expert_base = sb("expert_base", [P, E])
        expert_base_i, token_i, tile_i = sb("expert_base_i", [P, E], I32), sb("token_i", [P, TT], I32), sb("tile_i", [P, 1], I32)
        token_f, tile_f, spare_f = sb("token_f", [P, TT]), sb("tile_f", [P, 1]), sb("spare_f", [P, 1])
        slot_idx = sb("slot_idx", [P, TT, 8], I32)
        entry = sb("entry", [P, TT, K, 2])
        tri, ones_m = sb("tri", [P, P]), sb("ones_m", [P, P])
        cnt_i, tiles_f, ends_f, ends_i = sb("cnt_i", [P, E], I32), sb("tiles_f", [P, E]), sb("ends_f", [P, E]), sb("ends_i", [P, E], I32)
        ones_e, before, before_n = sb("ones_e", [P, E]), sb("before", [P, E]), sb("before_n", [P, E])
        ncol = sb("ncol", [P, 2])
        sched_f, sched_i, turns_i = sb("sched_f", [P, 2]), sb("sched_i", [P, 2], I32), sb("turns_i", [P, 2], I32)
        sched = sb("sched", [1, SCHED, 2], I32)
        idx_in, idx_out = sb("idx_in", [P, 2], I32), sb("idx_out", [P, 2], I32)
        w_out = sb("w_out", [P, 2])
        xg, xg_T = sb("xg", [P, 2, H]), sb("xg_T", [P, HC, P])
        silu_g, h_tok, hg_T = sb("silu_g", [P, 2, F]), sb("h_tok", [P, 2, F]), sb("hg_T", [FW, FK, P])
        y_tok = sb("y_tok", [P, 2, H])

        ln_stats, ln_var, ln_rstd, ln_done = sem("ln_stats"), sem("ln_var"), sem("ln_rstd"), sem("ln_done")
        weights_in, xh_stored, const_set, blank_set, table_blank = (sem(n) for n in
            ("weights_in", "xh_stored", "const_set", "blank_set", "table_blank"))
        xt_turned, xt_copied, lT_done, lT_copied, l_turned, logits_in = (sem(n) for n in
            ("xt_turned", "xt_copied", "lT_done", "lT_copied", "l_turned", "logits_in"))
        shifted, activated, chain = sem("shifted"), sem("activated"), sem("chain")
        mask_ready, ranked, entries_ready, sched_ready = sem("mask_ready"), sem("ranked"), sem("entries_ready"), sem("sched_ready")
        scattered = [soft_sem("scattered_a"), soft_sem("scattered_b")]
        sched_out, sched_in, table_in = sem("sched_out"), sem("sched_in"), sem("table_in")
        gu_done, silu_done, h_done, y_done, y_added = (sem(n) for n in ("gu_done", "silu_done", "h_done", "y_done", "y_added"))
        acc_set, expert_w = sem("acc_set"), sem("expert_w")
        in_cols, gathered, xg_turned, xg_copied = sem("in_cols"), [soft_sem("gathered_a"), soft_sem("gathered_b")], sem("xg_turned"), sem("xg_copied")
        egu_done, esilu_done, eh_done, eh_turned, eh_copied, ey_done, ey_copied = (sem(n) for n in
            ("egu_done", "esilu_done", "eh_done", "eh_turned", "eh_copied", "ey_done", "ey_copied"))
        out_cols, accumulated, result_out = sem("out_cols"), soft_sem("accumulated"), sem("result_out")

        block = ctx.enter_context(nc.Block())

        @block.sync
        def _(sp):
            sp.dma_start(w_router[:], t["w_router"].rearrange("(c p) e -> p c e", p=P)).then_inc(weights_in, 16)
            sp.dma_start(w_sh_gate[:], t["w_sh_gate"].rearrange("(c p) f -> p c f", p=P)).then_inc(weights_in, 16)
            sp.dma_start(w_sh_up[:], t["w_sh_up"].rearrange("(c p) f -> p c f", p=P)).then_inc(weights_in, 16)
            sp.dma_start(w_sh_down[:], t["w_sh_down"].rearrange("(c p) h -> p c h", p=P)).then_inc(weights_in, 16)
            sp.wait_ge(blank_set, 1)
            sp.dma_start(xh_rows[TOK:ROWS, :], zero_tile[:]).then_inc(xh_stored, 16)
            sp.dma_start(acc_rows[TOK:ROWS, :], zero_tile[:]).then_inc(acc_set, 16)
            sp.dma_start(table.rearrange("(e p j) c -> p e (j c)", e=E, p=P),
                         blank[:].rearrange("p j c -> p (j c)")[:, None, :].to_broadcast([P, E, CAPT * 2])
                         ).then_inc(table_blank, 16)
            with sp.Fori(0, B) as b:
                sp.wait_ge(ln_done, TPB * b + TPB)
                sp.dma_start(xh_rows[bass.ds(b * S, S), :].rearrange("(n p) d -> p n d", p=P), xh[:]).then_inc(xh_stored, 16)
            sp.wait_ge(sched_ready, 1)
            sp.dma_start(sched_dram, sched_i[:]).then_inc(sched_out, 16)
            sp.wait_ge(sched_out, 16)
            sp.dma_start(sched[0:1, 0:P, :].rearrange("a i c -> a (i c)"),
                         sched_dram.rearrange("(a i) c -> a (i c)", a=1)).then_inc(sched_in, 16)
            for half in range(2):
                sp.wait_ge(scattered[half], 16 * (TT * K // 2))
            sp.dma_start(table_sb[:, 0:DUMMY, :].rearrange("p (e j) c -> p e (j c)", e=E),
                         table.rearrange("(e p j) c -> p e (j c)", e=E, p=P)).then_inc(table_in, 16)

            def load_expert(e, half):
                sp.dma_start(w_gu[:, half, :, 0:F], t["wg"](e).rearrange("a (c p) f -> p (a c) f", p=P)).then_inc(expert_w, 16)
                sp.dma_start(w_gu[:, half, :, F:2 * F], t["wu"](e).rearrange("a (c p) f -> p (a c) f", p=P)).then_inc(expert_w, 16)
                sp.dma_start(w_dn[:, half, :, :], t["wd"](e).rearrange("a (c p) h -> p (a c) h", p=FW)).then_inc(expert_w, 16)

            load_expert(0, 0)
            sp.wait_ge(expert_w, 48)
            load_expert(1, 1)
            sp.wait_ge(y_added, TT)
            sp.dma_start(acc_rows[0:TOK, :].rearrange("(n p) d -> p n d", p=P), x[:]).then_inc(acc_set, 16)
            with sp.Fori(1, E // 2) as pair:
                for half in range(2):
                    e = pair * 2 + half
                    sp.wait_ge(expert_w, 48 * e)
                    end = sp.value_load(ends_i[0:1, bass.ds(e - 2, 1)], min_val=1, max_val=P)
                    sp.wait_ge(ey_done, end)
                    load_expert(e, half)
            turns = sp.value_load(turns_i[0:1, 0:1], min_val=4, max_val=64)
            sp.wait_ge(accumulated, turns * 32 + 16)
            if layer == 0:
                sp.dma_start(x[:], acc_rows[0:TOK, :].rearrange("(n p) d -> p n d", p=P)).then_inc(result_out, 16)
            else:
                sp.dma_start(t["out"], acc_rows[0:TOK, :]).then_inc(result_out, 16)
            sp.wait_ge(result_out, 16)

        @block.gpsimd
        def _(pool):
            pool.memset(minus_half[:], -0.5).then_inc(const_set, 1)
            pool.wait_ge(ln_var, 1)
            pool.wait_ge(const_set, 1)
            pool.tensor_tensor(out=rstd[:], in0=mean_var[:, :, 1], in1=minus_half[:], op=ALU.pow).then_inc(ln_rstd, 1)
            pool.iota(tile_i[:], pattern=[[0, 1]], base=0, channel_multiplier=1).then_inc(const_set, 1)
            pool.iota(token_i[:], pattern=[[P, TT]], base=0, channel_multiplier=1).then_inc(const_set, 1)
            pool.iota(expert_base_i[:], pattern=[[CAP, E]], base=1, channel_multiplier=0).then_inc(const_set, 1)
            pool.memset(zero_tile[:], 0.0).then_inc(const_set, 1)
            pool.memset(blank[:], 0.0).then_inc(const_set, 1)
            pool.wait_ge(const_set, 6)
            pool.tensor_copy(tile_f[:], tile_i[:]).then_inc(const_set, 1)
            pool.wait_ge(const_set, 7)
            pool.tensor_scalar(blank[:, :, 0], zero_tile[:, 0:CAPT], tile_f[:, 0:1],
                               float(TOK), ALU.add, ALU.add).then_inc(blank_set, 1)
            pool.memset(tri[:], 1.0).then_inc(const_set, 1)
            pool.memset(ones_m[:], 1.0).then_inc(const_set, 1)
            pool.memset(ones_e[:], 1.0).then_inc(const_set, 1)
            pool.memset(reset_e[:], 1.0).then_inc(const_set, 1)
            pool.memset(reset_t[:], 1.0).then_inc(const_set, 1)
            pool.memset(table_sb[:, DUMMY, 1:2], 0.0).then_inc(const_set, 1)
            pool.tensor_copy(token_f[:], token_i[:]).then_inc(const_set, 1)
            pool.tensor_copy(expert_base[:], expert_base_i[:]).then_inc(const_set, 1)
            pool.memset(sched[0:1, P:SCHED, 0:1], DUMMY).then_inc(const_set, 1)
            pool.memset(sched[0:1, P:SCHED, 1:2], E - 1).then_inc(const_set, 1)
            pool.wait_ge(const_set, 17)
            pool.affine_select(out=tri[:], in_=tri[:], compare_op=ALU.is_gt, fill=0.0, base=0,
                               pattern=[[1, P]], channel_multiplier=-1).then_inc(const_set, 1)
            pool.memset(reset_e[:, :, 0:1], 0.0).then_inc(const_set, 1)
            pool.memset(reset_t[:, :, 0:1], 0.0).then_inc(const_set, 1)
            pool.wait_ge(blank_set, 1)
            pool.tensor_copy(table_sb[:, DUMMY, 0:1], blank[:, 0, 0:1]).then_inc(const_set, 1)
            pool.wait_ge(const_set, 21)

            pool.wait_ge(entries_ready, 1)
            pool.wait_ge(table_blank, 16)
            for i in range(TT):
                for k in range(K):
                    pool.indirect_dma_start(table, bass.IndirectOffsetOnAxis(ap=slot_idx[:, i, k:k + 1], axis=0),
                                            entry[:, i, k, :], None).then_inc(scattered[(i * K + k) % 2], 16)
            pool.wait_ge(table_in, 16)
            pool.wait_ge(xh_stored, 16 * (B + 1))
            pool.wait_ge(acc_set, 32)

            def gather(i, half):
                col = pool.value_load(sched[0:1, bass.ds(i, 1), 0:1].rearrange("a i c -> a (i c)"), min_val=0, max_val=DUMMY)
                pool.tensor_copy(idx_in[:, half:half + 1], table_sb[:, bass.ds(col, 1), 0:1].rearrange("p a c -> p (a c)")
                                 ).then_inc(in_cols, 1)
                pool.wait_ge(in_cols, i + 1)
                pool.nop(nofuse=True)
                pool.indirect_dma_start(xg[:, half, :], None, xh_rows,
                                        bass.IndirectOffsetOnAxis(ap=idx_in[:, half:half + 1], axis=0)
                                        ).then_inc(gathered[half], 16)

            def scatter(i, half, first=False):
                col = pool.value_load(sched[0:1, bass.ds(i, 1), 0:1].rearrange("a i c -> a (i c)"), min_val=0, max_val=DUMMY)
                pool.tensor_copy(w_out[:, half:half + 1], table_sb[:, bass.ds(col, 1), 1:2].rearrange("p a c -> p (a c)")
                                 ).then_inc(out_cols, 1)
                pool.tensor_copy(idx_out[:, half:half + 1], table_sb[:, bass.ds(col, 1), 0:1].rearrange("p a c -> p (a c)")
                                 ).then_inc(out_cols, 1)
                pool.wait_ge(out_cols, 2 * i + 2)
                pool.wait_ge(ey_copied, i + 1)
                if not first:
                    pool.wait_ge(accumulated, 16 * i)
                pool.nop(nofuse=True)
                pool.indirect_dma_start(acc_rows, bass.IndirectOffsetOnAxis(ap=idx_out[:, half:half + 1], axis=0),
                                        y_tok[:, half, :], None, compute_op=ALU.add).then_inc(accumulated, 16)

            def first():
                gather(0, 0)
                gather(1, 1)
                pool.wait_ge(xg_turned, 1)
                pool.wait_ge(gathered[0], 16)
                gather(2, 0)

            def step(i, half):
                pool.wait_ge(xg_turned, i + 1)
                gather(i + 2, half)
                scatter(i - 1, 1 - half)

            eng = pool
            eng.wait_ge(sched_in, 16)
            turns = eng.value_load(turns_i[0:1, 0:1], min_val=4, max_val=64)
            first()
            pool.wait_ge(xg_turned, 2)
            gather(3, 1)
            scatter(0, 0, first=True)
            pool.wait_ge(xg_turned, 3)
            gather(4, 0)
            scatter(1, 1)
            with eng.Fori(1, turns) as turn:
                step(turn * 2 + 1, 1)
                step(turn * 2 + 2, 0)
            scatter(turns * 2, 0)
            pool.wait_ge(gathered[0], turns * 16 + 32)

        @block.tensor
        def _(pe):
            ident = t["ident"]
            pe.wait_ge(weights_in, 64)
            with pe.Fori(0, B) as b:
                for c in range(TPB):
                    pe.wait_ge(ln_done, TPB * b + c + 1)
                    if c >= 2:
                        pe.wait_ge(xt_copied, TPB * b + (c - 1))
                    for d in range(HC):
                        mm = pe.transpose(bank[:, c % 2, d * P:(d + 1) * P], xh[:, c, d * P:(d + 1) * P], ident[:])
                    mm.then_inc(xt_turned, 1)
                pe.wait_ge(xt_copied, TPB * b + TPB)
                for d in range(HC):
                    mm = pe.matmul(bank[0:E, 2, :], w_router[:, d, :], xT[:, d, bass.ds(b * S, S)], start=(d == 0), stop=(d == HC - 1))
                mm.then_inc(lT_done, 1)
                pe.wait_ge(lT_copied, b + 1)
                pe.nop(nofuse=True)
                for c in range(TPB):
                    mm = pe.transpose(bank[:, 3, c * E:(c + 1) * E], logits_T[:, c * P:(c + 1) * P], ident[0:E, 0:E])
                mm.then_inc(l_turned, 1)
                pe.wait_ge(logits_in, b + 1)

            def shared_gu(g, f):
                n = g * FC + f
                if not isinstance(g, int) or g * FC + f >= NBK:
                    pe.wait_ge(h_done, n + (1 - NBK))
                for w, o in ((w_sh_gate, 0), (w_sh_up, 1)):
                    for d in range(HC):
                        mm = pe.matmul(bank[:, 2 * (f % NBK) + o, :], w[:, d, f * P:(f + 1) * P],
                                       xT[:, d, bass.ds(g * S, S)], start=(d == 0), stop=(d == HC - 1))
                mm.then_inc(gu_done, 1)

            def shared_group(g):
                for f in range(FC):
                    shared_gu(g, f)
                pe.wait_ge(h_done, g * FC + FC)
                for c in range(TPB):
                    if not isinstance(g, int) or c >= 2:
                        pe.wait_ge(y_added, TPB * g + (c - 1))
                    for f in range(FC):
                        mm = pe.matmul(bank[:, 6 + c % 2, :], h_T[:, f, c * P:(c + 1) * P], w_sh_down[:, f, :],
                                       start=(f == 0), stop=(f == FC - 1))
                    mm.then_inc(y_done, 1)

            def rank():
                pe.wait_ge(mask_ready, 1)
                pe.wait_ge(const_set, 21)
                for o, m in ((4, tri), (5, ones_m)):
                    mm = pe.matmul(bank[:, o, 0:TT * E], m[:], mask[:].rearrange("p t e -> p (t e)"), start=True, stop=True)
                mm.then_inc(ranked, 1)

            rank()
            pe.wait_ge(entries_ready, 1)
            shared_group(0)
            with pe.Fori(1, B) as g:
                shared_group(g)
            pe.wait_ge(y_added, TT)

            def turn_x(i, half):
                if isinstance(i, int):
                    pe.wait_ge(gathered[half], 16 * (i // 2 + 1))
                else:
                    pe.wait_ge(gathered[half], 8 * i + (16 if half == 0 else 8))
                if not isinstance(i, int) or i >= 1:
                    pe.wait_ge(xg_copied, i + 0)
                for d in range(HC):
                    mm = pe.transpose(bank[:, 6, d * P:(d + 1) * P], xg[:, half, d * P:(d + 1) * P], ident[:])
                mm.then_inc(xg_turned, 1)

            def gate_up(i, half, e):
                pe.wait_ge(expert_w, 48 * e + 48)
                pe.wait_ge(xg_copied, i + 1)
                if not isinstance(i, int) or i >= 2:
                    pe.wait_ge(eh_done, i + (-1))
                for d in range(HC):
                    mm = pe.matmul(bank[:, half, 0:2 * F], xg_T[:, d, :],
                                   w_gu[:, bass.ds(pe.snap(e % 2), 1), d, :].rearrange("p a f -> p (a f)"),
                                   start=(d == 0), stop=(d == HC - 1))
                mm.then_inc(egu_done, 1)

            def turn_h(i, half):
                pe.wait_ge(eh_done, i + 1)
                if not isinstance(i, int) or i >= 1:
                    pe.wait_ge(eh_copied, i + 0)
                for f in range(FK):
                    mm = pe.transpose(bank[0:FW, 7, f * P:(f + 1) * P], h_tok[:, half, f * FW:(f + 1) * FW], ident[:])
                mm.then_inc(eh_turned, 1)

            def down(i, half, e, before=None):
                pe.wait_ge(eh_copied, i + 1)
                if before is not None:
                    pe.wait_ge(ey_copied, before)
                elif not isinstance(i, int) or i >= 2:
                    pe.wait_ge(ey_copied, i + (-1))
                for f in range(FK):
                    mm = pe.matmul(bank[:, 2 + half, :], hg_T[:, f, :],
                                   w_dn[:, bass.ds(pe.snap(e % 2), 1), f, :].rearrange("p a f -> p (a f)"),
                                   start=(f == 0), stop=(f == FK - 1))
                mm.then_inc(ey_done, 1)

            def expert_of(i):
                return pe.value_load(sched[0:1, bass.ds(i, 1), 1:2].rearrange("a i c -> a (i c)"), min_val=0, max_val=E - 1)

            def first():
                turn_x(0, 0)
                gate_up(0, 0, expert_of(0))
                turn_x(1, 1)
                turn_h(0, 0)

            def step(i, half):
                gate_up(i, half, expert_of(i))
                turn_x(i + 1, 1 - half)
                down(i - 1, 1 - half, expert_of(i - 1))
                turn_h(i, half)

            pe.wait_ge(sched_in, 16)
            turns = pe.value_load(turns_i[0:1, 0:1], min_val=4, max_val=64)
            first()
            step(1, 1)
            step(2, 0)
            with pe.Fori(1, turns) as turn:
                step(turn * 2 + 1, 1)
                step(turn * 2 + 2, 0)
            down(turns * 2, 0, expert_of(turns * 2), pe.value_load(turns_i[0:1, 1:2], min_val=7, max_val=127))

        @block.scalar
        def _(act):
            with act.Fori(0, B) as b:
                for c in range(TPB):
                    act.wait_ge(xt_turned, TPB * b + c + 1)
                    act.activation(xT[:, :, bass.ds(b * S + c * P, P)], bank[:, c % 2, :].rearrange("p (d m) -> p d m", d=HC),
                                   ACT.Copy).then_inc(xt_copied, 1)
                act.wait_ge(lT_done, b + 1)
                act.activation(logits_T[:], bank[0:E, 2, :], ACT.Copy).then_inc(lT_copied, 1)
                act.wait_ge(l_turned, b + 1)
                act.activation(logits[:, bass.ds(b * TPB, TPB), :].rearrange("p t e -> p (t e)"),
                               bank[:, 3, 0:TPB * E], ACT.Copy).then_inc(logits_in, 1)
            if layer == 0:
                act.wait_ge(shifted, 1)
                act.activation(prob[:], above[:], ACT.Exp).then_inc(activated, 1)
            else:
                act.wait_ge(logits_in, B)
                act.activation(prob[:], logits[:], ACT.Sigmoid).then_inc(activated, 1)

            def shared(g):
                for f in range(FC):
                    n = g * FC + f
                    act.wait_ge(gu_done, n + 1)
                    if not isinstance(g, int) or g * FC + f >= NBK:
                        act.wait_ge(h_done, n + (1 - NBK))
                    act.activation(silu_T[:, f % NBK, :], bank[:, 2 * (f % NBK), :], ACT.Silu).then_inc(silu_done, 1)

            shared(0)
            with act.Fori(1, B) as g:
                shared(g)

            def silu(i, half):
                act.wait_ge(egu_done, i + 1)
                if not isinstance(i, int) or i >= 2:
                    act.wait_ge(eh_done, i + (-1))
                act.activation(silu_g[:, half, :], bank[:, half, 0:F], ACT.Silu).then_inc(esilu_done, 1)

            def y_out(i, half, before=None):
                act.wait_ge(ey_done, i + 1)
                act.wait_ge(out_cols, 2 * i + 2)
                if before is not None:
                    act.wait_ge(accumulated, 16 * before)
                elif not isinstance(i, int) or i >= 2:
                    act.wait_ge(accumulated, 16 * i + (-16))
                act.activation(y_tok[:, half, :], bank[:, 2 + half, :], ACT.Copy, scale=w_out[:, half:half + 1]
                               ).then_inc(ey_copied, 1)

            def step(i, half):
                silu(i, half)
                y_out(i - 1, 1 - half)

            act.wait_ge(sched_in, 16)
            turns = act.value_load(turns_i[0:1, 0:1], min_val=4, max_val=64)
            silu(0, 0)
            step(1, 1)
            step(2, 0)
            with act.Fori(1, turns) as turn:
                step(turn * 2 + 1, 1)
                step(turn * 2 + 2, 0)
            y_out(turns * 2, 0, act.value_load(turns_i[0:1, 1:2], min_val=7, max_val=127))

        @block.vector
        def _(dve):
            for i in range(TT):
                dve.bn_stats(stats[:, i, :], x[:, i, :]).then_inc(ln_stats, 1)
            for i in range(TT):
                dve.wait_ge(ln_stats, i + 1)
                dve.bn_aggr(mean_var[:, i, :], stats[:, i, :]).then_inc(ln_stats, 1)
            dve.wait_ge(ln_stats, 2 * TT)
            dve.tensor_scalar(mean_var[:, :, 1], mean_var[:, :, 1], EPS, None, ALU.add).then_inc(ln_var, 1)
            dve.wait_ge(ln_rstd, 1)
            for i in range(TT):
                if i >= TPB:
                    dve.wait_ge(xt_turned, i - TPB + 1)
                    dve.wait_ge(xh_stored, 16 * (i // TPB) + 16)
                dve.tensor_scalar(xh[:, i % TPB, :], x[:, i, :], mean_var[:, i, 0:1], rstd[:, i:i + 1],
                                  ALU.subtract, ALU.mult).then_inc(ln_done, 1)
            count = [0]

            def then(ins):
                count[0] += 1
                ins.then_inc(chain, 1)
                dve.wait_ge(chain, count[0])

            def over_e(a):
                return a[:, :, None].to_broadcast([P, TT, E])

            dve.wait_ge(const_set, 21)
            if layer == 0:
                dve.wait_ge(logits_in, B)
                then(dve.tensor_reduce(stat1[:], logits[:], AX.X, ALU.max))
                dve.tensor_tensor(above[:], logits[:], over_e(stat1), ALU.subtract).then_inc(shifted, 1)
                dve.wait_ge(activated, 1)
                then(dve.tensor_reduce(stat1[:], prob[:], AX.X, ALU.add))
                then(dve.reciprocal(stat2[:], stat1[:]))
                then(dve.tensor_tensor(prob[:], prob[:], over_e(stat2), ALU.mult))
            else:
                dve.wait_ge(activated, 1)
            for i in range(TT):
                ins = dve.max(top[:, i, :], prob[:, i, :])
            then(ins)
            kth = top[:, :, K - 1:K].to_broadcast([P, TT, E])
            then(dve.tensor_tensor(above[:], prob[:], kth, ALU.is_gt))
            then(dve.tensor_tensor(tied[:], prob[:], kth, ALU.is_equal))
            then(dve.tensor_reduce(stat1[:], above[:], AX.X, ALU.add))
            then(dve.tensor_scalar(stat1[:], stat1[:], -1.0, float(K), ALU.mult, ALU.add))
            flat = "p t e -> p (t e)"
            then(dve.tensor_tensor_scan(tmp[:].rearrange(flat), reset_e[:].rearrange(flat), tied[:].rearrange(flat), 0.0,
                                        ALU.mult, ALU.add))
            then(dve.tensor_tensor(tmp[:], tmp[:], over_e(stat1), ALU.is_le))
            then(dve.tensor_tensor(tied[:], tied[:], tmp[:], ALU.mult))
            dve.tensor_tensor(mask[:], above[:], tied[:], ALU.add).then_inc(mask_ready, 1)
            then(dve.tensor_reduce(stat1[:], top[:, :, 0:K], AX.X, ALU.add))
            if layer == 1:
                then(dve.tensor_scalar(stat1[:], stat1[:], 1e-20, None, ALU.add))
            then(dve.reciprocal(stat2[:], stat1[:]))
            then(dve.tensor_scalar(stat2[:], stat2[:], gate[:, 0:1], None, ALU.mult))
            then(dve.tensor_tensor(weight[:], prob[:], over_e(stat2), ALU.mult))
            dve.wait_ge(ranked, 1)
            then(dve.tensor_copy(total_t[:], bank[:, 5, 0:TT * E].rearrange("p (t e) -> p e t", t=TT)))
            flat_t = "p e t -> p (e t)"
            then(dve.tensor_tensor_scan(cum_t[:].rearrange(flat_t), reset_t[:].rearrange(flat_t), total_t[:].rearrange(flat_t),
                                        0.0, ALU.mult, ALU.add))
            then(dve.tensor_tensor(total_t[:], cum_t[:], total_t[:], ALU.subtract))
            then(dve.tensor_tensor(rank_i[:], bank[:, 4, 0:TT * E].rearrange("p (t e) -> p t e", t=TT),
                                   total_t[:].rearrange("p e t -> p t e"), ALU.add))
            then(dve.tensor_scalar(rank_a[:], rank_i[:], P - 1, CAPT.bit_length() - 1, ALU.bitwise_and, ALU.logical_shift_left))
            then(dve.tensor_scalar(rank_i[:], rank_i[:], P.bit_length() - 1, None, ALU.logical_shift_right))
            then(dve.tensor_tensor(row1[:], rank_a[:], rank_i[:], ALU.add))
            then(dve.tensor_tensor(row1[:], row1[:], expert_base[:, None, :].to_broadcast([P, TT, E]), ALU.add))
            then(dve.tensor_tensor(row1[:], row1[:], mask[:], ALU.mult))
            for i in range(TT):
                ins = dve.max(top_rows[:, i, :], row1[:, i, :])
            then(ins)
            then(dve.tensor_scalar(slot_idx[:], top_rows[:], -1.0, None, ALU.add))
            for k in range(K):
                then(dve.tensor_tensor(tmp[:], row1[:], top_rows[:, :, k:k + 1].to_broadcast([P, TT, E]), ALU.is_equal))
                then(dve.tensor_tensor(tmp[:], tmp[:], weight[:], ALU.mult))
                then(dve.tensor_reduce(entry[:, :, k, 1], tmp[:], AX.X, ALU.add))
            dve.tensor_copy(entry[:, :, :, 0], token_f[:, :, None].to_broadcast([P, TT, K])).then_inc(entries_ready, 1)
            then(dve.tensor_scalar(cnt_i[:], cum_t[:, :, TT - 1], float(P - 1), None, ALU.add))
            then(dve.tensor_scalar(cnt_i[:], cnt_i[:], P.bit_length() - 1, None, ALU.logical_shift_right))
            then(dve.tensor_scalar(tiles_f[:], cnt_i[:], 1.0, None, ALU.max))
            then(dve.tensor_tensor_scan(ends_f[:], ones_e[:], tiles_f[:], 0.0, ALU.mult, ALU.add))
            then(dve.tensor_copy(ends_i[:], ends_f[:]))
            then(dve.tensor_scalar(before[:], ends_f[:], tile_f[:, 0:1], None, ALU.is_le))
            then(dve.tensor_tensor(before_n[:], before[:], tiles_f[:], ALU.mult))
            then(dve.tensor_reduce(ncol[:, 0:1], before[:], AX.X, ALU.add))
            then(dve.tensor_reduce(ncol[:, 1:2], before_n[:], AX.X, ALU.add))
            then(dve.tensor_scalar(sched_f[:, 1:2], ncol[:, 0:1], float(E - 1), None, ALU.min))
            then(dve.tensor_scalar(sched_f[:, 0:1], ncol[:, 0:1], float(CAPT), tile_f[:, 0:1], ALU.mult, ALU.add))
            then(dve.tensor_tensor(sched_f[:, 0:1], sched_f[:, 0:1], ncol[:, 1:2], ALU.subtract))
            then(dve.tensor_scalar(sched_f[:, 0:1], sched_f[:, 0:1], float(DUMMY), None, ALU.min))
            then(dve.tensor_scalar(turns_i[:, 0:1], ends_i[:, E - 1:E], 1, None, ALU.logical_shift_right))
            then(dve.tensor_scalar(turns_i[:, 1:2], turns_i[:, 0:1], 2.0, -1.0, ALU.mult, ALU.add))
            dve.tensor_copy(sched_i[:], sched_f[:]).then_inc(sched_ready, 1)

            def shared(g):
                for f in range(FC):
                    n = g * FC + f
                    dve.wait_ge(silu_done, n + 1)
                    if f == 0 and not isinstance(g, int):
                        dve.wait_ge(y_done, TPB * g)
                    dve.tensor_tensor(h_T[:, f, :], silu_T[:, f % NBK, :], bank[:, 2 * (f % NBK) + 1, :], ALU.mult
                                      ).then_inc(h_done, 1)
                for c in range(TPB):
                    dve.wait_ge(y_done, TPB * g + c + 1)
                    xc = x[:, bass.ds(g * TPB + c, 1), :].rearrange("p a d -> p (a d)")
                    dve.scalar_tensor_tensor(xc, bank[:, 6 + c % 2, :], gate[:, 0:1], xc, ALU.mult, ALU.add).then_inc(y_added, 1)

            shared(0)
            with dve.Fori(1, B) as g:
                shared(g)

            def copy_x(i, half):
                dve.wait_ge(xg_turned, i + 1)
                if not isinstance(i, int) or i >= 1:
                    dve.wait_ge(egu_done, i + 0)
                dve.tensor_copy(xg_T[:].rearrange("p d m -> p (d m)"), bank[:, 6, :]).then_inc(xg_copied, 1)

            def times_up(i, half):
                dve.wait_ge(esilu_done, i + 1)
                if not isinstance(i, int) or i >= 2:
                    dve.wait_ge(eh_turned, i + (-1))
                dve.tensor_tensor(h_tok[:, half, :], silu_g[:, half, :], bank[:, half, F:2 * F], ALU.mult).then_inc(eh_done, 1)

            def copy_h(i, half):
                dve.wait_ge(eh_turned, i + 1)
                if not isinstance(i, int) or i >= 1:
                    dve.wait_ge(ey_done, i + 0)
                dve.tensor_copy(hg_T[:].rearrange("p f m -> p (f m)"), bank[0:FW, 7, 0:FK * P]).then_inc(eh_copied, 1)

            def step(i, half):
                times_up(i, half)
                copy_x(i + 1, 1 - half)
                copy_h(i, half)

            dve.wait_ge(sched_in, 16)
            turns = dve.value_load(turns_i[0:1, 0:1], min_val=4, max_val=64)
            copy_x(0, 0)
            times_up(0, 0)
            copy_x(1, 1)
            copy_h(0, 0)
            step(1, 1)
            step(2, 0)
            with dve.Fori(1, turns) as turn:
                step(turn * 2 + 1, 1)
                step(turn * 2 + 2, 0)


INPUTS = ["x", "ctx_512", "g_xattn", "g_ffn",
          "L0_ffn_w_gate", "L0_ffn_w_gate_up", "L0_ffn_w_down", "L0_ffn_w_sh_gate_up", "L0_ffn_w_sh_down",
          "L1_ffn_gate_w", "L1_ffn_wg", "L1_ffn_wu", "L1_ffn_wd", "L1_ffn_sg", "L1_ffn_su", "L1_ffn_sd"]


def build_program(nc, arg, out):
    with ExitStack() as ctx:
        x = ctx.enter_context(nc.sbuf_tensor("x_res", [P, TT, H], F32))
        ident = ctx.enter_context(nc.sbuf_tensor("ident", [P, P], F32))
        ident_r = ctx.enter_context(nc.sbuf_tensor("ident_r", [P, P], F32R))
        gates = ctx.enter_context(nc.sbuf_tensor("gates", [P, 2], F32))
        x_loaded = ctx.enter_context(nc.semaphore("x_loaded"))
        ident_made = ctx.enter_context(nc.semaphore("ident_made"))
        soft_sems = [{name: ctx.enter_context(nc.semaphore(f"{name}_{layer}")) for name in SOFT_SEMS}
                     for layer in range(2)]
        sems = {}

        def sem(name):
            if name not in sems:
                sems[name] = ctx.enter_context(nc.semaphore(name))
            return sems[name]

        with nc.Block() as block:
            @block.sync
            def _(sp):
                sp.dma_start(x[:], arg["x"].rearrange("b (n p) d -> p (b n) d", p=P)).then_inc(x_loaded, 16)
                sp.wait_ge(x_loaded, 16)

            @block.gpsimd
            def _(pool):
                pool.memset(ident[:], 0.0).then_inc(ident_made, 1)
                pool.wait_ge(ident_made, 1)
                pool.affine_select(out=ident[:], in_=ident[:], compare_op=ALU.not_equal, fill=1.0, base=0,
                                   pattern=[[-1, P]], channel_multiplier=1).then_inc(ident_made, 1)

            @block.vector
            def _(dve):
                dve.wait_ge(ident_made, 2)
                dve.tensor_copy(ident_r[:], ident[:]).then_inc(ident_made, 1)

        shared = {"sem": sem, "soft_sems": soft_sems, "x": x, "ident": ident, "ident_r": ident_r, "gates": gates,
                  "ctx": arg["ctx_512"], "g_xattn": arg["g_xattn"], "g_ffn": arg["g_ffn"],
                  "out": out.rearrange("b s d -> (b s) d")}
        w_sh_gu, w_gu = arg["L0_ffn_w_sh_gate_up"], arg["L0_ffn_w_gate_up"]
        layer0 = dict(shared, E=8, F=256, FS=1024, K=2, w_router=arg["L0_ffn_w_gate"],
                      w_sh_gate=w_sh_gu[:, 0:1024], w_sh_up=w_sh_gu[:, 1024:2048], w_sh_down=arg["L0_ffn_w_sh_down"],
                      wg=lambda e: w_gu[bass.ds(e, 1), :, 0:256],
                      wu=lambda e: w_gu[bass.ds(e, 1), :, 256:512],
                      wd=lambda e: arg["L0_ffn_w_down"][bass.ds(e, 1), :, :])
        layer1 = dict(shared, E=32, F=192, FS=384, K=6, w_router=arg["L1_ffn_gate_w"],
                      w_sh_gate=arg["L1_ffn_sg"], w_sh_up=arg["L1_ffn_su"], w_sh_down=arg["L1_ffn_sd"],
                      wg=lambda e: arg["L1_ffn_wg"][bass.ds(e, 1), :, :],
                      wu=lambda e: arg["L1_ffn_wu"][bass.ds(e, 1), :, :],
                      wd=lambda e: arg["L1_ffn_wd"][bass.ds(e, 1), :, :])
        make_attention(nc, 0, layer0)
        make_ffn(nc, 0, layer0)
        numbers = [handle.num for handle in sems.values()]
        nc.all_engine_barrier(sems_to_clear=range(min(numbers), max(numbers) + 1))
        make_attention(nc, 1, layer1)
        make_ffn(nc, 1, layer1)


def kernel(**inputs):
    import numpy as np
    import concourse.bacc as bacc
    from concourse.bass_utils import run_bass_kernel_spmd

    nc = bacc.Bacc("TRN2", target_bir_lowering=False, num_devices=1)
    arrays, arg = {}, {}
    for name in INPUTS:
        a = np.ascontiguousarray(inputs[name])
        arrays[f"in_{name}"] = a
        arg[name] = nc.dram_tensor(f"in_{name}", a.shape, mybir.dt.from_np(a.dtype), kind="ExternalInput").ap()
    out = nc.dram_tensor("out_x", (B, S, H), F32, kind="ExternalOutput").ap()
    build_program(nc, arg, out)
    result = run_bass_kernel_spmd(nc, [arrays], core_ids=[0])
    return result.results[0]["out_x"]
```

```python
from contextlib import ExitStack

import concourse.bass as bass
from concourse import mybir

ALU = mybir.AluOpType
ACT = mybir.ActivationFunctionType
AX = mybir.AxisListType
F32 = mybir.dt.float32
F32R = mybir.dt.float32r
I32 = mybir.dt.int32

P = 128
B, S, H = 4, 512, 512
TOK = B * S
TT = TOK // P
TPB = S // P
QH, KVH = 32, 8
D = H // QH
G = QH // KVH
KVD = KVH * D
EPS = 1e-5
UNITS = B * KVH
RING = 4
LAG_MAX, LAG_NEG, LAG_EXP, LAG_OUT = 1, 2, 3, 4


TURN_NEG_AT, TURN_OUT_AT, TURN_AT, PV_AT = 1, 3, (6, 7, 10, 12), 2
COPY_OUT_AT, COPY_NEG_AT, COPY_TURN_AT, SCALE_AT = 1, 2, (4, 5, 6, 7), 4


def make_attention(nc, layer, t):
    x = t["x"]
    with ExitStack() as ctx:
        def sb(name, shape, dt=F32):
            return ctx.enter_context(nc.sbuf_tensor(f"{name}_{layer}", shape, dt))

        def sem(name):
            return t["sem"]("attn_" + name)

        score_ps = ctx.enter_context(nc.psum_tensor(f"score_ps_{layer}", [P, 2, 2, S], F32))
        max_ps = ctx.enter_context(nc.psum_tensor(f"max_ps_{layer}", [P, 2, S], F32))
        out_ps = ctx.enter_context(nc.psum_tensor(f"out_ps_{layer}", [P, S], F32))
        turn_ps = ctx.enter_context(nc.psum_tensor(f"turn_ps_{layer}", [P, S], F32))

        xh = sb("xh", [P, UNITS + 1, TPB * G, D])
        ctx_tok = sb("ctx_tok", [P, TT, KVD])
        ctx_unit = sb("ctx_unit", [P, UNITS + 1, TPB, D])
        stats = sb("stats", [P, TT, 6])
        mean_var = sb("mean_var", [P, TT, 2])
        rstd = sb("rstd", [P, TT])
        minus_half = sb("minus_half", [P, TT])
        gate_raw = sb("gate_raw", [P, 2])
        gate = t["gates"]
        q_stack = sb("q_stack", [P, 2, TPB * G, 4, D], F32R)
        k_stack = sb("k_stack", [P, 2, TPB, 12, D], F32R)
        q_turned = sb("q_turned", [P, RING, 2, S], F32R)
        k_turned = sb("k_turned", [P, RING, 2, S], F32R)
        v_ones = sb("v_ones", [P, RING, TPB, 32])
        maxima = sb("maxima", [P, 2, TPB, G])
        neg_max = sb("neg_max", [P, 2, TPB, 2 * G], F32R)
        neg_rows = sb("neg_rows", [2 * G, 2, S], F32R)
        probs = sb("probs", [P, 2, 2, 2, S])
        out_rows = sb("out_rows", [P, S])
        recip = sb("recip", [P, TPB * G])
        scaled = sb("scaled", [P, TPB * G, D])

        ctx_loaded, gate_loaded = sem("ctx_loaded"), sem("gate_loaded")
        x_loaded = [sem(f"x_loaded_{b}") for b in range(B)]
        ln_stats, ln_var, ln_rstd, ln_done = sem("ln_stats"), sem("ln_var"), sem("ln_rstd"), sem("ln_done")
        gate_ready, ctx_sorted, pool_set, filled = sem("gate_ready"), sem("ctx_sorted"), sem("pool_set"), sem("filled")
        q_hi, k_hi, stacked = sem("q_hi"), sem("k_hi"), sem("stacked")
        turned, turn_copied = sem("turned"), sem("turn_copied")
        max_scored, max_taken = sem("max_scored"), sem("max_taken")
        neg_hi, neg_split, neg_turned, neg_copied = sem("neg_hi"), sem("neg_split"), sem("neg_turned"), sem("neg_copied")
        neg_placed = [sem("neg_placed_even"), sem("neg_placed_odd")]
        scored, exped, v_ready, pv_done = sem("scored"), sem("exped"), sem("v_ready"), sem("pv_done")
        out_copied, out_turned = sem("out_copied"), sem("out_turned")
        recip_raw, recip_ready, out_read, x_added = sem("recip_raw"), sem("recip_ready"), sem("out_read"), sem("x_added")

        def steps(eng, step):
            for k in range(RING):
                step(0, k)
            with eng.Fori(1, UNITS // RING) as turn:
                for k in range(RING):
                    step(turn * RING, k)
            for k in range(RING):
                step(UNITS, k)

        def stage(it, k, lag):
            if isinstance(it, int) and not 0 <= it + k - lag < UNITS:
                return None
            return it + (k - lag)

        block = ctx.enter_context(nc.Block())

        @block.sync
        def _(sp):
            def load_x(b):
                sp.dma_start(x[:, b * TPB:(b + 1) * TPB, :],
                             t["x_rows"][b * S:(b + 1) * S, :].rearrange("(n p) d -> p n d", p=P)).then_inc(x_loaded[b], 16)

            load_x(0)
            sp.dma_start(ctx_tok[:], t["ctx"].rearrange("b (n p) d -> p (b n) d", p=P)).then_inc(ctx_loaded, 16)
            for i, g in enumerate((t["g_xattn"], t["g_ffn"])):
                sp.dma_start(gate_raw[:, i:i + 1], g[layer:layer + 1].rearrange("(a n) -> a n", a=1).to_broadcast([P, 1])
                             ).then_inc(gate_loaded, 16)
            for b in range(1, B):
                load_x(b)

            def step(it, k):
                u = stage(it, k, LAG_NEG)
                if u is None:
                    return
                par, slot = (k - LAG_NEG) % 2, (k - LAG_NEG) % RING
                sp.wait_ge(neg_copied, u + 1)
                for part in range(2):
                    for a in range(2):
                        row, dst = part * G + 2 * a, 64 * a + 48 + part
                        sp.dma_start(q_turned[dst:dst + 1, slot, :, :].bitcast(F32),
                                     neg_rows[row:row + 2, par, :].bitcast(F32)).then_inc(neg_placed[par], 16)

            steps(sp, step)

        @block.gpsimd
        def _(pool):
            pool.memset(minus_half[:], -0.5).then_inc(pool_set, 1)
            pool.memset(v_ones[:], 0.0).then_inc(pool_set, 1)
            pool.wait_ge(pool_set, 2)
            pool.memset(v_ones[:, :, :, D:D + 1], 1.0).then_inc(pool_set, 1)
            pool.wait_ge(pool_set, 3)

            def root(b):
                tiles = slice(b * TPB, (b + 1) * TPB)
                pool.wait_ge(ln_var, b + 1)
                pool.tensor_tensor(out=rstd[:, tiles], in0=mean_var[:, tiles, 1], in1=minus_half[:, tiles], op=ALU.pow
                                   ).then_inc(ln_rstd, 1)


            def stack(it, k):
                if isinstance(it, int) and it + k >= UNITS:
                    return
                u, par = it + k, k % 2
                q, kk = q_stack[:, par, :, :, :], k_stack[:, par, :, :, :]
                qx = xh[:, bass.ds(u, 1), :, :].rearrange("p a h d -> p (a h) d")
                kx = ctx_unit[:, bass.ds(u, 1), :, :].rearrange("p a c d -> p (a c) d")
                if not isinstance(it, int) or it + k >= 2:
                    pool.wait_ge(turned, 4 * it + 4 * (k - 1))
                    pool.nop(nofuse=True)
                pool.tensor_copy(q[:, :, 0:3:2, :], qx[:, :, None, :].to_broadcast([P, TPB * G, 2, D])).then_inc(q_hi, 1)
                pool.tensor_copy(kk[:, :, 4:6, :], kx[:, :, None, :].to_broadcast([P, TPB, 2, D])).then_inc(k_hi, 1)
                pool.wait_ge(q_hi, it + k + 1)
                pool.nop(nofuse=True)
                pool.tensor_tensor(out=q[:, :, 1, :], in0=qx, in1=q[:, :, 0, :].bitcast(F32), op=ALU.subtract)
                pool.wait_ge(k_hi, it + k + 1)
                pool.nop(nofuse=True)
                pool.tensor_tensor(out=kk[:, :, 6, :], in0=kx, in1=kk[:, :, 4, :].bitcast(F32), op=ALU.subtract).then_inc(stacked, 1)

            def add_x(it, k):
                if (u := stage(it, k, LAG_OUT)) is None:
                    return
                b, g = u // KVH, u % KVH
                xu = x[:, bass.ds(b * TPB, TPB), bass.ds(g * (G * D), G * D)]
                pool.wait_ge(out_read, u + 1)
                pool.nop(nofuse=True)
                pool.tensor_tensor(out=xu, in0=xu, in1=scaled[:].rearrange("p (c h) d -> p c (h d)", c=TPB), op=ALU.add
                                   ).then_inc(x_added, 1)

            def put_v(it, k):
                u = stage(it, k, 0)
                if u is None:
                    return
                if not isinstance(it, int) or it + k >= RING:
                    pool.wait_ge(pv_done, 4 * it + 4 * (k - RING + 1))
                    pool.nop(nofuse=True)
                pool.tensor_copy(v_ones[:, k, :, 0:D],
                                 ctx_unit[:, bass.ds(u, 1), :, :].rearrange("p a c d -> p (a c) d")
                                 ).then_inc(v_ready, 1)

            root(0)
            pool.wait_ge(ln_done, TPB)
            pool.wait_ge(ctx_sorted, 1)
            pool.wait_ge(filled, 5)
            stack(0, 0)

            def step(it, k):
                if isinstance(it, int) and it == 0 and k < B - 1:
                    root(k + 1)
                elif isinstance(it, int) and it == 0:
                    pool.wait_ge(ln_done, TT)
                put_v(it, k)
                stack(it, k + 1)
                add_x(it, k)

            steps(pool, step)

        @block.tensor
        def _(pe):
            ident, ident_r = t["ident"], t["ident_r"]

            def turn_q_or_k(it, k, n):
                if stage(it, k, 0) is None:
                    return
                if n == 0:
                    pe.wait_ge(stacked, it + k + 1)
                if n == 0:
                    if stage(it, k, 1) is not None:
                        pe.wait_ge(turn_copied, 4 * it + 4 * k)
                    if stage(it, k, LAG_NEG) is not None:
                        pe.wait_ge(neg_copied, it + (k - LAG_NEG + 1))
                    if stage(it, k, LAG_OUT) is not None:
                        pe.wait_ge(out_read, it + (k - LAG_OUT + 1))
                else:
                    pe.wait_ge(turn_copied, 4 * it + 4 * k + n)
                for c in range(TPB):
                    if n < 2:
                        src = q_stack[:, k % 2, G * c + 2 * n:G * c + 2 * n + 2, :, :].rearrange("p h s d -> p (h s d)")
                    else:
                        src = k_stack[:, k % 2, c, 4 * (3 - n):4 * (3 - n) + 8, :].rearrange("p s d -> p (s d)")
                    mm = pe.transpose(turn_ps[:, c * P:(c + 1) * P].bitcast(F32R), src, ident_r[:])
                mm.then_inc(turned, 1)

            def turn_neg(it, k):
                if (u := stage(it, k, LAG_NEG)) is None:
                    return
                pe.wait_ge(neg_split, u + 1)
                if stage(it, k, 1) is not None:
                    pe.wait_ge(turn_copied, 4 * it + 4 * k)
                elif (out := stage(it, k, LAG_OUT)) is not None:
                    pe.wait_ge(out_read, out)
                for c in range(TPB):
                    mm = pe.transpose(turn_ps[0:2 * G, c * P:(c + 1) * P].bitcast(F32R),
                                      neg_max[:, (k - LAG_NEG) % 2, c, :], ident_r[:])
                mm.then_inc(neg_turned, 1)

            def turn_out(it, k):
                if (u := stage(it, k, LAG_OUT)) is None:
                    return
                pe.wait_ge(out_copied, u + 1)
                if stage(it, k, LAG_NEG) is not None:
                    pe.wait_ge(neg_copied, it + (k - LAG_NEG + 1))
                elif u > 0:
                    pe.wait_ge(out_read, u)
                for c in range(TPB):
                    mm = pe.transpose(turn_ps[:, c * P:(c + 1) * P], out_rows[:, c * P:(c + 1) * P], ident[:])
                mm.then_inc(out_turned, 1)

            def score_for_max(it, k, c, h):
                if (u := stage(it, k, LAG_MAX)) is None:
                    return
                slot = (k - LAG_MAX) % RING
                n = c * G + h
                if n == 0:
                    pe.wait_ge(turn_copied, 4 * u + 4)
                first = isinstance(it, int) and it + k - LAG_MAX == 0
                if not (first and n < 2):
                    pe.wait_ge(max_taken, TPB * G * u + (n - 1))
                pe.matmul(max_ps[:, n % 2, :], q_turned[:, slot, h // 2, c * P:(c + 1) * P],
                          k_turned[:, slot, h % 2, :], start=True, stop=True).then_inc(max_scored, 1)

            def score_for_exp(it, k, c, pair):
                lag, c = (LAG_EXP, c) if c < TPB else (LAG_EXP - 1, 0)
                if (u := stage(it, k, lag)) is None:
                    return
                slot = (k - lag) % RING
                if c == 0 and pair == 0:
                    pe.wait_ge(neg_placed[(k - lag) % 2], 32 * u + (64 if (k - lag) % 2 == 0 else 32))
                first = isinstance(it, int) and it + k - lag == 0
                n = 2 * c + pair
                if not (first and n < 2):
                    pe.wait_ge(exped, 2 * TPB * u + (n - 1))
                for a in range(2):
                    mm = pe.matmul(score_ps[:, pair, a, :], k_turned[:, slot, a, c * P:(c + 1) * P],
                                   q_turned[:, slot, pair, :], start=True, stop=True)
                mm.then_inc(scored, 1)

            def probs_times_v(it, k, c):
                if (u := stage(it, k, LAG_EXP)) is None:
                    return
                slot = (k - LAG_EXP) % RING
                first = isinstance(it, int) and it + k - LAG_EXP == 0
                if c == 0:
                    pe.wait_ge(v_ready, u + 1)
                    if not first:
                        pe.wait_ge(out_copied, u + 0)
                pe.wait_ge(exped, 2 * TPB * u + 2 * c + 2)
                for h in range(G):
                    mm = pe.matmul(out_ps[32 * h:32 * h + 32, :], v_ones[:, slot, c, :],
                                   probs[:, c % 2, h // 2, h % 2, :], start=(c == 0), stop=(c == TPB - 1))
                mm.then_inc(pv_done, 1)

            def step(it, k):
                for slot in range(TPB * G):
                    c, h = slot // G, slot % G
                    if h == PV_AT:
                        probs_times_v(it, k, c)
                    score_for_max(it, k, c, h)
                    if slot == TURN_NEG_AT:
                        turn_neg(it, k)
                    if slot == TURN_OUT_AT:
                        turn_out(it, k)
                    for n in range(4):
                        if slot == TURN_AT[n]:
                            turn_q_or_k(it, k, n)
                    if h % 2 == 0:
                        score_for_exp(it, k, c + 1, h // 2)

            steps(pe, step)

        @block.scalar
        def _(act):
            act.wait_ge(gate_loaded, 32)
            act.activation(gate[:], gate_raw[:], ACT.Tanh).then_inc(gate_ready, 1)
            act.wait_ge(ctx_loaded, 16)
            for b in range(B):
                ins = act.activation(ctx_unit[:, b * KVH:(b + 1) * KVH, :, :].rearrange("p g c d -> p c g d"),
                                     ctx_tok[:, b * TPB:(b + 1) * TPB, :].rearrange("p c (g d) -> p c g d", g=KVH),
                                     ACT.Copy)
            ins.then_inc(ctx_sorted, 1)

            def copy_neg(it, k):
                if (u := stage(it, k, LAG_NEG)) is None:
                    return
                act.wait_ge(neg_turned, u + 1)
                if not isinstance(it, int) or it + k - LAG_NEG >= 2:
                    par = (k - LAG_NEG) % 2
                    act.wait_ge(neg_placed[par], 32 * u + (0 if par == 0 else -32))
                act.activation(neg_rows[:, (k - LAG_NEG) % 2, :], turn_ps[0:2 * G, :], ACT.Copy).then_inc(neg_copied, 1)

            def copy_turned(it, k, n):
                if stage(it, k, 0) is None:
                    return
                act.wait_ge(turned, 4 * it + 4 * k + n + 1)
                if n == 0 and (not isinstance(it, int) or it + k >= RING):
                    act.wait_ge(pv_done, 4 * it + 4 * (k - RING + 1))
                dst = (q_turned if n < 2 else k_turned)[:, k, n % 2, :]
                act.activation(dst, turn_ps[:], ACT.Copy).then_inc(turn_copied, 1)

            def exp(it, k, c, pair):
                if (u := stage(it, k, LAG_EXP)) is None:
                    return
                first = isinstance(it, int) and it + k - LAG_EXP == 0
                act.wait_ge(scored, 2 * TPB * u + 2 * c + pair + 1)
                if not (first and c < 2):
                    act.wait_ge(pv_done, TPB * u + (c - 1))
                act.activation(probs[:, c % 2, pair, :, :], score_ps[:, pair, :, :], ACT.Exp,
                               scale=float(D) ** -0.5).then_inc(exped, 1)

            def copy_out(it, k):
                if (u := stage(it, k, LAG_OUT)) is None:
                    return
                act.wait_ge(pv_done, TPB * u + TPB)
                if not (isinstance(it, int) and it + k - LAG_OUT == 0):
                    act.wait_ge(out_turned, u + 0)
                act.activation(out_rows[:], out_ps[:], ACT.Copy).then_inc(out_copied, 1)

            def step(it, k):
                for n in range(2 * TPB):
                    exp(it, k, n // 2, n % 2)
                    if n == COPY_OUT_AT:
                        copy_out(it, k)
                    if n == COPY_NEG_AT:
                        copy_neg(it, k)
                    for turn in range(4):
                        if n == COPY_TURN_AT[turn]:
                            copy_turned(it, k, turn)

            steps(act, step)

        @block.vector
        def _(dve):
            dve.memset(q_stack[:].bitcast(F32), 0.0).then_inc(filled, 1)
            dve.memset(k_stack[:].bitcast(F32), 0.0).then_inc(filled, 1)
            dve.memset(xh[:, UNITS, :, :], 0.0).then_inc(filled, 1)
            dve.memset(ctx_unit[:, UNITS, :, :], 0.0).then_inc(filled, 1)
            dve.wait_ge(filled, 4)
            dve.memset(k_stack[:, :, :, 7, 0:2].bitcast(F32), 1.0).then_inc(filled, 1)

            def layernorm(b):
                tiles = range(b * TPB, (b + 1) * TPB)
                dve.wait_ge(x_loaded[b], 16)
                for i in tiles:
                    dve.bn_stats(stats[:, i, :], x[:, i, :]).then_inc(ln_stats, 1)
                dve.wait_ge(ln_stats, 2 * TPB * b + TPB)
                for i in tiles:
                    dve.bn_aggr(mean_var[:, i, :], stats[:, i, :]).then_inc(ln_stats, 1)
                dve.wait_ge(ln_stats, 2 * TPB * b + 2 * TPB)
                var = mean_var[:, b * TPB:(b + 1) * TPB, 1]
                dve.tensor_scalar(var, var, EPS, None, ALU.add).then_inc(ln_var, 1)
                dve.wait_ge(ln_rstd, b + 1)
                for c, i in enumerate(tiles):
                    dve.tensor_scalar(xh[:, b * KVH:(b + 1) * KVH, c * G:(c + 1) * G, :].rearrange("p g h d -> p g (h d)"),
                                      x[:, i, :].rearrange("p (g e) -> p g e", g=KVH),
                                      mean_var[:, i, 0:1], rstd[:, i:i + 1], ALU.subtract, ALU.mult).then_inc(ln_done, 1)

            layernorm(0)
            dve.wait_ge(gate_ready, 1)

            def take_max(it, k, c, heads):
                if (u := stage(it, k, LAG_MAX)) is None:
                    return
                for h in heads:
                    n = c * G + h
                    dve.wait_ge(max_scored, TPB * G * u + n + 1)
                    col = 2 * (h % 2) + h // 2
                    dve.tensor_reduce(maxima[:, (k - LAG_MAX) % 2, c, col:col + 1], max_ps[:, n % 2, :],
                                      AX.X, ALU.max).then_inc(max_taken, 1)

            def split_neg(it, k):
                if (u := stage(it, k, LAG_MAX)) is None:
                    return
                par = (k - LAG_MAX) % 2
                dve.wait_ge(max_taken, TPB * G * u + TPB * G)
                if not isinstance(it, int) or it + k - LAG_MAX >= 2:
                    dve.wait_ge(neg_turned, u + (-1))
                dve.tensor_scalar(neg_max[:, par, :, 0:G], maxima[:, par, :, :], -1.0, None, ALU.mult).then_inc(neg_hi, 1)
                dve.wait_ge(neg_hi, u + 1)
                dve.scalar_tensor_tensor(neg_max[:, par, :, G:2 * G], maxima[:, par, :, :], -1.0,
                                         neg_max[:, par, :, 0:G].bitcast(F32), ALU.mult, ALU.subtract
                                         ).then_inc(neg_split, 1)

            def scale_out(it, k):
                if (u := stage(it, k, LAG_OUT)) is None:
                    return
                turned_out = turn_ps[:].rearrange("p (c h e) -> p (c h) e", c=TPB, h=G)
                dve.wait_ge(out_turned, u + 1)
                if not (isinstance(it, int) and it + k - LAG_OUT == 0):
                    dve.wait_ge(out_read, u + 0)
                dve.reciprocal(recip[:], turned_out[:, :, D]).then_inc(recip_raw, 1)
                dve.wait_ge(recip_raw, u + 1)
                dve.tensor_scalar(recip[:], recip[:], gate[:, 0:1], None, ALU.mult).then_inc(recip_ready, 1)
                dve.wait_ge(recip_ready, u + 1)
                if not (isinstance(it, int) and it + k - LAG_OUT == 0):
                    dve.wait_ge(x_added, u + 0)
                dve.tensor_tensor(scaled[:], turned_out[:, :, 0:D],
                                  recip[:, :, None].to_broadcast([P, TPB * G, D]), ALU.mult).then_inc(out_read, 1)

            def step(it, k):
                if isinstance(it, int) and it == 0 and k < B - 1:
                    layernorm(k + 1)
                for n in range(TPB * G):
                    take_max(it, k, n // G, (n % G,))
                    if n == SCALE_AT:
                        scale_out(it, k)
                split_neg(it, k)

            steps(dve, step)
            dve.wait_ge(x_added, UNITS)


CAP = TOK
CAPT = CAP // P
SCHED = P + 8
SOFT_SEMS = ("scattered_a", "scattered_b", "gathered_a", "gathered_b", "accumulated")


def make_ffn(nc, layer, t):
    x, gate = t["x"], t["gates"][:, 1:2]
    E, F, FS, K = t["E"], t["F"], t["FS"], t["K"]
    HC = H // P
    FC = FS // P
    FK = 2
    FW = F // FK
    NBK = 2 if FC % 2 == 0 else FC
    ROWS = TOK + P
    DUMMY = E * CAPT
    with ExitStack() as ctx:
        def sb(name, shape, dt=F32):
            return ctx.enter_context(nc.sbuf_tensor(f"{name}_f{layer}", shape, dt))

        def sem(name):
            return t["sem"]("ffn_" + name)

        def soft_sem(name):
            return t["soft_sems"][layer][name]

        def dram(name, shape, dt=F32):
            return nc.dram_tensor(f"{name}_f{layer}", shape, dt, kind="Internal").ap()

        bank = ctx.enter_context(nc.psum_tensor(f"bank_f{layer}", [P, 8, 512], F32))
        xh_rows = dram("xh_rows", (ROWS, H))
        acc_rows = dram("acc_rows", (ROWS, H))
        table = dram("table", (E * CAP, 2))
        sched_dram = dram("sched_dram", (P, 2), I32)

        stats, mean_var = sb("stats", [P, TT, 6]), sb("mean_var", [P, TT, 2])
        rstd, minus_half = sb("rstd", [P, TT]), sb("minus_half", [P, TT])
        xh = sb("xh", [P, 2, TPB, H])
        xT = sb("xT", [P, HC, TOK])
        w_router = sb("w_router", [P, HC, E])
        logits_T = sb("logits_T", [E, S])
        logits = sb("logits", [P, TT, E])
        w_sh_gate, w_sh_up = sb("w_sh_gate", [P, HC, FS]), sb("w_sh_up", [P, HC, FS])
        w_sh_down = sb("w_sh_down", [P, FC, H])
        silu_T = sb("silu_T", [P, NBK, S])
        h_T = sb("h_T", [P, FC, S])
        w_gu = sb("w_gu", [P, 2, HC, 2 * F])
        w_dn = sb("w_dn", [FW, 2, FK, H])
        zero_tile = sb("zero_tile", [P, H])
        table_sb = sb("table_sb", [P, DUMMY + 1, 2])
        blank = sb("blank", [P, CAPT, 2])
        prob, above, tied, tmp, weight, mask, row1 = (sb(n, [P, TT, E]) for n in
            ("prob", "above", "tied", "tmp", "weight", "mask", "row1"))
        rank_i, rank_a = sb("rank_i", [P, TT, E], I32), sb("rank_a", [P, TT, E], I32)
        reset_e = sb("reset_e", [P, TT, E])
        reset_t, total_t, cum_t = sb("reset_t", [P, E, TT]), sb("total_t", [P, E, TT]), sb("cum_t", [P, E, TT])
        top, top_rows = sb("top", [P, TT, 8]), sb("top_rows", [P, TT, 8])
        stat1, stat2 = sb("stat1", [P, TT]), sb("stat2", [P, TT])
        expert_base = sb("expert_base", [P, E])
        expert_base_i, token_i, tile_i = sb("expert_base_i", [P, E], I32), sb("token_i", [P, TT], I32), sb("tile_i", [P, 1], I32)
        token_f, tile_f, spare_f = sb("token_f", [P, TT]), sb("tile_f", [P, 1]), sb("spare_f", [P, 1])
        slot_idx = sb("slot_idx", [P, TT, 8], I32)
        entry = sb("entry", [P, TT, K, 2])
        tri, ones_m = sb("tri", [P, P]), sb("ones_m", [P, P])
        cnt_i, tiles_f, ends_f, ends_i = sb("cnt_i", [P, E], I32), sb("tiles_f", [P, E]), sb("ends_f", [P, E]), sb("ends_i", [P, E], I32)
        ones_e, before, before_n = sb("ones_e", [P, E]), sb("before", [P, E]), sb("before_n", [P, E])
        ncol = sb("ncol", [P, 2])
        sched_f, sched_i, turns_i = sb("sched_f", [P, 2]), sb("sched_i", [P, 2], I32), sb("turns_i", [P, 2], I32)
        sched = sb("sched", [1, SCHED, 2], I32)
        idx_in, idx_out = sb("idx_in", [P, 2], I32), sb("idx_out", [P, 2], I32)
        w_out = sb("w_out", [P, 2])
        xg, xg_T = sb("xg", [P, 2, H]), sb("xg_T", [P, HC, P])
        silu_g, h_tok, hg_T = sb("silu_g", [P, 2, F]), sb("h_tok", [P, 2, F]), sb("hg_T", [FW, FK, P])
        y_tok = sb("y_tok", [P, 2, H])

        ln_stats, ln_var, ln_rstd, ln_done = sem("ln_stats"), sem("ln_var"), sem("ln_rstd"), sem("ln_done")
        weights_in, spare_stored, const_set, blank_set, table_blank = (sem(n) for n in
            ("weights_in", "spare_stored", "const_set", "blank_set", "table_blank"))
        xh_stored = [sem("xh_stored_even"), sem("xh_stored_odd")]
        xt_turned, xt_copied, lT_done, lT_copied, l_turned, logits_in = (sem(n) for n in
            ("xt_turned", "xt_copied", "lT_done", "lT_copied", "l_turned", "logits_in"))
        shifted, activated, chain = sem("shifted"), sem("activated"), sem("chain")
        mask_ready, ranked, ranks_read, y0_added = sem("mask_ready"), sem("ranked"), sem("ranks_read"), sem("y0_added")
        entries_ready, sched_ready = sem("entries_ready"), sem("sched_ready")
        scattered = [soft_sem("scattered_a"), soft_sem("scattered_b")]
        sched_out, sched_in, table_in = sem("sched_out"), sem("sched_in"), sem("table_in")
        gu_done, silu_done, h_done, y_done, y_read = (sem(n) for n in ("gu_done", "silu_done", "h_done", "y_done", "y_read"))
        acc_set, expert_w = sem("acc_set"), sem("expert_w")
        in_cols, gathered, xg_turned, xg_copied = sem("in_cols"), [soft_sem("gathered_a"), soft_sem("gathered_b")], sem("xg_turned"), sem("xg_copied")
        egu_done, esilu_done, eh_done, eh_turned, eh_copied, ey_done, ey_copied = (sem(n) for n in
            ("egu_done", "esilu_done", "eh_done", "eh_turned", "eh_copied", "ey_done", "ey_copied"))
        out_cols, accumulated, result_out = sem("out_cols"), soft_sem("accumulated"), sem("result_out")

        def y0(c):
            return (y_tok if c < 2 else xg)[:, c % 2, :]

        block = ctx.enter_context(nc.Block())

        @block.sync
        def _(sp):
            sp.dma_start(w_router[:], t["w_router"].rearrange("(c p) e -> p c e", p=P)).then_inc(weights_in, 16)
            sp.dma_start(w_sh_gate[:], t["w_sh_gate"].rearrange("(c p) f -> p c f", p=P)).then_inc(weights_in, 16)
            sp.dma_start(w_sh_up[:], t["w_sh_up"].rearrange("(c p) f -> p c f", p=P)).then_inc(weights_in, 16)
            sp.dma_start(w_sh_down[:], t["w_sh_down"].rearrange("(c p) h -> p c h", p=P)).then_inc(weights_in, 16)
            sp.wait_ge(blank_set, 1)
            sp.dma_start(xh_rows[TOK:ROWS, :], zero_tile[:]).then_inc(spare_stored, 16)
            sp.dma_start(acc_rows[TOK:ROWS, :], zero_tile[:]).then_inc(acc_set, 16)
            sp.dma_start(table.rearrange("(e p j) c -> p e (j c)", e=E, p=P),
                         blank[:].rearrange("p j c -> p (j c)")[:, None, :].to_broadcast([P, E, CAPT * 2])
                         ).then_inc(table_blank, 16)
            for b in range(B):
                sp.wait_ge(ln_done, TPB * b + TPB)
                sp.dma_start(xh_rows[b * S:(b + 1) * S, :].rearrange("(n p) d -> p n d", p=P), xh[:, b % 2, :, :]
                             ).then_inc(xh_stored[b % 2], 16)

            def load_expert(e, half):
                sp.dma_start(w_gu[:, half, :, 0:F], t["wg"](e).rearrange("a (c p) f -> p (a c) f", p=P)).then_inc(expert_w, 16)
                sp.dma_start(w_gu[:, half, :, F:2 * F], t["wu"](e).rearrange("a (c p) f -> p (a c) f", p=P)).then_inc(expert_w, 16)
                sp.dma_start(w_dn[:, half, :, :], t["wd"](e).rearrange("a (c p) h -> p (a c) h", p=FW)).then_inc(expert_w, 16)

            load_expert(0, 0)
            sp.wait_ge(expert_w, 48)
            load_expert(1, 1)
            sp.wait_ge(sched_ready, 1)
            sp.dma_start(sched_dram, sched_i[:]).then_inc(sched_out, 16)
            sp.wait_ge(sched_out, 16)
            sp.dma_start(sched[0:1, 0:P, :].rearrange("a i c -> a (i c)"),
                         sched_dram.rearrange("(a i) c -> a (i c)", a=1)).then_inc(sched_in, 16)
            with sp.Fori(1, B) as b:
                sp.wait_ge(y_read, TPB * b + TPB)
                sp.dma_start(acc_rows[bass.ds(b * S, S), :].rearrange("(n p) d -> p n d", p=P),
                             x[:, bass.ds(b * TPB, TPB), :]).then_inc(acc_set, 16)
            for half in range(2):
                sp.wait_ge(scattered[half], 16 * (TT * K // 2))
            sp.dma_start(table_sb[:, 0:DUMMY, :].rearrange("p (e j) c -> p e (j c)", e=E),
                         table.rearrange("(e p j) c -> p e (j c)", e=E, p=P)).then_inc(table_in, 16)
            sp.wait_ge(y0_added, TPB)
            sp.dma_start(acc_rows[0:S, :].rearrange("(n p) d -> p n d", p=P), x[:, 0:TPB, :]).then_inc(acc_set, 16)
            with sp.Fori(1, E // 2) as pair:
                for half in range(2):
                    e = pair * 2 + half
                    sp.wait_ge(expert_w, 48 * e)
                    end = sp.value_load(ends_i[0:1, bass.ds(e - 2, 1)], min_val=1, max_val=P)
                    sp.wait_ge(ey_done, end)
                    load_expert(e, half)
            turns = sp.value_load(turns_i[0:1, 0:1], min_val=4, max_val=64)
            sp.wait_ge(accumulated, turns * 32 + 16)
            sp.nop(nofuse=True)
            if layer == 1:
                sp.dma_start(t["out"], acc_rows[0:TOK, :]).then_inc(result_out, 16)
                sp.wait_ge(result_out, 16)

        @block.gpsimd
        def _(pool):
            pool.memset(minus_half[:], -0.5).then_inc(const_set, 1)
            pool.wait_ge(ln_var, 1)
            pool.wait_ge(const_set, 1)
            pool.tensor_tensor(out=rstd[:], in0=mean_var[:, :, 1], in1=minus_half[:], op=ALU.pow).then_inc(ln_rstd, 1)
            pool.iota(tile_i[:], pattern=[[0, 1]], base=0, channel_multiplier=1).then_inc(const_set, 1)
            pool.iota(token_i[:], pattern=[[P, TT]], base=0, channel_multiplier=1).then_inc(const_set, 1)
            pool.iota(expert_base_i[:], pattern=[[CAP, E]], base=1, channel_multiplier=0).then_inc(const_set, 1)
            pool.memset(zero_tile[:], 0.0).then_inc(const_set, 1)
            pool.memset(blank[:], 0.0).then_inc(const_set, 1)
            pool.wait_ge(const_set, 6)
            pool.tensor_copy(tile_f[:], tile_i[:]).then_inc(const_set, 1)
            pool.wait_ge(const_set, 7)
            pool.tensor_scalar(blank[:, :, 0], zero_tile[:, 0:CAPT], tile_f[:, 0:1],
                               float(TOK), ALU.add, ALU.add).then_inc(blank_set, 1)
            pool.memset(tri[:], 1.0).then_inc(const_set, 1)
            pool.memset(ones_m[:], 1.0).then_inc(const_set, 1)
            pool.memset(ones_e[:], 1.0).then_inc(const_set, 1)
            pool.memset(reset_e[:], 1.0).then_inc(const_set, 1)
            pool.memset(reset_t[:], 1.0).then_inc(const_set, 1)
            pool.memset(table_sb[:, DUMMY, 1:2], 0.0).then_inc(const_set, 1)
            pool.tensor_copy(token_f[:], token_i[:]).then_inc(const_set, 1)
            pool.tensor_copy(expert_base[:], expert_base_i[:]).then_inc(const_set, 1)
            pool.memset(sched[0:1, P:SCHED, 0:1], DUMMY).then_inc(const_set, 1)
            pool.memset(sched[0:1, P:SCHED, 1:2], E - 1).then_inc(const_set, 1)
            pool.wait_ge(const_set, 17)
            pool.affine_select(out=tri[:], in_=tri[:], compare_op=ALU.is_gt, fill=0.0, base=0,
                               pattern=[[1, P]], channel_multiplier=-1).then_inc(const_set, 1)
            pool.memset(reset_e[:, :, 0:1], 0.0).then_inc(const_set, 1)
            pool.memset(reset_t[:, :, 0:1], 0.0).then_inc(const_set, 1)
            pool.wait_ge(blank_set, 1)
            pool.tensor_copy(table_sb[:, DUMMY, 0:1], blank[:, 0, 0:1]).then_inc(const_set, 1)
            pool.wait_ge(const_set, 21)

            for f in range(FC):
                pool.wait_ge(silu_done, f + 1)
                pool.tensor_tensor(out=h_T[:, f, :], in0=silu_T[:, f % NBK, :], in1=h_T[:, f, :], op=ALU.mult
                                   ).then_inc(h_done, 1)

            pool.wait_ge(table_blank, 16)
            for k in range(K):
                pool.wait_ge(entries_ready, k + 1)
                for i in range(TT):
                    pool.indirect_dma_start(table, bass.IndirectOffsetOnAxis(ap=slot_idx[:, i, k:k + 1], axis=0),
                                            entry[:, i, k, :], None).then_inc(scattered[i % 2], 16)
            for c in range(TPB):
                pool.wait_ge(y_read, c + 1)
                pool.tensor_tensor(out=x[:, c, :], in0=x[:, c, :], in1=y0(c), op=ALU.add).then_inc(y0_added, 1)
            pool.wait_ge(table_in, 16)
            pool.wait_ge(spare_stored, 16)
            for half in range(2):
                pool.wait_ge(xh_stored[half], 16 * (B // 2))

            def gather(i, half):
                col = pool.value_load(sched[0:1, bass.ds(i, 1), 0:1].rearrange("a i c -> a (i c)"), min_val=0, max_val=DUMMY)
                pool.tensor_copy(idx_in[:, half:half + 1], table_sb[:, bass.ds(col, 1), 0:1].rearrange("p a c -> p (a c)")
                                 ).then_inc(in_cols, 1)
                pool.wait_ge(in_cols, i + 1)
                pool.nop(nofuse=True)
                pool.indirect_dma_start(xg[:, half, :], None, xh_rows,
                                        bass.IndirectOffsetOnAxis(ap=idx_in[:, half:half + 1], axis=0)
                                        ).then_inc(gathered[half], 16)

            def scatter(i, half, first=False):
                col = pool.value_load(sched[0:1, bass.ds(i, 1), 0:1].rearrange("a i c -> a (i c)"), min_val=0, max_val=DUMMY)
                pool.tensor_copy(w_out[:, half:half + 1], table_sb[:, bass.ds(col, 1), 1:2].rearrange("p a c -> p (a c)")
                                 ).then_inc(out_cols, 1)
                pool.tensor_copy(idx_out[:, half:half + 1], table_sb[:, bass.ds(col, 1), 0:1].rearrange("p a c -> p (a c)")
                                 ).then_inc(out_cols, 1)
                pool.wait_ge(out_cols, 2 * i + 2)
                pool.wait_ge(ey_copied, i + 1)
                if not first:
                    pool.wait_ge(accumulated, 16 * i)
                pool.nop(nofuse=True)
                pool.indirect_dma_start(acc_rows, bass.IndirectOffsetOnAxis(ap=idx_out[:, half:half + 1], axis=0),
                                        y_tok[:, half, :], None, compute_op=ALU.add).then_inc(accumulated, 16)

            def first():
                gather(0, 0)
                gather(1, 1)
                pool.wait_ge(xg_turned, 1)
                pool.wait_ge(gathered[0], 16)
                gather(2, 0)

            def step(i, half):
                pool.wait_ge(xg_turned, i + 1)
                gather(i + 2, half)
                scatter(i - 1, 1 - half)

            eng = pool
            eng.wait_ge(sched_in, 16)
            turns = eng.value_load(turns_i[0:1, 0:1], min_val=4, max_val=64)
            first()
            pool.wait_ge(xg_turned, 2)
            gather(3, 1)
            pool.wait_ge(acc_set, 16 * (B + 1))
            scatter(0, 0, first=True)
            pool.wait_ge(xg_turned, 3)
            gather(4, 0)
            scatter(1, 1)
            with eng.Fori(1, turns) as turn:
                step(turn * 2 + 1, 1)
                step(turn * 2 + 2, 0)
            scatter(turns * 2, 0)
            pool.wait_ge(gathered[0], turns * 16 + 32)

        @block.tensor
        def _(pe):
            ident = t["ident"]
            pe.wait_ge(weights_in, 64)

            def turn_batch(b):
                for c in range(TPB):
                    pe.wait_ge(ln_done, TPB * b + c + 1)
                    if not isinstance(b, int) or TPB * b + c >= 2:
                        pe.wait_ge(xt_copied, TPB * b + (c - 1))
                    for d in range(HC):
                        mm = pe.transpose(bank[:, c % 2, d * P:(d + 1) * P],
                                          xh[:, b % 2, c, d * P:(d + 1) * P], ident[:])
                    mm.then_inc(xt_turned, 1)

            def logits_batch(b):
                pe.wait_ge(xt_copied, TPB * b + TPB)
                if not isinstance(b, int) or b >= 1:
                    pe.wait_ge(lT_copied, b + 0)
                for d in range(HC):
                    mm = pe.matmul(bank[0:E, 2, :], w_router[:, d, :], xT[:, d, bass.ds(b * S, S)],
                                   start=(d == 0), stop=(d == HC - 1))
                mm.then_inc(lT_done, 1)

            def turn_logits(b):
                pe.wait_ge(lT_copied, b + 1)
                if not isinstance(b, int) or b >= 1:
                    pe.wait_ge(logits_in, b + 0)
                pe.nop(nofuse=True)
                for c in range(TPB):
                    mm = pe.transpose(bank[:, 3, c * E:(c + 1) * E], logits_T[:, c * P:(c + 1) * P], ident[0:E, 0:E])
                mm.then_inc(l_turned, 1)

            turn_batch(0)
            turn_batch(1)
            logits_batch(0)
            for b in range(2, B):
                turn_batch(b)
                turn_logits(b - 2)
                logits_batch(b - 1)
            turn_logits(B - 2)
            logits_batch(B - 1)
            turn_logits(B - 1)
            pe.wait_ge(logits_in, B)

            def rank():
                pe.wait_ge(mask_ready, 1)
                pe.wait_ge(const_set, 21)
                for o, m in ((6, tri), (7, ones_m)):
                    mm = pe.matmul(bank[:, o, 0:TT * E], m[:], mask[:].rearrange("p t e -> p (t e)"), start=True, stop=True)
                mm.then_inc(ranked, 1)

            def shared_gu(g, f):
                n = g * FC + f
                if not isinstance(g, int) or g * FC + f >= NBK:
                    pe.wait_ge(h_done, n + (1 - NBK))
                for w, o in ((w_sh_gate, 0), (w_sh_up, 1)):
                    for d in range(HC):
                        mm = pe.matmul(bank[:, 2 * (f % NBK) + o, :], w[:, d, f * P:(f + 1) * P],
                                       xT[:, d, bass.ds(g * S, S)], start=(d == 0), stop=(d == HC - 1))
                mm.then_inc(gu_done, 1)

            def shared_group(g):
                for f in range(FC):
                    shared_gu(g, f)
                    if isinstance(g, int) and f == 0:
                        rank()
                pe.wait_ge(h_done, g * FC + FC)
                if isinstance(g, int):
                    pe.wait_ge(ranks_read, 2)
                for c in range(TPB):
                    if not isinstance(g, int) or c >= 2:
                        pe.wait_ge(y_read, TPB * g + (c - 1))
                    for f in range(FC):
                        mm = pe.matmul(bank[:, 6 + c % 2, :], h_T[:, f, c * P:(c + 1) * P], w_sh_down[:, f, :],
                                       start=(f == 0), stop=(f == FC - 1))
                    mm.then_inc(y_done, 1)

            shared_group(0)
            with pe.Fori(1, B) as g:
                shared_group(g)
            pe.wait_ge(y_read, TT)

            def turn_x(i, half):
                if isinstance(i, int):
                    pe.wait_ge(gathered[half], 16 * (i // 2 + 1))
                else:
                    pe.wait_ge(gathered[half], 8 * i + (16 if half == 0 else 8))
                if not isinstance(i, int) or i >= 1:
                    pe.wait_ge(xg_copied, i + 0)
                for d in range(HC):
                    mm = pe.transpose(bank[:, 6, d * P:(d + 1) * P], xg[:, half, d * P:(d + 1) * P], ident[:])
                mm.then_inc(xg_turned, 1)

            def gate_up(i, half, e):
                pe.wait_ge(expert_w, 48 * e + 48)
                pe.wait_ge(xg_copied, i + 1)
                if not isinstance(i, int) or i >= 2:
                    pe.wait_ge(eh_done, i + (-1))
                for d in range(HC):
                    mm = pe.matmul(bank[:, half, 0:2 * F], xg_T[:, d, :],
                                   w_gu[:, bass.ds(pe.snap(e % 2), 1), d, :].rearrange("p a f -> p (a f)"),
                                   start=(d == 0), stop=(d == HC - 1))
                mm.then_inc(egu_done, 1)

            def turn_h(i, half):
                pe.wait_ge(eh_done, i + 1)
                if not isinstance(i, int) or i >= 1:
                    pe.wait_ge(eh_copied, i + 0)
                for f in range(FK):
                    mm = pe.transpose(bank[0:FW, 7, f * P:(f + 1) * P], h_tok[:, half, f * FW:(f + 1) * FW], ident[:])
                mm.then_inc(eh_turned, 1)

            def down(i, half, e, before=None):
                pe.wait_ge(eh_copied, i + 1)
                if before is not None:
                    pe.wait_ge(ey_copied, before)
                elif not isinstance(i, int) or i >= 2:
                    pe.wait_ge(ey_copied, i + (-1))
                for f in range(FK):
                    mm = pe.matmul(bank[:, 2 + half, :], hg_T[:, f, :],
                                   w_dn[:, bass.ds(pe.snap(e % 2), 1), f, :].rearrange("p a f -> p (a f)"),
                                   start=(f == 0), stop=(f == FK - 1))
                mm.then_inc(ey_done, 1)

            def expert_of(i):
                return pe.value_load(sched[0:1, bass.ds(i, 1), 1:2].rearrange("a i c -> a (i c)"), min_val=0, max_val=E - 1)

            def first():
                turn_x(0, 0)
                gate_up(0, 0, expert_of(0))
                turn_x(1, 1)
                turn_h(0, 0)

            def step(i, half):
                gate_up(i, half, expert_of(i))
                turn_x(i + 1, 1 - half)
                down(i - 1, 1 - half, expert_of(i - 1))
                turn_h(i, half)

            pe.wait_ge(sched_in, 16)
            turns = pe.value_load(turns_i[0:1, 0:1], min_val=4, max_val=64)
            first()
            step(1, 1)
            step(2, 0)
            with pe.Fori(1, turns) as turn:
                step(turn * 2 + 1, 1)
                step(turn * 2 + 2, 0)
            down(turns * 2, 0, expert_of(turns * 2), pe.value_load(turns_i[0:1, 1:2], min_val=7, max_val=127))

        @block.scalar
        def _(act):
            def copy_batch(b):
                for c in range(TPB):
                    act.wait_ge(xt_turned, TPB * b + c + 1)
                    act.activation(xT[:, :, bass.ds(b * S + c * P, P)], bank[:, c % 2, :].rearrange("p (d m) -> p d m", d=HC),
                                   ACT.Copy).then_inc(xt_copied, 1)

            def copy_logits_T(b):
                act.wait_ge(lT_done, b + 1)
                if b >= 1:
                    act.wait_ge(l_turned, b)
                act.activation(logits_T[:], bank[0:E, 2, :], ACT.Copy).then_inc(lT_copied, 1)

            def copy_logits(b):
                act.wait_ge(l_turned, b + 1)
                act.activation(logits[:, b * TPB:(b + 1) * TPB, :].rearrange("p t e -> p (t e)"),
                               bank[:, 3, 0:TPB * E], ACT.Copy).then_inc(logits_in, 1)

            copy_batch(0)
            copy_batch(1)
            copy_logits_T(0)
            for b in range(2, B):
                copy_batch(b)
                copy_logits(b - 2)
                copy_logits_T(b - 1)
            copy_logits(B - 2)
            copy_logits_T(B - 1)
            copy_logits(B - 1)
            if layer == 0:
                act.wait_ge(shifted, 1)
                act.activation(prob[:], above[:], ACT.Exp).then_inc(activated, 1)
            else:
                act.wait_ge(logits_in, B)
                act.activation(prob[:], logits[:], ACT.Sigmoid).then_inc(activated, 1)

            def shared(g):
                for f in range(FC):
                    n = g * FC + f
                    act.wait_ge(gu_done, n + 1)
                    if not isinstance(g, int) or g * FC + f >= NBK:
                        act.wait_ge(h_done, n + (1 - NBK))
                    if isinstance(g, int):
                        act.activation(h_T[:, f, :], bank[:, 2 * (f % NBK) + 1, :], ACT.Copy)
                    act.activation(silu_T[:, f % NBK, :], bank[:, 2 * (f % NBK), :], ACT.Silu).then_inc(silu_done, 1)
                if isinstance(g, int):
                    for c in range(TPB):
                        act.wait_ge(y_done, c + 1)
                        act.activation(y0(c), bank[:, 6 + c % 2, :], ACT.Copy, scale=gate[:, 0:1]).then_inc(y_read, 1)

            shared(0)
            with act.Fori(1, B) as g:
                shared(g)

            def silu(i, half):
                act.wait_ge(egu_done, i + 1)
                if not isinstance(i, int) or i >= 2:
                    act.wait_ge(eh_done, i + (-1))
                act.activation(silu_g[:, half, :], bank[:, half, 0:F], ACT.Silu).then_inc(esilu_done, 1)

            def y_out(i, half, before=None):
                act.wait_ge(ey_done, i + 1)
                act.wait_ge(out_cols, 2 * i + 2)
                if before is not None:
                    act.wait_ge(accumulated, 16 * before)
                elif not isinstance(i, int) or i >= 2:
                    act.wait_ge(accumulated, 16 * i + (-16))
                act.activation(y_tok[:, half, :], bank[:, 2 + half, :], ACT.Copy, scale=w_out[:, half:half + 1]
                               ).then_inc(ey_copied, 1)

            def step(i, half):
                silu(i, half)
                y_out(i - 1, 1 - half)

            act.wait_ge(sched_in, 16)
            turns = act.value_load(turns_i[0:1, 0:1], min_val=4, max_val=64)
            silu(0, 0)
            step(1, 1)
            step(2, 0)
            with act.Fori(1, turns) as turn:
                step(turn * 2 + 1, 1)
                step(turn * 2 + 2, 0)
            y_out(turns * 2, 0, act.value_load(turns_i[0:1, 1:2], min_val=7, max_val=127))

        @block.vector
        def _(dve):
            for i in range(TT):
                dve.bn_stats(stats[:, i, :], x[:, i, :]).then_inc(ln_stats, 1)
            for i in range(TT):
                dve.wait_ge(ln_stats, i + 1)
                dve.bn_aggr(mean_var[:, i, :], stats[:, i, :]).then_inc(ln_stats, 1)
            dve.wait_ge(ln_stats, 2 * TT)
            dve.tensor_scalar(mean_var[:, :, 1], mean_var[:, :, 1], EPS, None, ALU.add).then_inc(ln_var, 1)
            dve.wait_ge(ln_rstd, 1)
            for i in range(TT):
                if i >= 2 * TPB:
                    dve.wait_ge(xt_turned, i - 2 * TPB + 1)
                    dve.wait_ge(xh_stored[i // TPB % 2], 16 * (i // (2 * TPB)))
                dve.tensor_scalar(xh[:, (i // TPB) % 2, i % TPB, :], x[:, i, :], mean_var[:, i, 0:1], rstd[:, i:i + 1],
                                  ALU.subtract, ALU.mult).then_inc(ln_done, 1)
            count = [0]

            def then(ins, signal=None, value=None):
                if signal is not None:
                    ins.then_inc(signal, 1)
                    dve.wait_ge(signal, value)
                    return
                count[0] += 1
                ins.then_inc(chain, 1)
                dve.wait_ge(chain, count[0])

            def over_e(a):
                return a[:, :, None].to_broadcast([P, TT, E])

            dve.wait_ge(const_set, 21)
            if layer == 0:
                dve.wait_ge(logits_in, B)
                then(dve.tensor_reduce(stat1[:], logits[:], AX.X, ALU.max))
                dve.tensor_tensor(above[:], logits[:], over_e(stat1), ALU.subtract).then_inc(shifted, 1)
                dve.wait_ge(activated, 1)
                then(dve.tensor_reduce(stat1[:], prob[:], AX.X, ALU.add))
                then(dve.reciprocal(stat2[:], stat1[:]))
                then(dve.tensor_tensor(prob[:], prob[:], over_e(stat2), ALU.mult))
            else:
                dve.wait_ge(activated, 1)
            for i in range(TT):
                ins = dve.max(top[:, i, :], prob[:, i, :])
            then(ins)
            kth = top[:, :, K - 1:K].to_broadcast([P, TT, E])
            then(dve.tensor_tensor(above[:], prob[:], kth, ALU.is_gt))
            then(dve.tensor_tensor(tied[:], prob[:], kth, ALU.is_equal))
            then(dve.tensor_reduce(stat1[:], above[:], AX.X, ALU.add))
            then(dve.tensor_scalar(stat1[:], stat1[:], -1.0, float(K), ALU.mult, ALU.add))
            flat = "p t e -> p (t e)"
            then(dve.tensor_tensor_scan(tmp[:].rearrange(flat), reset_e[:].rearrange(flat), tied[:].rearrange(flat), 0.0,
                                        ALU.mult, ALU.add))
            then(dve.tensor_tensor(tmp[:], tmp[:], over_e(stat1), ALU.is_le))
            then(dve.tensor_tensor(tied[:], tied[:], tmp[:], ALU.mult))
            dve.tensor_tensor(mask[:], above[:], tied[:], ALU.add).then_inc(mask_ready, 1)
            then(dve.tensor_reduce(stat1[:], top[:, :, 0:K], AX.X, ALU.add))
            if layer == 1:
                then(dve.tensor_scalar(stat1[:], stat1[:], 1e-20, None, ALU.add))
            then(dve.reciprocal(stat2[:], stat1[:]))
            then(dve.tensor_scalar(stat2[:], stat2[:], gate[:, 0:1], None, ALU.mult))
            then(dve.tensor_tensor(weight[:], prob[:], over_e(stat2), ALU.mult))
            dve.wait_ge(ranked, 1)
            then(dve.tensor_copy(total_t[:], bank[:, 7, 0:TT * E].rearrange("p (t e) -> p e t", t=TT)), ranks_read, 1)
            flat_t = "p e t -> p (e t)"
            then(dve.tensor_tensor_scan(cum_t[:].rearrange(flat_t), reset_t[:].rearrange(flat_t), total_t[:].rearrange(flat_t),
                                        0.0, ALU.mult, ALU.add))
            then(dve.tensor_tensor(total_t[:], cum_t[:], total_t[:], ALU.subtract))
            then(dve.tensor_tensor(rank_i[:], bank[:, 6, 0:TT * E].rearrange("p (t e) -> p t e", t=TT),
                                   total_t[:].rearrange("p e t -> p t e"), ALU.add), ranks_read, 2)
            then(dve.tensor_scalar(rank_a[:], rank_i[:], P - 1, CAPT.bit_length() - 1, ALU.bitwise_and, ALU.logical_shift_left))
            then(dve.tensor_scalar(rank_i[:], rank_i[:], P.bit_length() - 1, None, ALU.logical_shift_right))
            then(dve.tensor_tensor(row1[:], rank_a[:], rank_i[:], ALU.add))
            then(dve.tensor_tensor(row1[:], row1[:], expert_base[:, None, :].to_broadcast([P, TT, E]), ALU.add))
            then(dve.tensor_tensor(row1[:], row1[:], mask[:], ALU.mult))
            for i in range(TT):
                ins = dve.max(top_rows[:, i, :], row1[:, i, :])
            then(ins)
            then(dve.tensor_scalar(slot_idx[:], top_rows[:], -1.0, None, ALU.add))
            then(dve.tensor_copy(entry[:, :, :, 0], token_f[:, :, None].to_broadcast([P, TT, K])))
            for k in range(K):
                then(dve.tensor_tensor(tmp[:], row1[:], top_rows[:, :, k:k + 1].to_broadcast([P, TT, E]), ALU.is_equal))
                then(dve.tensor_tensor(tmp[:], tmp[:], weight[:], ALU.mult))
                then(dve.tensor_reduce(entry[:, :, k, 1], tmp[:], AX.X, ALU.add), entries_ready, k + 1)
            then(dve.tensor_scalar(cnt_i[:], cum_t[:, :, TT - 1], float(P - 1), None, ALU.add))
            then(dve.tensor_scalar(cnt_i[:], cnt_i[:], P.bit_length() - 1, None, ALU.logical_shift_right))
            then(dve.tensor_scalar(tiles_f[:], cnt_i[:], 1.0, None, ALU.max))
            then(dve.tensor_tensor_scan(ends_f[:], ones_e[:], tiles_f[:], 0.0, ALU.mult, ALU.add))
            then(dve.tensor_copy(ends_i[:], ends_f[:]))
            then(dve.tensor_scalar(before[:], ends_f[:], tile_f[:, 0:1], None, ALU.is_le))
            then(dve.tensor_tensor(before_n[:], before[:], tiles_f[:], ALU.mult))
            then(dve.tensor_reduce(ncol[:, 0:1], before[:], AX.X, ALU.add))
            then(dve.tensor_reduce(ncol[:, 1:2], before_n[:], AX.X, ALU.add))
            then(dve.tensor_scalar(sched_f[:, 1:2], ncol[:, 0:1], float(E - 1), None, ALU.min))
            then(dve.tensor_scalar(sched_f[:, 0:1], ncol[:, 0:1], float(CAPT), tile_f[:, 0:1], ALU.mult, ALU.add))
            then(dve.tensor_tensor(sched_f[:, 0:1], sched_f[:, 0:1], ncol[:, 1:2], ALU.subtract))
            then(dve.tensor_scalar(sched_f[:, 0:1], sched_f[:, 0:1], float(DUMMY), None, ALU.min))
            then(dve.tensor_scalar(turns_i[:, 0:1], ends_i[:, E - 1:E], 1, None, ALU.logical_shift_right))
            then(dve.tensor_scalar(turns_i[:, 1:2], turns_i[:, 0:1], 2.0, -1.0, ALU.mult, ALU.add))
            dve.tensor_copy(sched_i[:], sched_f[:]).then_inc(sched_ready, 1)

            def shared(g):
                for f in range(FC):
                    n = g * FC + f
                    dve.wait_ge(silu_done, n + 1)
                    if f == 0:
                        dve.wait_ge(y_done, TPB * g)
                    dve.tensor_tensor(h_T[:, f, :], silu_T[:, f % NBK, :], bank[:, 2 * (f % NBK) + 1, :], ALU.mult
                                      ).then_inc(h_done, 1)
                for c in range(TPB):
                    dve.wait_ge(y_done, TPB * g + c + 1)
                    if c == 0:
                        dve.wait_ge(y_read, TPB * g)
                    xc = x[:, bass.ds(g * TPB + c, 1), :].rearrange("p a d -> p (a d)")
                    dve.scalar_tensor_tensor(xc, bank[:, 6 + c % 2, :], gate[:, 0:1], xc, ALU.mult, ALU.add).then_inc(y_read, 1)

            with dve.Fori(1, B) as g:
                shared(g)

            def copy_x(i, half):
                dve.wait_ge(xg_turned, i + 1)
                if not isinstance(i, int) or i >= 1:
                    dve.wait_ge(egu_done, i + 0)
                dve.tensor_copy(xg_T[:].rearrange("p d m -> p (d m)"), bank[:, 6, :]).then_inc(xg_copied, 1)

            def times_up(i, half):
                dve.wait_ge(esilu_done, i + 1)
                if not isinstance(i, int) or i >= 2:
                    dve.wait_ge(eh_turned, i + (-1))
                dve.tensor_tensor(h_tok[:, half, :], silu_g[:, half, :], bank[:, half, F:2 * F], ALU.mult).then_inc(eh_done, 1)

            def copy_h(i, half):
                dve.wait_ge(eh_turned, i + 1)
                if not isinstance(i, int) or i >= 1:
                    dve.wait_ge(ey_done, i + 0)
                dve.tensor_copy(hg_T[:].rearrange("p f m -> p (f m)"), bank[0:FW, 7, 0:FK * P]).then_inc(eh_copied, 1)

            def step(i, half):
                times_up(i, half)
                copy_x(i + 1, 1 - half)
                copy_h(i, half)

            dve.wait_ge(sched_in, 16)
            turns = dve.value_load(turns_i[0:1, 0:1], min_val=4, max_val=64)
            copy_x(0, 0)
            times_up(0, 0)
            copy_x(1, 1)
            copy_h(0, 0)
            step(1, 1)
            step(2, 0)
            with dve.Fori(1, turns) as turn:
                step(turn * 2 + 1, 1)
                step(turn * 2 + 2, 0)
    return acc_rows


INPUTS = ["x", "ctx_512", "g_xattn", "g_ffn",
          "L0_ffn_w_gate", "L0_ffn_w_gate_up", "L0_ffn_w_down", "L0_ffn_w_sh_gate_up", "L0_ffn_w_sh_down",
          "L1_ffn_gate_w", "L1_ffn_wg", "L1_ffn_wu", "L1_ffn_wd", "L1_ffn_sg", "L1_ffn_su", "L1_ffn_sd"]


def build_program(nc, arg, out):
    with ExitStack() as ctx:
        x = ctx.enter_context(nc.sbuf_tensor("x_res", [P, TT, H], F32))
        ident = ctx.enter_context(nc.sbuf_tensor("ident", [P, P], F32))
        ident_r = ctx.enter_context(nc.sbuf_tensor("ident_r", [P, P], F32R))
        gates = ctx.enter_context(nc.sbuf_tensor("gates", [P, 2], F32))
        ident_made = ctx.enter_context(nc.semaphore("ident_made"))
        soft_sems = [{name: ctx.enter_context(nc.semaphore(f"{name}_{layer}")) for name in SOFT_SEMS}
                     for layer in range(2)]
        sems = {}

        def sem(name):
            if name not in sems:
                sems[name] = ctx.enter_context(nc.semaphore(name))
            return sems[name]

        with nc.Block() as block:
            @block.gpsimd
            def _(pool):
                pool.memset(ident[:], 0.0).then_inc(ident_made, 1)
                pool.wait_ge(ident_made, 1)
                pool.affine_select(out=ident[:], in_=ident[:], compare_op=ALU.not_equal, fill=1.0, base=0,
                                   pattern=[[-1, P]], channel_multiplier=1).then_inc(ident_made, 1)

            @block.vector
            def _(dve):
                dve.wait_ge(ident_made, 2)
                dve.tensor_copy(ident_r[:], ident[:]).then_inc(ident_made, 1)

        shared = {"sem": sem, "soft_sems": soft_sems, "x": x, "ident": ident, "ident_r": ident_r, "gates": gates,
                  "ctx": arg["ctx_512"], "g_xattn": arg["g_xattn"], "g_ffn": arg["g_ffn"],
                  "out": out.rearrange("b s d -> (b s) d")}
        w_sh_gu, w_gu = arg["L0_ffn_w_sh_gate_up"], arg["L0_ffn_w_gate_up"]
        layer0 = dict(shared, E=8, F=256, FS=1024, K=2, w_router=arg["L0_ffn_w_gate"],
                      w_sh_gate=w_sh_gu[:, 0:1024], w_sh_up=w_sh_gu[:, 1024:2048], w_sh_down=arg["L0_ffn_w_sh_down"],
                      wg=lambda e: w_gu[bass.ds(e, 1), :, 0:256],
                      wu=lambda e: w_gu[bass.ds(e, 1), :, 256:512],
                      wd=lambda e: arg["L0_ffn_w_down"][bass.ds(e, 1), :, :])
        layer1 = dict(shared, E=32, F=192, FS=384, K=6, w_router=arg["L1_ffn_gate_w"],
                      w_sh_gate=arg["L1_ffn_sg"], w_sh_up=arg["L1_ffn_su"], w_sh_down=arg["L1_ffn_sd"],
                      wg=lambda e: arg["L1_ffn_wg"][bass.ds(e, 1), :, :],
                      wu=lambda e: arg["L1_ffn_wu"][bass.ds(e, 1), :, :],
                      wd=lambda e: arg["L1_ffn_wd"][bass.ds(e, 1), :, :])
        layer0["x_rows"] = arg["x"].rearrange("b s d -> (b s) d")
        make_attention(nc, 0, layer0)
        layer1["x_rows"] = make_ffn(nc, 0, layer0)
        numbers = [handle.num for handle in sems.values()]
        nc.all_engine_barrier(sems_to_clear=range(min(numbers), max(numbers) + 1))
        make_attention(nc, 1, layer1)
        make_ffn(nc, 1, layer1)


def kernel(**inputs):
    import numpy as np
    import concourse.bacc as bacc
    from concourse.bass_utils import run_bass_kernel_spmd

    nc = bacc.Bacc("TRN2", target_bir_lowering=False, num_devices=1)
    arrays, arg = {}, {}
    for name in INPUTS:
        a = np.ascontiguousarray(inputs[name])
        arrays[f"in_{name}"] = a
        arg[name] = nc.dram_tensor(f"in_{name}", a.shape, mybir.dt.from_np(a.dtype), kind="ExternalInput").ap()
    out = nc.dram_tensor("out_x", (B, S, H), F32, kind="ExternalOutput").ap()
    build_program(nc, arg, out)
    result = run_bass_kernel_spmd(nc, [arrays], core_ids=[0])
    return result.results[0]["out_x"]
```

```python
from contextlib import ExitStack

import concourse.bass as bass
from concourse import mybir

ALU = mybir.AluOpType
ACT = mybir.ActivationFunctionType
AX = mybir.AxisListType
F32 = mybir.dt.float32
F32R = mybir.dt.float32r
I32 = mybir.dt.int32

P = 128
B, S, H = 4, 512, 512
TOK = B * S
TT = TOK // P
TPB = S // P
QH, KVH = 32, 8
D = H // QH
G = QH // KVH
KVD = KVH * D
EPS = 1e-5
UNITS = B * KVH
RING = 4
LAG_MAX, LAG_NEG, LAG_EXP, LAG_OUT = 1, 2, 3, 4


TURN_NEG_AT, TURN_OUT_AT, TURN_AT, PV_AT = 1, 3, (6, 7, 10, 12), 2
COPY_OUT_AT, COPY_NEG_AT, COPY_TURN_AT, SCALE_AT = 1, 2, (4, 5, 6, 7), 4


def make_attention(nc, layer, t):
    x = t["x"]
    with ExitStack() as ctx:
        def sb(name, shape, dt=F32):
            return ctx.enter_context(nc.sbuf_tensor(f"{name}_{layer}", shape, dt))

        def sem(name):
            return t["sem"]("attn_" + name)

        score_ps = ctx.enter_context(nc.psum_tensor(f"score_ps_{layer}", [P, 2, 2, S], F32))
        max_ps = ctx.enter_context(nc.psum_tensor(f"max_ps_{layer}", [P, 2, S], F32))
        out_ps = ctx.enter_context(nc.psum_tensor(f"out_ps_{layer}", [P, S], F32))
        turn_ps = ctx.enter_context(nc.psum_tensor(f"turn_ps_{layer}", [P, S], F32))

        xh = sb("xh", [P, UNITS + 1, TPB * G, D])
        ctx_tok = sb("ctx_tok", [P, TT, KVD])
        ctx_unit = sb("ctx_unit", [P, UNITS + 1, TPB, D])
        stats, mean_var, rstd, minus_half = t["stats"], t["mean_var"], t["rstd"], t["minus_half"]
        gate_raw = sb("gate_raw", [P, 2])
        gate = t["gates"]
        q_stack = sb("q_stack", [P, 2, TPB * G, 4, D], F32R)
        k_stack = sb("k_stack", [P, 2, TPB, 12, D], F32R)
        q_turned = sb("q_turned", [P, RING, 2, S], F32R)
        k_turned = sb("k_turned", [P, RING, 2, S], F32R)
        v_ones = sb("v_ones", [P, RING, TPB, 32])
        maxima = sb("maxima", [P, 2, TPB, G])
        neg_max = sb("neg_max", [P, 2, TPB, 2 * G], F32R)
        neg_rows = sb("neg_rows", [2 * G, 2, S], F32R)
        probs = sb("probs", [P, 2, 2, 2, S])
        out_rows = sb("out_rows", [P, S])
        recip = sb("recip", [P, TPB * G])
        scaled = sb("scaled", [P, TPB * G, D])

        ctx_loaded, gate_loaded = sem("ctx_loaded"), sem("gate_loaded")
        x_loaded = [sem(f"x_loaded_{b}") for b in range(B)]
        ln_stats, ln_var, ln_rstd, ln_done = sem("ln_stats"), sem("ln_var"), sem("ln_rstd"), sem("ln_done")
        gate_ready, ctx_sorted, pool_set, filled = sem("gate_ready"), sem("ctx_sorted"), sem("pool_set"), sem("filled")
        q_hi, k_hi, stacked = sem("q_hi"), sem("k_hi"), sem("stacked")
        turned, turn_copied = sem("turned"), sem("turn_copied")
        max_scored, max_taken = sem("max_scored"), sem("max_taken")
        neg_hi, neg_split, neg_turned, neg_copied = sem("neg_hi"), sem("neg_split"), sem("neg_turned"), sem("neg_copied")
        neg_placed = [sem("neg_placed_even"), sem("neg_placed_odd")]
        scored, exped, v_ready, pv_done = sem("scored"), sem("exped"), sem("v_ready"), sem("pv_done")
        out_copied, out_turned = sem("out_copied"), sem("out_turned")
        recip_raw, recip_ready, out_read, x_added = sem("recip_raw"), sem("recip_ready"), sem("out_read"), sem("x_added")

        def steps(eng, step):
            for k in range(RING):
                step(0, k)
            with eng.Fori(1, UNITS // RING) as turn:
                for k in range(RING):
                    step(turn * RING, k)
            for k in range(RING):
                step(UNITS, k)

        def stage(it, k, lag):
            if isinstance(it, int) and not 0 <= it + k - lag < UNITS:
                return None
            return it + (k - lag)

        block = ctx.enter_context(nc.Block())

        @block.sync
        def _(sp):
            def load_x(b):
                sp.dma_start(x[:, b * TPB:(b + 1) * TPB, :],
                             t["x_rows"][b * S:(b + 1) * S, :].rearrange("(n p) d -> p n d", p=P)).then_inc(x_loaded[b], 16)

            load_x(0)
            sp.dma_start(ctx_tok[:], t["ctx"].rearrange("b (n p) d -> p (b n) d", p=P)).then_inc(ctx_loaded, 16)
            for i, g in enumerate((t["g_xattn"], t["g_ffn"])):
                sp.dma_start(gate_raw[:, i:i + 1], g[layer:layer + 1].rearrange("(a n) -> a n", a=1).to_broadcast([P, 1])
                             ).then_inc(gate_loaded, 16)
            for b in range(1, B):
                load_x(b)

            def step(it, k):
                u = stage(it, k, LAG_NEG)
                if u is None:
                    return
                par, slot = (k - LAG_NEG) % 2, (k - LAG_NEG) % RING
                sp.wait_ge(neg_copied, u + 1)
                for part in range(2):
                    for a in range(2):
                        row, dst = part * G + 2 * a, 64 * a + 48 + part
                        sp.dma_start(q_turned[dst:dst + 1, slot, :, :].bitcast(F32),
                                     neg_rows[row:row + 2, par, :].bitcast(F32)).then_inc(neg_placed[par], 16)

            steps(sp, step)

        @block.gpsimd
        def _(pool):
            pool.memset(minus_half[:], -0.5).then_inc(pool_set, 1)
            pool.memset(v_ones[:], 0.0).then_inc(pool_set, 1)
            pool.wait_ge(pool_set, 2)
            pool.memset(v_ones[:, :, :, D:D + 1], 1.0).then_inc(pool_set, 1)
            pool.wait_ge(pool_set, 3)

            def root(b, n=0):
                tiles = slice(b * TPB, (b + 1) * TPB)
                pool.wait_ge(ln_var, n + b + 1)
                pool.tensor_tensor(out=rstd[:, tiles], in0=mean_var[:, tiles, 1], in1=minus_half[:, tiles], op=ALU.pow
                                   ).then_inc(ln_rstd, 1)


            def stack(it, k):
                if isinstance(it, int) and it + k >= UNITS:
                    return
                u, par = it + k, k % 2
                q, kk = q_stack[:, par, :, :, :], k_stack[:, par, :, :, :]
                qx = xh[:, bass.ds(u, 1), :, :].rearrange("p a h d -> p (a h) d")
                kx = ctx_unit[:, bass.ds(u, 1), :, :].rearrange("p a c d -> p (a c) d")
                if not isinstance(it, int) or it + k >= 2:
                    pool.wait_ge(turned, 4 * it + 4 * (k - 1))
                    pool.nop(nofuse=True)
                pool.tensor_copy(q[:, :, 0:3:2, :], qx[:, :, None, :].to_broadcast([P, TPB * G, 2, D])).then_inc(q_hi, 1)
                pool.tensor_copy(kk[:, :, 4:6, :], kx[:, :, None, :].to_broadcast([P, TPB, 2, D])).then_inc(k_hi, 1)
                pool.wait_ge(q_hi, it + k + 1)
                pool.nop(nofuse=True)
                pool.tensor_tensor(out=q[:, :, 1, :], in0=qx, in1=q[:, :, 0, :].bitcast(F32), op=ALU.subtract)
                pool.wait_ge(k_hi, it + k + 1)
                pool.nop(nofuse=True)
                pool.tensor_tensor(out=kk[:, :, 6, :], in0=kx, in1=kk[:, :, 4, :].bitcast(F32), op=ALU.subtract).then_inc(stacked, 1)

            def add_x(it, k):
                if (u := stage(it, k, LAG_OUT)) is None:
                    return
                b, g = u // KVH, u % KVH
                xu = x[:, bass.ds(b * TPB, TPB), bass.ds(g * (G * D), G * D)]
                pool.wait_ge(out_read, u + 1)
                pool.nop(nofuse=True)
                pool.tensor_tensor(out=xu, in0=xu, in1=scaled[:].rearrange("p (c h) d -> p c (h d)", c=TPB), op=ALU.add
                                   ).then_inc(x_added, 1)

            def put_v(it, k):
                u = stage(it, k, 0)
                if u is None:
                    return
                if not isinstance(it, int) or it + k >= RING:
                    pool.wait_ge(pv_done, 4 * it + 4 * (k - RING + 1))
                    pool.nop(nofuse=True)
                pool.tensor_copy(v_ones[:, k, :, 0:D],
                                 ctx_unit[:, bass.ds(u, 1), :, :].rearrange("p a c d -> p (a c) d")
                                 ).then_inc(v_ready, 1)

            root(0)
            pool.wait_ge(ln_done, TPB)
            pool.wait_ge(ctx_sorted, 1)
            pool.wait_ge(filled, 5)
            stack(0, 0)

            def step(it, k):
                if isinstance(it, int) and it == 0 and k < B - 1:
                    root(k + 1)
                elif isinstance(it, int) and it == 0:
                    pool.wait_ge(ln_done, TT)
                put_v(it, k)
                stack(it, k + 1)
                add_x(it, k)
                if isinstance(it, int) and it == UNITS and k >= 1:
                    root(k - 1, B)

            steps(pool, step)

        @block.tensor
        def _(pe):
            ident, ident_r = t["ident"], t["ident_r"]

            def turn_q_or_k(it, k, n):
                if stage(it, k, 0) is None:
                    return
                if n == 0:
                    pe.wait_ge(stacked, it + k + 1)
                if n == 0:
                    if stage(it, k, 1) is not None:
                        pe.wait_ge(turn_copied, 4 * it + 4 * k)
                    if stage(it, k, LAG_NEG) is not None:
                        pe.wait_ge(neg_copied, it + (k - LAG_NEG + 1))
                    if stage(it, k, LAG_OUT) is not None:
                        pe.wait_ge(out_read, it + (k - LAG_OUT + 1))
                else:
                    pe.wait_ge(turn_copied, 4 * it + 4 * k + n)
                for c in range(TPB):
                    if n < 2:
                        src = q_stack[:, k % 2, G * c + 2 * n:G * c + 2 * n + 2, :, :].rearrange("p h s d -> p (h s d)")
                    else:
                        src = k_stack[:, k % 2, c, 4 * (3 - n):4 * (3 - n) + 8, :].rearrange("p s d -> p (s d)")
                    mm = pe.transpose(turn_ps[:, c * P:(c + 1) * P].bitcast(F32R), src, ident_r[:])
                mm.then_inc(turned, 1)

            def turn_neg(it, k):
                if (u := stage(it, k, LAG_NEG)) is None:
                    return
                pe.wait_ge(neg_split, u + 1)
                if stage(it, k, 1) is not None:
                    pe.wait_ge(turn_copied, 4 * it + 4 * k)
                elif (out := stage(it, k, LAG_OUT)) is not None:
                    pe.wait_ge(out_read, out)
                for c in range(TPB):
                    mm = pe.transpose(turn_ps[0:2 * G, c * P:(c + 1) * P].bitcast(F32R),
                                      neg_max[:, (k - LAG_NEG) % 2, c, :], ident_r[:])
                mm.then_inc(neg_turned, 1)

            def turn_out(it, k):
                if (u := stage(it, k, LAG_OUT)) is None:
                    return
                pe.wait_ge(out_copied, u + 1)
                if stage(it, k, LAG_NEG) is not None:
                    pe.wait_ge(neg_copied, it + (k - LAG_NEG + 1))
                elif u > 0:
                    pe.wait_ge(out_read, u)
                for c in range(TPB):
                    mm = pe.transpose(turn_ps[:, c * P:(c + 1) * P], out_rows[:, c * P:(c + 1) * P], ident[:])
                mm.then_inc(out_turned, 1)

            def score_for_max(it, k, c, h):
                if (u := stage(it, k, LAG_MAX)) is None:
                    return
                slot = (k - LAG_MAX) % RING
                n = c * G + h
                if n == 0:
                    pe.wait_ge(turn_copied, 4 * u + 4)
                first = isinstance(it, int) and it + k - LAG_MAX == 0
                if not (first and n < 2):
                    pe.wait_ge(max_taken, TPB * G * u + (n - 1))
                pe.matmul(max_ps[:, n % 2, :], q_turned[:, slot, h // 2, c * P:(c + 1) * P],
                          k_turned[:, slot, h % 2, :], start=True, stop=True).then_inc(max_scored, 1)

            def score_for_exp(it, k, c, pair):
                lag, c = (LAG_EXP, c) if c < TPB else (LAG_EXP - 1, 0)
                if (u := stage(it, k, lag)) is None:
                    return
                slot = (k - lag) % RING
                if c == 0 and pair == 0:
                    pe.wait_ge(neg_placed[(k - lag) % 2], 32 * u + (64 if (k - lag) % 2 == 0 else 32))
                first = isinstance(it, int) and it + k - lag == 0
                n = 2 * c + pair
                if not (first and n < 2):
                    pe.wait_ge(exped, 2 * TPB * u + (n - 1))
                for a in range(2):
                    mm = pe.matmul(score_ps[:, pair, a, :], k_turned[:, slot, a, c * P:(c + 1) * P],
                                   q_turned[:, slot, pair, :], start=True, stop=True)
                mm.then_inc(scored, 1)

            def probs_times_v(it, k, c):
                if (u := stage(it, k, LAG_EXP)) is None:
                    return
                slot = (k - LAG_EXP) % RING
                first = isinstance(it, int) and it + k - LAG_EXP == 0
                if c == 0:
                    pe.wait_ge(v_ready, u + 1)
                    if not first:
                        pe.wait_ge(out_copied, u + 0)
                pe.wait_ge(exped, 2 * TPB * u + 2 * c + 2)
                for h in range(G):
                    mm = pe.matmul(out_ps[32 * h:32 * h + 32, :], v_ones[:, slot, c, :],
                                   probs[:, c % 2, h // 2, h % 2, :], start=(c == 0), stop=(c == TPB - 1))
                mm.then_inc(pv_done, 1)

            def step(it, k):
                for slot in range(TPB * G):
                    c, h = slot // G, slot % G
                    if h == PV_AT:
                        probs_times_v(it, k, c)
                    score_for_max(it, k, c, h)
                    if slot == TURN_NEG_AT:
                        turn_neg(it, k)
                    if slot == TURN_OUT_AT:
                        turn_out(it, k)
                    for n in range(4):
                        if slot == TURN_AT[n]:
                            turn_q_or_k(it, k, n)
                    if h % 2 == 0:
                        score_for_exp(it, k, c + 1, h // 2)

            steps(pe, step)

        @block.scalar
        def _(act):
            act.wait_ge(gate_loaded, 32)
            act.activation(gate[:], gate_raw[:], ACT.Tanh).then_inc(gate_ready, 1)
            act.wait_ge(ctx_loaded, 16)
            for b in range(B):
                ins = act.activation(ctx_unit[:, b * KVH:(b + 1) * KVH, :, :].rearrange("p g c d -> p c g d"),
                                     ctx_tok[:, b * TPB:(b + 1) * TPB, :].rearrange("p c (g d) -> p c g d", g=KVH),
                                     ACT.Copy)
            ins.then_inc(ctx_sorted, 1)

            def copy_neg(it, k):
                if (u := stage(it, k, LAG_NEG)) is None:
                    return
                act.wait_ge(neg_turned, u + 1)
                if not isinstance(it, int) or it + k - LAG_NEG >= 2:
                    par = (k - LAG_NEG) % 2
                    act.wait_ge(neg_placed[par], 32 * u + (0 if par == 0 else -32))
                act.activation(neg_rows[:, (k - LAG_NEG) % 2, :], turn_ps[0:2 * G, :], ACT.Copy).then_inc(neg_copied, 1)

            def copy_turned(it, k, n):
                if stage(it, k, 0) is None:
                    return
                act.wait_ge(turned, 4 * it + 4 * k + n + 1)
                if n == 0 and (not isinstance(it, int) or it + k >= RING):
                    act.wait_ge(pv_done, 4 * it + 4 * (k - RING + 1))
                dst = (q_turned if n < 2 else k_turned)[:, k, n % 2, :]
                act.activation(dst, turn_ps[:], ACT.Copy).then_inc(turn_copied, 1)

            def exp(it, k, c, pair):
                if (u := stage(it, k, LAG_EXP)) is None:
                    return
                first = isinstance(it, int) and it + k - LAG_EXP == 0
                act.wait_ge(scored, 2 * TPB * u + 2 * c + pair + 1)
                if not (first and c < 2):
                    act.wait_ge(pv_done, TPB * u + (c - 1))
                act.activation(probs[:, c % 2, pair, :, :], score_ps[:, pair, :, :], ACT.Exp,
                               scale=float(D) ** -0.5).then_inc(exped, 1)

            def copy_out(it, k):
                if (u := stage(it, k, LAG_OUT)) is None:
                    return
                act.wait_ge(pv_done, TPB * u + TPB)
                if not (isinstance(it, int) and it + k - LAG_OUT == 0):
                    act.wait_ge(out_turned, u + 0)
                act.activation(out_rows[:], out_ps[:], ACT.Copy).then_inc(out_copied, 1)

            def step(it, k):
                for n in range(2 * TPB):
                    exp(it, k, n // 2, n % 2)
                    if n == COPY_OUT_AT:
                        copy_out(it, k)
                    if n == COPY_NEG_AT:
                        copy_neg(it, k)
                    for turn in range(4):
                        if n == COPY_TURN_AT[turn]:
                            copy_turned(it, k, turn)

            steps(act, step)

        @block.vector
        def _(dve):
            dve.memset(q_stack[:].bitcast(F32), 0.0).then_inc(filled, 1)
            dve.memset(k_stack[:].bitcast(F32), 0.0).then_inc(filled, 1)
            dve.memset(xh[:, UNITS, :, :], 0.0).then_inc(filled, 1)
            dve.memset(ctx_unit[:, UNITS, :, :], 0.0).then_inc(filled, 1)
            dve.wait_ge(filled, 4)
            dve.memset(k_stack[:, :, :, 7, 0:2].bitcast(F32), 1.0).then_inc(filled, 1)

            def moments(b, n=0):
                tiles = range(b * TPB, (b + 1) * TPB)
                for i in tiles:
                    dve.bn_stats(stats[:, i, :], x[:, i, :]).then_inc(ln_stats, 1)
                dve.wait_ge(ln_stats, 2 * TPB * (n + b) + TPB)
                for i in tiles:
                    dve.bn_aggr(mean_var[:, i, :], stats[:, i, :]).then_inc(ln_stats, 1)
                dve.wait_ge(ln_stats, 2 * TPB * (n + b) + 2 * TPB)
                var = mean_var[:, b * TPB:(b + 1) * TPB, 1]
                dve.tensor_scalar(var, var, EPS, None, ALU.add).then_inc(ln_var, 1)

            def layernorm(b):
                dve.wait_ge(x_loaded[b], 16)
                moments(b)
                dve.wait_ge(ln_rstd, b + 1)
                for c in range(TPB):
                    i = b * TPB + c
                    dve.tensor_scalar(xh[:, b * KVH:(b + 1) * KVH, c * G:(c + 1) * G, :].rearrange("p g h d -> p g (h d)"),
                                      x[:, i, :].rearrange("p (g e) -> p g e", g=KVH),
                                      mean_var[:, i, 0:1], rstd[:, i:i + 1], ALU.subtract, ALU.mult).then_inc(ln_done, 1)

            layernorm(0)
            dve.wait_ge(gate_ready, 1)

            def take_max(it, k, c, heads):
                if (u := stage(it, k, LAG_MAX)) is None:
                    return
                for h in heads:
                    n = c * G + h
                    dve.wait_ge(max_scored, TPB * G * u + n + 1)
                    col = 2 * (h % 2) + h // 2
                    dve.tensor_reduce(maxima[:, (k - LAG_MAX) % 2, c, col:col + 1], max_ps[:, n % 2, :],
                                      AX.X, ALU.max).then_inc(max_taken, 1)

            def split_neg(it, k):
                if (u := stage(it, k, LAG_MAX)) is None:
                    return
                par = (k - LAG_MAX) % 2
                dve.wait_ge(max_taken, TPB * G * u + TPB * G)
                if not isinstance(it, int) or it + k - LAG_MAX >= 2:
                    dve.wait_ge(neg_turned, u + (-1))
                dve.tensor_scalar(neg_max[:, par, :, 0:G], maxima[:, par, :, :], -1.0, None, ALU.mult).then_inc(neg_hi, 1)
                dve.wait_ge(neg_hi, u + 1)
                dve.scalar_tensor_tensor(neg_max[:, par, :, G:2 * G], maxima[:, par, :, :], -1.0,
                                         neg_max[:, par, :, 0:G].bitcast(F32), ALU.mult, ALU.subtract
                                         ).then_inc(neg_split, 1)

            def scale_out(it, k):
                if (u := stage(it, k, LAG_OUT)) is None:
                    return
                turned_out = turn_ps[:].rearrange("p (c h e) -> p (c h) e", c=TPB, h=G)
                dve.wait_ge(out_turned, u + 1)
                if not (isinstance(it, int) and it + k - LAG_OUT == 0):
                    dve.wait_ge(out_read, u + 0)
                dve.reciprocal(recip[:], turned_out[:, :, D]).then_inc(recip_raw, 1)
                dve.wait_ge(recip_raw, u + 1)
                dve.tensor_scalar(recip[:], recip[:], gate[:, 0:1], None, ALU.mult).then_inc(recip_ready, 1)
                dve.wait_ge(recip_ready, u + 1)
                if not (isinstance(it, int) and it + k - LAG_OUT == 0):
                    dve.wait_ge(x_added, u + 0)
                dve.tensor_tensor(scaled[:], turned_out[:, :, 0:D],
                                  recip[:, :, None].to_broadcast([P, TPB * G, D]), ALU.mult).then_inc(out_read, 1)

            def step(it, k):
                if isinstance(it, int) and it == 0 and k < B - 1:
                    layernorm(k + 1)
                if isinstance(it, int) and it == UNITS and k >= 1:
                    dve.wait_ge(x_added, KVH * k)
                    moments(k - 1, B)
                for n in range(TPB * G):
                    take_max(it, k, n // G, (n % G,))
                    if n == SCALE_AT:
                        scale_out(it, k)
                split_neg(it, k)

            steps(dve, step)
            dve.wait_ge(x_added, UNITS)


CAP = TOK
CAPT = CAP // P
SCHED = P + 8
PRODUCTS = ((0, 0), (0, 1), (1, 0))
SOFT_SEMS = ("scattered_a", "scattered_b", "gathered_a", "gathered_b", "accumulated", "table_in")


def make_ffn(nc, layer, t):
    x, gate = t["x"], t["gates"][:, 1:2]
    E, F, FS, K = t["E"], t["F"], t["FS"], t["K"]
    HC = H // P
    FC = FS // P
    FK = 2
    FW = F // FK
    NBK = 2 if FC % 2 == 0 else FC
    ROWS = TOK + P
    DUMMY = E * CAPT
    with ExitStack() as ctx:
        def sb(name, shape, dt=F32):
            return ctx.enter_context(nc.sbuf_tensor(f"{name}_f{layer}", shape, dt))

        def sem(name):
            return t["sem"]("ffn_" + name)

        def soft_sem(name):
            return t["soft_sems"][layer][name]

        def dram(name, shape, dt=F32):
            return nc.dram_tensor(f"{name}_f{layer}", shape, dt, kind="Internal").ap()

        bank = ctx.enter_context(nc.psum_tensor(f"bank_f{layer}", [P, 8, 512], F32))
        xh_rows = dram("xh_rows", (ROWS, H))
        acc_rows = dram("acc_rows", (ROWS, H))
        table = dram("table", (E * CAP, 2))
        sched_dram = dram("sched_dram", (P, 3), I32)

        stats, mean_var, rstd, minus_half = t["stats"], t["mean_var"], t["rstd"], t["minus_half"]
        xh = sb("xh", [P, 2, TPB, H])
        w_router = sb("w_router", [P, HC, E])
        logits_T = sb("logits_T", [E, S])
        logits = sb("logits", [P, TT, E])
        w_gu = sb("w_gu", [P, 2, HC, 2 * F])
        w_dn = sb("w_dn", [FW, 2, FK, H])
        zero_tile = sb("zero_tile", [P, H])
        table_sb = sb("table_sb", [P, DUMMY + 1, 2])
        blank = sb("blank", [P, CAPT, 2])
        prob, above, tied, tmp, weight, mask, row1 = (sb(n, [P, TT, E]) for n in
            ("prob", "above", "tied", "tmp", "weight", "mask", "row1"))
        rank_i, rank_a = sb("rank_i", [P, TT, E], I32), sb("rank_a", [P, TT, E], I32)
        reset_e = sb("reset_e", [P, TT, E])
        reset_t, total_t, cum_t = sb("reset_t", [P, E, TT]), sb("total_t", [P, E, TT]), sb("cum_t", [P, E, TT])
        top, top_rows = sb("top", [P, TT, 8]), sb("top_rows", [P, TT, 8])
        stat1, stat2 = sb("stat1", [P, TT]), sb("stat2", [P, TT])
        expert_base = sb("expert_base", [P, E])
        expert_base_i, token_i, tile_i = sb("expert_base_i", [P, E], I32), sb("token_i", [P, TT], I32), sb("tile_i", [P, 1], I32)
        token_f, tile_f, spare_f = sb("token_f", [P, TT]), sb("tile_f", [P, 1]), sb("spare_f", [P, 1])
        slot_idx = sb("slot_idx", [P, TT, 8], I32)
        entry = sb("entry", [P, TT, K, 2])
        tri, ones_m = sb("tri", [P, P]), sb("ones_m", [P, P])
        cnt_i, tiles_f, ends_f, ends_i = sb("cnt_i", [P, E], I32), sb("tiles_f", [P, E]), sb("ends_f", [P, E]), sb("ends_i", [P, E], I32)
        ones_e, before, before_n = sb("ones_e", [P, E]), sb("before", [P, E]), sb("before_n", [P, E])
        ncol, next_e, has_next = sb("ncol", [P, 2]), sb("next_e", [P, 1]), sb("has_next", [P, 1])
        sched_f, sched_i, turns_i = sb("sched_f", [P, 3]), sb("sched_i", [P, 3], I32), sb("turns_i", [P, 3], I32)
        sched = sb("sched", [1, SCHED, 3], I32)
        idx_in, idx_out = sb("idx_in", [P, 2], I32), sb("idx_out", [P, 2], I32)
        w_out = sb("w_out", [P, 2])
        xg, y_tok = sb("xg", [P, 2, H]), sb("y_tok", [P, 2, H])
        with ExitStack() as first_use:
            def sb_first(name, shape):
                return first_use.enter_context(nc.sbuf_tensor(f"{name}_f{layer}", shape, F32))

            w_sh_gate, w_sh_up = sb_first("w_sh_gate", [P, HC, FS]), sb_first("w_sh_up", [P, HC, FS])
            w_sh_down = sb_first("w_sh_down", [P, FC, H])
            xT = sb_first("xT", [P, HC, TOK])
            silu_T, h_T = sb_first("silu_T", [P, NBK, S]), sb_first("h_T", [P, FC, S])
        w_gu_parts = sb("w_gu_parts", [P, 2, 2, HC, 2 * F], F32R)
        w_dn_parts = sb("w_dn_parts", [FW, 2, 2, FK, H], F32R)
        xg_T = sb("xg_T", [P, 2, 2, HC, P], F32R)
        silu_g, h_tok, hg_T = sb("silu_g", [P, 2, F]), sb("h_tok", [P, 2, F]), sb("hg_T", [FW, 2, 2, FK, P], F32R)

        ln_stats, ln_var, ln_rstd, ln_done = sem("ln_stats"), sem("ln_var"), sem("ln_rstd"), sem("ln_done")
        weights_in, spare_stored, const_set, blank_set, table_blank = (sem(n) for n in
            ("weights_in", "spare_stored", "const_set", "blank_set", "table_blank"))
        router_in = sem("router_in")
        xh_stored = [sem("xh_stored_even"), sem("xh_stored_odd")]
        xt_turned, xt_copied, lT_done, lT_copied, l_turned, logits_in = (sem(n) for n in
            ("xt_turned", "xt_copied", "lT_done", "lT_copied", "l_turned", "logits_in"))
        shifted, activated, chain = sem("shifted"), sem("activated"), sem("chain")
        mask_ready, ranked, ranks_read, y0_added = sem("mask_ready"), sem("ranked"), sem("ranks_read"), sem("y0_added")
        entries_ready, sched_ready = sem("entries_ready"), sem("sched_ready")
        scattered = [soft_sem("scattered_a"), soft_sem("scattered_b")]
        sched_out, sched_in, table_in = sem("sched_out"), sem("sched_in"), soft_sem("table_in")
        gu_done, silu_done, h_done, y_done, y_read = (sem(n) for n in ("gu_done", "silu_done", "h_done", "y_done", "y_read"))
        acc_set, expert_w = sem("acc_set"), sem("expert_w")
        in_cols, gathered, xg_turned, xg_copied = sem("in_cols"), [soft_sem("gathered_a"), soft_sem("gathered_b")], sem("xg_turned"), sem("xg_copied")
        egu_done, esilu_done, eh_done, eh_turned, eh_copied, ey_done, ey_copied = (sem(n) for n in
            ("egu_done", "esilu_done", "eh_done", "eh_turned", "eh_copied", "ey_done", "ey_copied"))
        gu_hi_done, gu_split, dn_hi_done, dn_split, xg_hi, eh_hi = (sem(n) for n in
            ("gu_hi_done", "gu_split", "dn_hi_done", "dn_split", "xg_hi", "eh_hi"))
        out_cols, accumulated, result_out = sem("out_cols"), soft_sem("accumulated"), sem("result_out")

        def y0(c):
            return (y_tok if c < 2 else xg)[:, c % 2, :]

        block = ctx.enter_context(nc.Block())

        @block.sync
        def _(sp):
            sp.dma_start(w_router[:], t["w_router"].rearrange("(c p) e -> p c e", p=P)).then_inc(router_in, 16)
            sp.wait_ge(blank_set, 1)
            sp.dma_start(xh_rows[TOK:ROWS, :], zero_tile[:]).then_inc(spare_stored, 16)
            sp.dma_start(acc_rows[TOK:ROWS, :], zero_tile[:]).then_inc(acc_set, 16)
            sp.dma_start(table.rearrange("(e p j) c -> p e (j c)", e=E, p=P),
                         blank[:].rearrange("p j c -> p (j c)")[:, None, :].to_broadcast([P, E, CAPT * 2])
                         ).then_inc(table_blank, 16)
            for b in range(B):
                sp.wait_ge(ln_done, TPB * b + TPB)
                sp.dma_start(xh_rows[b * S:(b + 1) * S, :].rearrange("(n p) d -> p n d", p=P), xh[:, b % 2, :, :]
                             ).then_inc(xh_stored[b % 2], 16)
                if b == 1:
                    sp.dma_start(w_sh_gate[:], t["w_sh_gate"].rearrange("(c p) f -> p c f", p=P)).then_inc(weights_in, 16)
                    sp.dma_start(w_sh_up[:], t["w_sh_up"].rearrange("(c p) f -> p c f", p=P)).then_inc(weights_in, 16)
                    sp.dma_start(w_sh_down[:], t["w_sh_down"].rearrange("(c p) h -> p c h", p=P)).then_inc(weights_in, 16)

            def load_expert(e, half):
                sp.dma_start(w_gu[:, half, :, 0:F], t["wg"](e).rearrange("a (c p) f -> p (a c) f", p=P)).then_inc(expert_w, 16)
                sp.dma_start(w_gu[:, half, :, F:2 * F], t["wu"](e).rearrange("a (c p) f -> p (a c) f", p=P)).then_inc(expert_w, 16)
                sp.dma_start(w_dn[:, half, :, :], t["wd"](e).rearrange("a (c p) h -> p (a c) h", p=FW)).then_inc(expert_w, 16)

            load_expert(0, 0)
            sp.wait_ge(expert_w, 48)
            load_expert(1, 1)
            sp.wait_ge(sched_ready, 1)
            sp.dma_start(sched_dram, sched_i[:]).then_inc(sched_out, 16)
            sp.wait_ge(sched_out, 16)
            sp.dma_start(sched[0:1, 0:P, :].rearrange("a i c -> a (i c)"),
                         sched_dram.rearrange("(a i) c -> a (i c)", a=1)).then_inc(sched_in, 16)
            with sp.Fori(1, B) as b:
                sp.wait_ge(y_read, TPB * b + TPB)
                sp.dma_start(acc_rows[bass.ds(b * S, S), :].rearrange("(n p) d -> p n d", p=P),
                             x[:, bass.ds(b * TPB, TPB), :]).then_inc(acc_set, 16)
            sp.wait_ge(y0_added, TPB)
            sp.dma_start(acc_rows[0:S, :].rearrange("(n p) d -> p n d", p=P), x[:, 0:TPB, :]).then_inc(acc_set, 16)
            with sp.Fori(1, E // 2) as pair:
                for half in range(2):
                    e = pair * 2 + half
                    sp.wait_ge(expert_w, 48 * e)
                    sp.nop(nofuse=True)
                    sp.wait_ge(gu_split, 2 * e - 2)
                    sp.nop(nofuse=True)
                    sp.wait_ge(dn_split, e - 1)
                    sp.nop(nofuse=True)
                    load_expert(e, half)
            turns = sp.value_load(turns_i[0:1, 0:1], min_val=4, max_val=64)
            sp.wait_ge(accumulated, turns * 32 + 16)
            sp.nop(nofuse=True)
            if layer == 1:
                sp.dma_start(t["out"], acc_rows[0:TOK, :]).then_inc(result_out, 16)
                sp.wait_ge(result_out, 16)

        @block.gpsimd
        def _(pool):
            pool.wait_ge(ln_var, 1)
            pool.tensor_tensor(out=rstd[:, TT - TPB:TT], in0=mean_var[:, TT - TPB:TT, 1], in1=minus_half[:, TT - TPB:TT],
                               op=ALU.pow).then_inc(ln_rstd, 1)
            pool.iota(tile_i[:], pattern=[[0, 1]], base=0, channel_multiplier=1).then_inc(const_set, 1)
            pool.iota(token_i[:], pattern=[[P, TT]], base=0, channel_multiplier=1).then_inc(const_set, 1)
            pool.iota(expert_base_i[:], pattern=[[CAP, E]], base=1, channel_multiplier=0).then_inc(const_set, 1)
            pool.memset(zero_tile[:], 0.0).then_inc(const_set, 1)
            pool.memset(blank[:], 0.0).then_inc(const_set, 1)
            pool.wait_ge(const_set, 5)
            pool.tensor_copy(tile_f[:], tile_i[:]).then_inc(const_set, 1)
            pool.wait_ge(const_set, 6)
            pool.tensor_scalar(blank[:, :, 0], zero_tile[:, 0:CAPT], tile_f[:, 0:1],
                               float(TOK), ALU.add, ALU.add).then_inc(blank_set, 1)
            pool.memset(tri[:], 1.0).then_inc(const_set, 1)
            pool.memset(ones_m[:], 1.0).then_inc(const_set, 1)
            pool.memset(ones_e[:], 1.0).then_inc(const_set, 1)
            pool.memset(reset_e[:], 1.0).then_inc(const_set, 1)
            pool.memset(reset_t[:], 1.0).then_inc(const_set, 1)
            pool.memset(table_sb[:, DUMMY, 1:2], 0.0).then_inc(const_set, 1)
            pool.tensor_copy(token_f[:], token_i[:]).then_inc(const_set, 1)
            pool.tensor_copy(expert_base[:], expert_base_i[:]).then_inc(const_set, 1)
            pool.memset(sched[0:1, P:SCHED, 0:1], DUMMY).then_inc(const_set, 1)
            pool.memset(sched[0:1, P:SCHED, 1:2], E - 1).then_inc(const_set, 1)
            pool.memset(sched[0:1, P:SCHED, 2:3], 0).then_inc(const_set, 1)
            pool.wait_ge(const_set, 17)
            pool.affine_select(out=tri[:], in_=tri[:], compare_op=ALU.is_gt, fill=0.0, base=0,
                               pattern=[[1, P]], channel_multiplier=-1).then_inc(const_set, 1)
            pool.memset(reset_e[:, :, 0:1], 0.0).then_inc(const_set, 1)
            pool.memset(reset_t[:, :, 0:1], 0.0).then_inc(const_set, 1)
            pool.wait_ge(blank_set, 1)
            pool.tensor_copy(table_sb[:, DUMMY, 0:1], blank[:, 0, 0:1]).then_inc(const_set, 1)
            pool.wait_ge(const_set, 21)

            for f in range(FC):
                pool.wait_ge(silu_done, f + 1)
                pool.tensor_tensor(out=h_T[:, f, :], in0=silu_T[:, f % NBK, :], in1=h_T[:, f, :], op=ALU.mult
                                   ).then_inc(h_done, 1)

            pool.wait_ge(table_blank, 16)
            for k in range(K):
                pool.wait_ge(entries_ready, k + 1)
                for i in range(TT):
                    pool.indirect_dma_start(table, bass.IndirectOffsetOnAxis(ap=slot_idx[:, i, k:k + 1], axis=0),
                                            entry[:, i, k, :], None).then_inc(scattered[i % 2], 16)
            for half in range(2):
                pool.wait_ge(scattered[half], 16 * (TT * K // 2))
            pool.dma_start(table_sb[:, 0:DUMMY, :].rearrange("p (e j) c -> p e (j c)", e=E),
                           table.rearrange("(e p j) c -> p e (j c)", e=E, p=P)).then_inc(table_in, 16)
            for c in range(TPB):
                pool.wait_ge(y_read, c + 1)
                pool.tensor_tensor(out=x[:, c, :], in0=x[:, c, :], in1=y0(c), op=ALU.add).then_inc(y0_added, 1)
            pool.wait_ge(table_in, 16)
            pool.wait_ge(spare_stored, 16)
            for half in range(2):
                pool.wait_ge(xh_stored[half], 16 * (B // 2))

            def gather(i, half):
                col = pool.value_load(sched[0:1, bass.ds(i, 1), 0:1].rearrange("a i c -> a (i c)"), min_val=0, max_val=DUMMY)
                pool.tensor_copy(idx_in[:, half:half + 1], table_sb[:, bass.ds(col, 1), 0:1].rearrange("p a c -> p (a c)")
                                 ).then_inc(in_cols, 1)
                pool.wait_ge(in_cols, i + 1)
                pool.nop(nofuse=True)
                pool.indirect_dma_start(xg[:, half, :], None, xh_rows,
                                        bass.IndirectOffsetOnAxis(ap=idx_in[:, half:half + 1], axis=0)
                                        ).then_inc(gathered[half], 16)

            def scatter(i, half, first=False):
                col = pool.value_load(sched[0:1, bass.ds(i, 1), 0:1].rearrange("a i c -> a (i c)"), min_val=0, max_val=DUMMY)
                pool.tensor_copy(w_out[:, half:half + 1], table_sb[:, bass.ds(col, 1), 1:2].rearrange("p a c -> p (a c)")
                                 ).then_inc(out_cols, 1)
                pool.tensor_copy(idx_out[:, half:half + 1], table_sb[:, bass.ds(col, 1), 0:1].rearrange("p a c -> p (a c)")
                                 ).then_inc(out_cols, 1)
                pool.wait_ge(out_cols, 2 * i + 2)
                pool.wait_ge(ey_copied, i + 1)
                if not first:
                    pool.wait_ge(accumulated, 16 * i)
                pool.nop(nofuse=True)
                pool.indirect_dma_start(acc_rows, bass.IndirectOffsetOnAxis(ap=idx_out[:, half:half + 1], axis=0),
                                        y_tok[:, half, :], None, compute_op=ALU.add).then_inc(accumulated, 16)

            def step(i, half):
                pool.wait_ge(xg_turned, i + 2)
                gather(i + 3, 1 - half)
                scatter(i - 2, half)

            pool.wait_ge(sched_in, 16)
            turns = pool.value_load(turns_i[0:1, 0:1], min_val=4, max_val=64)
            gather(0, 0)
            gather(1, 1)
            for i in (2, 3, 4, 5):
                pool.wait_ge(xg_turned, i - 1)
                gather(i, i % 2)
            pool.wait_ge(acc_set, 16 * (B + 1))
            scatter(0, 0, first=True)
            with pool.Fori(1, turns) as turn:
                step(turn * 2 + 1, 1)
                step(turn * 2 + 2, 0)
            scatter(pool.value_load(turns_i[0:1, 1:2], min_val=7, max_val=127), 1)
            scatter(turns * 2, 0)
            for half in range(2):
                pool.wait_ge(gathered[half], turns * 16 + 32)

        @block.tensor
        def _(pe):
            ident = t["ident"]

            def turn_batch(b):
                for c in range(TPB):
                    pe.wait_ge(ln_done, TPB * b + c + 1)
                    if not isinstance(b, int) or TPB * b + c >= 2:
                        pe.wait_ge(xt_copied, TPB * b + (c - 1))
                    for d in range(HC):
                        mm = pe.transpose(bank[:, c % 2, d * P:(d + 1) * P],
                                          xh[:, b % 2, c, d * P:(d + 1) * P], ident[:])
                    mm.then_inc(xt_turned, 1)

            def logits_batch(b):
                pe.wait_ge(router_in, 16)
                pe.wait_ge(xt_copied, TPB * b + TPB)
                if not isinstance(b, int) or b >= 1:
                    pe.wait_ge(lT_copied, b + 0)
                for d in range(HC):
                    mm = pe.matmul(bank[0:E, 2, :], w_router[:, d, :], xT[:, d, bass.ds(b * S, S)],
                                   start=(d == 0), stop=(d == HC - 1))
                mm.then_inc(lT_done, 1)

            def turn_logits(b):
                pe.wait_ge(lT_copied, b + 1)
                if not isinstance(b, int) or b >= 1:
                    pe.wait_ge(logits_in, b + 0)
                pe.nop(nofuse=True)
                for c in range(TPB):
                    mm = pe.transpose(bank[:, 3, c * E:(c + 1) * E], logits_T[:, c * P:(c + 1) * P], ident[0:E, 0:E])
                mm.then_inc(l_turned, 1)

            turn_batch(0)
            turn_batch(1)
            logits_batch(0)
            for b in range(2, B):
                turn_batch(b)
                turn_logits(b - 2)
                logits_batch(b - 1)
            turn_logits(B - 2)
            logits_batch(B - 1)
            turn_logits(B - 1)
            pe.wait_ge(logits_in, B)
            pe.wait_ge(weights_in, 48)

            def rank():
                pe.wait_ge(mask_ready, 1)
                pe.wait_ge(const_set, 21)
                for o, m in ((6, tri), (7, ones_m)):
                    mm = pe.matmul(bank[:, o, 0:TT * E], m[:], mask[:].rearrange("p t e -> p (t e)"), start=True, stop=True)
                mm.then_inc(ranked, 1)

            def shared_gu(g, f):
                n = g * FC + f
                if not isinstance(g, int) or g * FC + f >= NBK:
                    pe.wait_ge(h_done, n + (1 - NBK))
                for w, o in ((w_sh_gate, 0), (w_sh_up, 1)):
                    for d in range(HC):
                        mm = pe.matmul(bank[:, 2 * (f % NBK) + o, :], w[:, d, f * P:(f + 1) * P],
                                       xT[:, d, bass.ds(g * S, S)], start=(d == 0), stop=(d == HC - 1))
                mm.then_inc(gu_done, 1)

            def shared_group(g):
                for f in range(FC):
                    shared_gu(g, f)
                    if isinstance(g, int) and f == 0:
                        rank()
                pe.wait_ge(h_done, g * FC + FC)
                if isinstance(g, int):
                    pe.wait_ge(ranks_read, 2)
                for c in range(TPB):
                    if not isinstance(g, int) or c >= 2:
                        pe.wait_ge(y_read, TPB * g + (c - 1))
                    for f in range(FC):
                        mm = pe.matmul(bank[:, 6 + c % 2, :], h_T[:, f, c * P:(c + 1) * P], w_sh_down[:, f, :],
                                       start=(f == 0), stop=(f == FC - 1))
                    mm.then_inc(y_done, 1)

            shared_group(0)
            with pe.Fori(1, B) as g:
                shared_group(g)
            pe.wait_ge(y_read, TT)

            def turn_x(i, half):
                if isinstance(i, int):
                    pe.wait_ge(gathered[half], 16 * (i // 2 + 1))
                else:
                    pe.wait_ge(gathered[half], 8 * i + (16 if half == 0 else 8))
                if not isinstance(i, int) or i >= 1:
                    pe.wait_ge(xg_copied, i + 0)
                for d in range(HC):
                    mm = pe.transpose(bank[:, 6, d * P:(d + 1) * P], xg[:, half, d * P:(d + 1) * P], ident[:])
                mm.then_inc(xg_turned, 1)

            def gate_up(i, half, e):
                pe.wait_ge(gu_split, 2 * e + 2)
                pe.wait_ge(xg_copied, i + 1)
                if not isinstance(i, int) or i >= 2:
                    pe.wait_ge(eh_done, i + (-1))
                n, par = 0, pe.snap(e % 2)
                for d in range(HC):
                    for x_part, w_part in PRODUCTS:
                        mm = pe.matmul(bank[:, half, 0:2 * F], xg_T[:, half, x_part, d, :],
                                       w_gu_parts[:, bass.ds(par, 1), w_part, d, :].rearrange("p a f -> p (a f)"),
                                       start=(n == 0), stop=(n == 3 * HC - 1))
                        n += 1
                mm.then_inc(egu_done, 1)

            def turn_h(i, half):
                pe.wait_ge(eh_done, i + 1)
                if not isinstance(i, int) or i >= 1:
                    pe.wait_ge(eh_copied, i + 0)
                for f in range(FK):
                    mm = pe.transpose(bank[0:FW, 7, f * P:(f + 1) * P], h_tok[:, half, f * FW:(f + 1) * FW], ident[:])
                mm.then_inc(eh_turned, 1)

            def down(i, half, e, before=None):
                pe.wait_ge(eh_copied, i + 1)
                if before is not None:
                    pe.wait_ge(ey_copied, before)
                elif not isinstance(i, int) or i >= 2:
                    pe.wait_ge(ey_copied, i + (-1))
                pe.wait_ge(dn_split, e + 1)
                n, par = 0, pe.snap(e % 2)
                for f in range(FK):
                    for h_part, w_part in PRODUCTS:
                        mm = pe.matmul(bank[:, 2 + half, :], hg_T[:, half, h_part, f, :],
                                       w_dn_parts[:, bass.ds(par, 1), w_part, f, :].rearrange("p a f -> p (a f)"),
                                       start=(n == 0), stop=(n == 3 * FK - 1))
                        n += 1
                mm.then_inc(ey_done, 1)

            def expert_of(i):
                return pe.value_load(sched[0:1, bass.ds(i, 1), 1:2].rearrange("a i c -> a (i c)"), min_val=0, max_val=E - 1)

            def last_tiles(n):
                return pe.value_load(turns_i[0:1, n:n + 1], min_val=6, max_val=127)

            def step(i, half):
                e_down, e_next = expert_of(i - 2), expert_of(i + 1)
                turn_h(i - 1, 1 - half)
                turn_x(i + 2, half)
                down(i - 2, half, e_down)
                gate_up(i + 1, 1 - half, e_next)

            pe.wait_ge(sched_in, 16)
            turns = pe.value_load(turns_i[0:1, 0:1], min_val=4, max_val=64)
            turn_x(0, 0)
            turn_x(1, 1)
            gate_up(0, 0, expert_of(0))
            turn_x(2, 0)
            gate_up(1, 1, expert_of(1))
            turn_h(0, 0)
            turn_x(3, 1)
            gate_up(2, 0, expert_of(2))
            step(2, 0)
            with pe.Fori(1, turns) as turn:
                step(turn * 2 + 1, 1)
                step(turn * 2 + 2, 0)
            turn_h(turns * 2, 0)
            down(turns * 2 - 1, 1, expert_of(turns * 2 - 1), last_tiles(2))
            down(turns * 2, 0, expert_of(turns * 2), last_tiles(1))

        @block.scalar
        def _(act):
            def copy_batch(b):
                for c in range(TPB):
                    act.wait_ge(xt_turned, TPB * b + c + 1)
                    act.activation(xT[:, :, bass.ds(b * S + c * P, P)], bank[:, c % 2, :].rearrange("p (d m) -> p d m", d=HC),
                                   ACT.Copy).then_inc(xt_copied, 1)

            def copy_logits_T(b):
                act.wait_ge(lT_done, b + 1)
                if b >= 1:
                    act.wait_ge(l_turned, b)
                act.activation(logits_T[:], bank[0:E, 2, :], ACT.Copy).then_inc(lT_copied, 1)

            def copy_logits(b):
                act.wait_ge(l_turned, b + 1)
                act.activation(logits[:, b * TPB:(b + 1) * TPB, :].rearrange("p t e -> p (t e)"),
                               bank[:, 3, 0:TPB * E], ACT.Copy).then_inc(logits_in, 1)

            copy_batch(0)
            copy_batch(1)
            copy_logits_T(0)
            for b in range(2, B):
                copy_batch(b)
                copy_logits(b - 2)
                copy_logits_T(b - 1)
            copy_logits(B - 2)
            copy_logits_T(B - 1)
            copy_logits(B - 1)
            if layer == 0:
                act.wait_ge(shifted, 1)
                act.activation(prob[:], above[:], ACT.Exp).then_inc(activated, 1)
            else:
                act.wait_ge(logits_in, B)
                act.activation(prob[:], logits[:], ACT.Sigmoid).then_inc(activated, 1)

            def shared(g):
                for f in range(FC):
                    n = g * FC + f
                    act.wait_ge(gu_done, n + 1)
                    if not isinstance(g, int) or g * FC + f >= NBK:
                        act.wait_ge(h_done, n + (1 - NBK))
                    if isinstance(g, int):
                        act.activation(h_T[:, f, :], bank[:, 2 * (f % NBK) + 1, :], ACT.Copy)
                    act.activation(silu_T[:, f % NBK, :], bank[:, 2 * (f % NBK), :], ACT.Silu).then_inc(silu_done, 1)
                if isinstance(g, int):
                    for c in range(TPB):
                        act.wait_ge(y_done, c + 1)
                        act.activation(y0(c), bank[:, 6 + c % 2, :], ACT.Copy, scale=gate[:, 0:1]).then_inc(y_read, 1)

            shared(0)
            with act.Fori(1, B) as g:
                shared(g)

            def split_of(i):
                return act.value_load(sched[0:1, bass.ds(i, 1), 2:3].rearrange("a i c -> a (i c)"), min_val=0, max_val=E - 1)

            def gu_hi(e, piece):
                act.wait_ge(expert_w, 48 * e + 48)
                par = e % 2 if isinstance(e, int) else act.snap(e % 2)
                rows = slice(piece * HC // 2, (piece + 1) * HC // 2)
                act.activation(w_gu_parts[:, bass.ds(par, 1), 0, rows, :].rearrange("p a d f -> p (a d f)"),
                               w_gu[:, bass.ds(par, 1), rows, :].rearrange("p a d f -> p (a d f)"), ACT.Copy
                               ).then_inc(gu_hi_done, 1)

            def dn_hi(e):
                par = e % 2 if isinstance(e, int) else act.snap(e % 2)
                act.activation(w_dn_parts[:, bass.ds(par, 1), 0, :, :].rearrange("p a f h -> p (a f h)"),
                               w_dn[:, bass.ds(par, 1), :, :].rearrange("p a f h -> p (a f h)"), ACT.Copy).then_inc(dn_hi_done, 1)

            def x_hi(i, half):
                act.wait_ge(xg_turned, i + 1)
                if not isinstance(i, int) or i >= 2:
                    act.wait_ge(egu_done, i + (-1))
                act.activation(xg_T[:, half, 0, :, :].rearrange("p d m -> p (d m)"), bank[:, 6, :], ACT.Copy).then_inc(xg_hi, 1)

            def h_hi(i, half, before=None):
                act.wait_ge(eh_turned, i + 1)
                if before is not None:
                    act.wait_ge(ey_done, before)
                elif not isinstance(i, int) or i >= 2:
                    act.wait_ge(ey_done, i + (-1))
                act.activation(hg_T[:, half, 0, :, :].rearrange("p f m -> p (f m)"), bank[0:FW, 7, 0:FK * P], ACT.Copy
                               ).then_inc(eh_hi, 1)

            def silu(i, half):
                act.wait_ge(egu_done, i + 1)
                if not isinstance(i, int) or i >= 2:
                    act.wait_ge(eh_done, i + (-1))
                act.activation(silu_g[:, half, :], bank[:, half, 0:F], ACT.Silu).then_inc(esilu_done, 1)

            def y_out(i, half, before=None):
                act.wait_ge(ey_done, i + 1)
                act.wait_ge(out_cols, 2 * i + 2)
                if before is not None:
                    act.wait_ge(accumulated, 16 * before)
                elif not isinstance(i, int) or i >= 2:
                    act.wait_ge(accumulated, 16 * i + (-16))
                act.activation(y_tok[:, half, :], bank[:, 2 + half, :], ACT.Copy, scale=w_out[:, half:half + 1]
                               ).then_inc(ey_copied, 1)

            def step(i, half):
                late = split_of(i - 1)
                with act.If(late != 0):
                    gu_hi(late, 1)
                silu(i, half)
                h_hi(i - 1, 1 - half)
                x_hi(i + 2, half)
                e = split_of(i)
                with act.If(e != 0):
                    gu_hi(e, 0)
                y_out(i - 2, half)
                with act.If(late != 0):
                    dn_hi(late)

            act.wait_ge(y_done, TT)
            gu_hi(0, 0)
            gu_hi(0, 1)
            dn_hi(0)
            act.wait_ge(sched_in, 16)
            turns = act.value_load(turns_i[0:1, 0:1], min_val=4, max_val=64)
            x_hi(0, 0)
            x_hi(1, 1)
            silu(0, 0)
            x_hi(2, 0)
            gu_hi(1, 0)
            gu_hi(1, 1)
            silu(1, 1)
            h_hi(0, 0)
            x_hi(3, 1)
            e = split_of(1)
            with act.If(e != 0):
                gu_hi(e, 0)
            dn_hi(1)
            step(2, 0)
            with act.Fori(1, turns) as turn:
                step(turn * 2 + 1, 1)
                step(turn * 2 + 2, 0)
            last = act.value_load(turns_i[0:1, 1:2], min_val=7, max_val=127)
            h_hi(turns * 2, 0, last)
            y_out(turns * 2 - 1, 1, act.value_load(turns_i[0:1, 2:3], min_val=6, max_val=126))
            y_out(turns * 2, 0, last)

        @block.vector
        def _(dve):
            last = range(TT - TPB, TT)
            for i in last:
                dve.bn_stats(stats[:, i, :], x[:, i, :]).then_inc(ln_stats, 1)
            dve.wait_ge(ln_stats, TPB)
            for i in last:
                dve.bn_aggr(mean_var[:, i, :], stats[:, i, :]).then_inc(ln_stats, 1)
            dve.wait_ge(ln_stats, 2 * TPB)
            dve.tensor_scalar(mean_var[:, TT - TPB:TT, 1], mean_var[:, TT - TPB:TT, 1], EPS, None, ALU.add).then_inc(ln_var, 1)
            for i in range(TT):
                if i >= 2 * TPB:
                    dve.wait_ge(xt_turned, i - 2 * TPB + 1)
                    dve.wait_ge(xh_stored[i // TPB % 2], 16 * (i // (2 * TPB)))
                if i == TT - TPB:
                    dve.wait_ge(ln_rstd, 1)
                dve.tensor_scalar(xh[:, (i // TPB) % 2, i % TPB, :], x[:, i, :], mean_var[:, i, 0:1], rstd[:, i:i + 1],
                                  ALU.subtract, ALU.mult).then_inc(ln_done, 1)
            count = [0]

            def then(ins, signal=None, value=None):
                if signal is not None:
                    ins.then_inc(signal, 1)
                    dve.wait_ge(signal, value)
                    return
                count[0] += 1
                ins.then_inc(chain, 1)
                dve.wait_ge(chain, count[0])

            def over_e(a):
                return a[:, :, None].to_broadcast([P, TT, E])

            dve.wait_ge(const_set, 21)
            if layer == 0:
                dve.wait_ge(logits_in, B)
                then(dve.tensor_reduce(stat1[:], logits[:], AX.X, ALU.max))
                dve.tensor_tensor(above[:], logits[:], over_e(stat1), ALU.subtract).then_inc(shifted, 1)
                dve.wait_ge(activated, 1)
                then(dve.tensor_reduce(stat1[:], prob[:], AX.X, ALU.add))
                then(dve.reciprocal(stat2[:], stat1[:]))
                then(dve.tensor_tensor(prob[:], prob[:], over_e(stat2), ALU.mult))
            else:
                dve.wait_ge(activated, 1)
            for i in range(TT):
                ins = dve.max(top[:, i, :], prob[:, i, :])
            then(ins)
            kth = top[:, :, K - 1:K].to_broadcast([P, TT, E])
            then(dve.tensor_tensor(above[:], prob[:], kth, ALU.is_gt))
            then(dve.tensor_tensor(tied[:], prob[:], kth, ALU.is_equal))
            then(dve.tensor_reduce(stat1[:], above[:], AX.X, ALU.add))
            then(dve.tensor_scalar(stat1[:], stat1[:], -1.0, float(K), ALU.mult, ALU.add))
            flat = "p t e -> p (t e)"
            then(dve.tensor_tensor_scan(tmp[:].rearrange(flat), reset_e[:].rearrange(flat), tied[:].rearrange(flat), 0.0,
                                        ALU.mult, ALU.add))
            then(dve.tensor_tensor(tmp[:], tmp[:], over_e(stat1), ALU.is_le))
            then(dve.tensor_tensor(tied[:], tied[:], tmp[:], ALU.mult))
            dve.tensor_tensor(mask[:], above[:], tied[:], ALU.add).then_inc(mask_ready, 1)
            then(dve.tensor_reduce(stat1[:], top[:, :, 0:K], AX.X, ALU.add))
            if layer == 1:
                then(dve.tensor_scalar(stat1[:], stat1[:], 1e-20, None, ALU.add))
            then(dve.reciprocal(stat2[:], stat1[:]))
            then(dve.tensor_scalar(stat2[:], stat2[:], gate[:, 0:1], None, ALU.mult))
            then(dve.tensor_tensor(weight[:], prob[:], over_e(stat2), ALU.mult))
            dve.wait_ge(ranked, 1)
            then(dve.tensor_copy(total_t[:], bank[:, 7, 0:TT * E].rearrange("p (t e) -> p e t", t=TT)), ranks_read, 1)
            flat_t = "p e t -> p (e t)"
            then(dve.tensor_tensor_scan(cum_t[:].rearrange(flat_t), reset_t[:].rearrange(flat_t), total_t[:].rearrange(flat_t),
                                        0.0, ALU.mult, ALU.add))
            then(dve.tensor_tensor(total_t[:], cum_t[:], total_t[:], ALU.subtract))
            then(dve.tensor_tensor(rank_i[:], bank[:, 6, 0:TT * E].rearrange("p (t e) -> p t e", t=TT),
                                   total_t[:].rearrange("p e t -> p t e"), ALU.add), ranks_read, 2)
            then(dve.tensor_scalar(rank_a[:], rank_i[:], P - 1, CAPT.bit_length() - 1, ALU.bitwise_and, ALU.logical_shift_left))
            then(dve.tensor_scalar(rank_i[:], rank_i[:], P.bit_length() - 1, None, ALU.logical_shift_right))
            then(dve.tensor_tensor(row1[:], rank_a[:], rank_i[:], ALU.add))
            then(dve.tensor_tensor(row1[:], row1[:], expert_base[:, None, :].to_broadcast([P, TT, E]), ALU.add))
            then(dve.tensor_tensor(row1[:], row1[:], mask[:], ALU.mult))
            for i in range(TT):
                ins = dve.max(top_rows[:, i, :], row1[:, i, :])
            then(ins)
            then(dve.tensor_scalar(slot_idx[:], top_rows[:], -1.0, None, ALU.add))
            then(dve.tensor_copy(entry[:, :, :, 0], token_f[:, :, None].to_broadcast([P, TT, K])))
            for k in range(K):
                then(dve.tensor_tensor(tmp[:], row1[:], top_rows[:, :, k:k + 1].to_broadcast([P, TT, E]), ALU.is_equal))
                then(dve.tensor_tensor(tmp[:], tmp[:], weight[:], ALU.mult))
                then(dve.tensor_reduce(entry[:, :, k, 1], tmp[:], AX.X, ALU.add), entries_ready, k + 1)
            then(dve.tensor_scalar(cnt_i[:], cum_t[:, :, TT - 1], float(P - 1), None, ALU.add))
            then(dve.tensor_scalar(cnt_i[:], cnt_i[:], P.bit_length() - 1, None, ALU.logical_shift_right))
            then(dve.tensor_scalar(tiles_f[:], cnt_i[:], 1.0, None, ALU.max))
            then(dve.tensor_tensor_scan(ends_f[:], ones_e[:], tiles_f[:], 0.0, ALU.mult, ALU.add))
            then(dve.tensor_copy(ends_i[:], ends_f[:]))
            then(dve.tensor_scalar(before[:], ends_f[:], tile_f[:, 0:1], None, ALU.is_le))
            then(dve.tensor_tensor(before_n[:], before[:], tiles_f[:], ALU.mult))
            then(dve.tensor_reduce(ncol[:, 0:1], before[:], AX.X, ALU.add))
            then(dve.tensor_reduce(ncol[:, 1:2], before_n[:], AX.X, ALU.add))
            then(dve.tensor_scalar(next_e[:], ncol[:, 0:1], 1.0, None, ALU.add))
            then(dve.tensor_scalar(has_next[:], next_e[:], float(E), None, ALU.is_lt))
            then(dve.tensor_tensor(next_e[:], next_e[:], has_next[:], ALU.mult))
            then(dve.tensor_tensor(has_next[:], ncol[:, 1:2], tile_f[:], ALU.is_equal))
            then(dve.tensor_tensor(sched_f[:, 2:3], next_e[:], has_next[:], ALU.mult))
            then(dve.tensor_scalar(sched_f[:, 1:2], ncol[:, 0:1], float(E - 1), None, ALU.min))
            then(dve.tensor_scalar(sched_f[:, 0:1], ncol[:, 0:1], float(CAPT), tile_f[:, 0:1], ALU.mult, ALU.add))
            then(dve.tensor_tensor(sched_f[:, 0:1], sched_f[:, 0:1], ncol[:, 1:2], ALU.subtract))
            then(dve.tensor_scalar(sched_f[:, 0:1], sched_f[:, 0:1], float(DUMMY), None, ALU.min))
            then(dve.tensor_scalar(turns_i[:, 0:1], ends_i[:, E - 1:E], 1, None, ALU.logical_shift_right))
            then(dve.tensor_scalar(turns_i[:, 1:2], turns_i[:, 0:1], 2.0, -1.0, ALU.mult, ALU.add))
            then(dve.tensor_scalar(turns_i[:, 2:3], turns_i[:, 0:1], 2.0, -2.0, ALU.mult, ALU.add))
            dve.tensor_copy(sched_i[:], sched_f[:]).then_inc(sched_ready, 1)

            def shared(g):
                for f in range(FC):
                    n = g * FC + f
                    dve.wait_ge(silu_done, n + 1)
                    if f == 0:
                        dve.wait_ge(y_done, TPB * g)
                    dve.tensor_tensor(h_T[:, f, :], silu_T[:, f % NBK, :], bank[:, 2 * (f % NBK) + 1, :], ALU.mult
                                      ).then_inc(h_done, 1)
                for c in range(TPB):
                    dve.wait_ge(y_done, TPB * g + c + 1)
                    if c == 0:
                        dve.wait_ge(y_read, TPB * g)
                    xc = x[:, bass.ds(g * TPB + c, 1), :].rearrange("p a d -> p (a d)")
                    dve.scalar_tensor_tensor(xc, bank[:, 6 + c % 2, :], gate[:, 0:1], xc, ALU.mult, ALU.add).then_inc(y_read, 1)

            with dve.Fori(1, B) as g:
                shared(g)

            def split_of(i):
                return dve.value_load(sched[0:1, bass.ds(i, 1), 2:3].rearrange("a i c -> a (i c)"), min_val=0, max_val=E - 1)

            def gu_lo(e, piece):
                dve.wait_ge(gu_hi_done, 2 * e + (piece + 1))
                par = e % 2 if isinstance(e, int) else dve.snap(e % 2)
                rows = slice(piece * HC // 2, (piece + 1) * HC // 2)
                parts = w_gu_parts[:, bass.ds(par, 1), :, rows, :].rearrange("p a s d f -> p (a s) (d f)")
                dve.tensor_tensor(parts[:, 1, :], w_gu[:, bass.ds(par, 1), rows, :].rearrange("p a d f -> p (a d f)"),
                                  parts[:, 0, :].bitcast(F32), ALU.subtract).then_inc(gu_split, 1)

            def dn_lo(e):
                dve.wait_ge(dn_hi_done, e + 1)
                par = e % 2 if isinstance(e, int) else dve.snap(e % 2)
                parts = w_dn_parts[:, bass.ds(par, 1), :, :, :].rearrange("p a s f h -> p (a s) (f h)")
                dve.tensor_tensor(parts[:, 1, :], w_dn[:, bass.ds(par, 1), :, :].rearrange("p a f h -> p (a f h)"),
                                  parts[:, 0, :].bitcast(F32), ALU.subtract).then_inc(dn_split, 1)

            def x_lo(i, half):
                dve.wait_ge(xg_hi, i + 1)
                dve.tensor_tensor(xg_T[:, half, 1, :, :].rearrange("p d m -> p (d m)"), bank[:, 6, :],
                                  xg_T[:, half, 0, :, :].rearrange("p d m -> p (d m)").bitcast(F32), ALU.subtract
                                  ).then_inc(xg_copied, 1)

            def h_lo(i, half):
                dve.wait_ge(eh_hi, i + 1)
                dve.tensor_tensor(hg_T[:, half, 1, :, :].rearrange("p f m -> p (f m)"), bank[0:FW, 7, 0:FK * P],
                                  hg_T[:, half, 0, :, :].rearrange("p f m -> p (f m)").bitcast(F32), ALU.subtract
                                  ).then_inc(eh_copied, 1)

            def times_up(i, half):
                dve.wait_ge(esilu_done, i + 1)
                if not isinstance(i, int) or i >= 2:
                    dve.wait_ge(eh_turned, i + (-1))
                dve.tensor_tensor(h_tok[:, half, :], silu_g[:, half, :], bank[:, half, F:2 * F], ALU.mult).then_inc(eh_done, 1)

            def step(i, half):
                late = split_of(i - 1)
                with dve.If(late != 0):
                    gu_lo(late, 1)
                times_up(i, half)
                h_lo(i - 1, 1 - half)
                x_lo(i + 2, half)
                e = split_of(i)
                with dve.If(e != 0):
                    gu_lo(e, 0)
                with dve.If(late != 0):
                    dn_lo(late)

            gu_lo(0, 0)
            gu_lo(0, 1)
            dn_lo(0)
            dve.wait_ge(sched_in, 16)
            turns = dve.value_load(turns_i[0:1, 0:1], min_val=4, max_val=64)
            x_lo(0, 0)
            x_lo(1, 1)
            times_up(0, 0)
            x_lo(2, 0)
            gu_lo(1, 0)
            gu_lo(1, 1)
            times_up(1, 1)
            h_lo(0, 0)
            x_lo(3, 1)
            e = split_of(1)
            with dve.If(e != 0):
                gu_lo(e, 0)
            dn_lo(1)
            step(2, 0)
            with dve.Fori(1, turns) as turn:
                step(turn * 2 + 1, 1)
                step(turn * 2 + 2, 0)
            h_lo(turns * 2, 0)
    return acc_rows


INPUTS = ["x", "ctx_512", "g_xattn", "g_ffn",
          "L0_ffn_w_gate", "L0_ffn_w_gate_up", "L0_ffn_w_down", "L0_ffn_w_sh_gate_up", "L0_ffn_w_sh_down",
          "L1_ffn_gate_w", "L1_ffn_wg", "L1_ffn_wu", "L1_ffn_wd", "L1_ffn_sg", "L1_ffn_su", "L1_ffn_sd"]


def build_program(nc, arg, out):
    with ExitStack() as ctx:
        x = ctx.enter_context(nc.sbuf_tensor("x_res", [P, TT, H], F32))
        ident = ctx.enter_context(nc.sbuf_tensor("ident", [P, P], F32))
        ident_r = ctx.enter_context(nc.sbuf_tensor("ident_r", [P, P], F32R))
        gates = ctx.enter_context(nc.sbuf_tensor("gates", [P, 2], F32))
        stats = ctx.enter_context(nc.sbuf_tensor("stats", [P, TT, 6], F32))
        mean_var = ctx.enter_context(nc.sbuf_tensor("mean_var", [P, TT, 2], F32))
        rstd = ctx.enter_context(nc.sbuf_tensor("rstd", [P, TT], F32))
        minus_half = ctx.enter_context(nc.sbuf_tensor("minus_half", [P, TT], F32))
        ident_made = ctx.enter_context(nc.semaphore("ident_made"))
        soft_sems = [{name: ctx.enter_context(nc.semaphore(f"{name}_{layer}")) for name in SOFT_SEMS}
                     for layer in range(2)]
        sems = {}

        def sem(name):
            if name not in sems:
                sems[name] = ctx.enter_context(nc.semaphore(name))
            return sems[name]

        with nc.Block() as block:
            @block.gpsimd
            def _(pool):
                pool.memset(ident[:], 0.0).then_inc(ident_made, 1)
                pool.wait_ge(ident_made, 1)
                pool.affine_select(out=ident[:], in_=ident[:], compare_op=ALU.not_equal, fill=1.0, base=0,
                                   pattern=[[-1, P]], channel_multiplier=1).then_inc(ident_made, 1)

            @block.vector
            def _(dve):
                dve.wait_ge(ident_made, 2)
                dve.tensor_copy(ident_r[:], ident[:]).then_inc(ident_made, 1)

        shared = {"sem": sem, "soft_sems": soft_sems, "x": x, "ident": ident, "ident_r": ident_r, "gates": gates,
                  "stats": stats, "mean_var": mean_var, "rstd": rstd, "minus_half": minus_half,
                  "ctx": arg["ctx_512"], "g_xattn": arg["g_xattn"], "g_ffn": arg["g_ffn"],
                  "out": out.rearrange("b s d -> (b s) d")}
        w_sh_gu, w_gu = arg["L0_ffn_w_sh_gate_up"], arg["L0_ffn_w_gate_up"]
        layer0 = dict(shared, E=8, F=256, FS=1024, K=2, w_router=arg["L0_ffn_w_gate"],
                      w_sh_gate=w_sh_gu[:, 0:1024], w_sh_up=w_sh_gu[:, 1024:2048], w_sh_down=arg["L0_ffn_w_sh_down"],
                      wg=lambda e: w_gu[bass.ds(e, 1), :, 0:256],
                      wu=lambda e: w_gu[bass.ds(e, 1), :, 256:512],
                      wd=lambda e: arg["L0_ffn_w_down"][bass.ds(e, 1), :, :])
        layer1 = dict(shared, E=32, F=192, FS=384, K=6, w_router=arg["L1_ffn_gate_w"],
                      w_sh_gate=arg["L1_ffn_sg"], w_sh_up=arg["L1_ffn_su"], w_sh_down=arg["L1_ffn_sd"],
                      wg=lambda e: arg["L1_ffn_wg"][bass.ds(e, 1), :, :],
                      wu=lambda e: arg["L1_ffn_wu"][bass.ds(e, 1), :, :],
                      wd=lambda e: arg["L1_ffn_wd"][bass.ds(e, 1), :, :])
        layer0["x_rows"] = arg["x"].rearrange("b s d -> (b s) d")
        make_attention(nc, 0, layer0)
        layer1["x_rows"] = make_ffn(nc, 0, layer0)
        numbers = [handle.num for handle in sems.values()]
        nc.all_engine_barrier(sems_to_clear=range(min(numbers), max(numbers) + 1))
        make_attention(nc, 1, layer1)
        make_ffn(nc, 1, layer1)


def kernel(**inputs):
    import numpy as np
    import concourse.bacc as bacc
    from concourse.bass_utils import run_bass_kernel_spmd

    nc = bacc.Bacc("TRN2", target_bir_lowering=False, num_devices=1)
    arrays, arg = {}, {}
    for name in INPUTS:
        a = np.ascontiguousarray(inputs[name])
        arrays[f"in_{name}"] = a
        arg[name] = nc.dram_tensor(f"in_{name}", a.shape, mybir.dt.from_np(a.dtype), kind="ExternalInput").ap()
    out = nc.dram_tensor("out_x", (B, S, H), F32, kind="ExternalOutput").ap()
    build_program(nc, arg, out)
    result = run_bass_kernel_spmd(nc, [arrays], core_ids=[0])
    return result.results[0]["out_x"]
```
